# Optimizing a Trainium2 kernel written in Bass

```python
import numpy as np
import jax
import jax.numpy as jnp

def _softmax(x, axis=-1):
    return jax.nn.softmax(x, axis=axis)

def _gelu(x):
    return jax.nn.gelu(x, approximate=True)

def _silu(x):
    return jax.nn.silu(x)

def _sigmoid(x):
    return jax.nn.sigmoid(x)

def _layernorm(x, axis=-1, eps=1e-05):
    m = jnp.mean(x, axis=axis, keepdims=True)
    v = jnp.var(x, axis=axis, keepdims=True)
    return (x - m) / jnp.sqrt(v + eps)

def _scatter_add(tgt, idx, src, axis=0):
    return tgt.at[idx].add(src)

def _segment_sum(src, seg, n):
    return jax.ops.segment_sum(src, seg, n)
kernel_name = 'mk_seq_postln_d1_jaxref_r4_0909f0'

def setup_inputs(seed: int=0):
    np.random.seed(seed)
    _w = jnp.asarray

    def _L0_attn_setup():
        import jax, jax.numpy as jnp
        import numpy as np
        H = 256
        NH = 16
        HD = H // NH
        B, S = (2, 512)
        key = jax.random.key(seed)
        ks = jax.random.split(key, 6)
        std = 0.02
        x = jax.random.normal(ks[0], (B, S, H), dtype=jnp.float32)
        w_qkv = jax.random.normal(ks[1], (3 * H, H), dtype=jnp.float32) * std
        b_qkv = jnp.zeros((3 * H,), dtype=jnp.float32)
        ln_g = jnp.ones((H,), dtype=jnp.float32)
        ln_b = jnp.zeros((H,), dtype=jnp.float32)
        w_ent = jax.random.normal(ks[2], (1, H), dtype=jnp.float32) * std
        b_ent = jnp.zeros((1,), dtype=jnp.float32)
        w_out = jax.random.normal(ks[3], (H, H), dtype=jnp.float32) * std
        b_out = jnp.zeros((H,), dtype=jnp.float32)
        return {'x': x, 'ln_g': ln_g, 'ln_b': ln_b, 'w_qkv': w_qkv, 'b_qkv': b_qkv, 'w_ent': w_ent, 'b_ent': b_ent, 'w_out': w_out, 'b_out': b_out}
    _L0_attn_in = _L0_attn_setup()

    def _L0_ffn_setup():
        import jax, jax.numpy as jnp
        import numpy as np
        B, N, D = (4, 2048, 256)
        HEADS, DH = (8, 64)
        HID = HEADS * DH
        WIN = 128
        NQ, NKV = (256, 512)
        EPS, N_ITERS, FETCH_K = (1.0, 50, 9.0 / 8.0)
        SCALE = DH ** (-0.5)

        def rmsnorm(x, gamma):
            norm = jnp.maximum(jnp.linalg.norm(x, axis=-1, keepdims=True), 1e-12)
            return x / norm * x.shape[-1] ** 0.5 * gamma

        def coor_descent(s, k):
            logk = jnp.log(jnp.asarray(k, s.dtype))

            def body(_, ab):
                a, b = ab
                a = EPS * (logk - jax.nn.logsumexp((s + b) / EPS, axis=-1, keepdims=True))
                b = -jax.nn.relu(s + a)
                return (a, b)
            a, b = jax.lax.fori_loop(0, N_ITERS, body, (jnp.zeros_like(s[..., :1]), -s))
            return jnp.exp((s + a + b) / EPS)

        def route(x, routing_token, num_tokens):
            s = jnp.einsum('bnd,d->bn', x, routing_token)
            k = min(num_tokens * FETCH_K, x.shape[1])
            scores = coor_descent(s, k)
            sel_scores, sel_idx = jax.lax.top_k(scores, num_tokens)
            sel_scores = sel_scores + jax.lax.stop_gradient(1.0 - sel_scores)
            return (sel_scores, sel_idx)

        def light_local_attn(x, gamma, wq, wkv, wo):
            b, n, d = x.shape
            xn = rmsnorm(x, gamma)
            q = xn @ wq
            k, v = jnp.split(xn @ wkv, 2, axis=-1)

            def win(t):
                return t.reshape(b, n // WIN, WIN, HEADS, DH).transpose(0, 1, 3, 2, 4)
            q, k, v = (win(q) * SCALE, win(k), win(v))
            attn = jax.nn.softmax(jnp.einsum('bwhid,bwhjd->bwhij', q, k), axis=-1)
            out = jnp.einsum('bwhij,bwhjd->bwhid', attn, v)
            out = out.transpose(0, 1, 3, 2, 4).reshape(b, n, HID)
            return out @ wo

        def heavy_attn(xq, context, scores_kv, gamma, wq, wkv_t, wo):
            b, nq, d = xq.shape
            nkv = context.shape[1]
            xqn = rmsnorm(xq, gamma)
            ctx = rmsnorm(context, gamma)[:, None]
            q = (xqn @ wq).reshape(b, nq, HEADS, DH).transpose(0, 2, 1, 3) * SCALE
            kvw = wkv_t.reshape(1, HEADS, 2 * DH, d)
            kv = jnp.einsum('rhdi,brni->brhnd', kvw, ctx)
            k, v = jnp.split(kv, 2, axis=-1)
            v = v * scores_kv[:, None, None, :, None]
            k = k.reshape(b, HEADS, nkv, DH)
            v = v.reshape(b, HEADS, nkv, DH)
            attn = jax.nn.softmax(jnp.einsum('bhid,bhjd->bhij', q, k), axis=-1)
            out = jnp.einsum('bhij,bhjd->bhid', attn, v)
            out = out.transpose(0, 2, 1, 3).reshape(b, nq, HID)
            return out @ wo
        key = jax.random.key(seed)
        ks = jax.random.split(key, 10)
        lin = lambda k, shape, fan: jax.random.normal(k, shape, jnp.float32) * fan ** (-0.5)
        return dict(x=jax.random.normal(ks[0], (B, N, D), jnp.float32), gamma_light=jnp.ones((D,), jnp.float32), wq_light=lin(ks[1], (D, HID), D), wkv_light=lin(ks[2], (D, 2 * HID), D), wo_light=lin(ks[3], (HID, D), HID), q_routing_token=jax.random.normal(ks[4], (D,), jnp.float32), kv_routing_token=jax.random.normal(ks[5], (D,), jnp.float32), gamma_heavy=jnp.ones((D,), jnp.float32), wq_heavy=lin(ks[6], (D, HID), D), wkv_heavy=lin(ks[7], (2 * HID, D), D), wo_heavy=lin(ks[8], (HID, D), HID))
    _L0_ffn_in = _L0_ffn_setup()
    _d = {'L0_attn_x': _L0_attn_in['x'], 'L0_attn_ln_g': _L0_attn_in['ln_g'], 'L0_attn_ln_b': _L0_attn_in['ln_b'], 'L0_attn_w_qkv': _L0_attn_in['w_qkv'], 'L0_attn_b_qkv': _L0_attn_in['b_qkv'], 'L0_attn_w_ent': _L0_attn_in['w_ent'], 'L0_attn_b_ent': _L0_attn_in['b_ent'], 'L0_attn_w_out': _L0_attn_in['w_out'], 'L0_attn_b_out': _L0_attn_in['b_out'], 'L0_ffn_gamma_light': _L0_ffn_in['gamma_light'], 'L0_ffn_wq_light': _L0_ffn_in['wq_light'], 'L0_ffn_wkv_light': _L0_ffn_in['wkv_light'], 'L0_ffn_wo_light': _L0_ffn_in['wo_light'], 'L0_ffn_q_routing_token': _L0_ffn_in['q_routing_token'], 'L0_ffn_kv_routing_token': _L0_ffn_in['kv_routing_token'], 'L0_ffn_gamma_heavy': _L0_ffn_in['gamma_heavy'], 'L0_ffn_wq_heavy': _L0_ffn_in['wq_heavy'], 'L0_ffn_wkv_heavy': _L0_ffn_in['wkv_heavy'], 'L0_ffn_wo_heavy': _L0_ffn_in['wo_heavy']}
    _x0 = _d['L0_attn_x']
    _d['L0_attn_x'] = jax.random.normal(jax.random.fold_in(jax.random.key(seed), 1), (8, 1024, 256), dtype=_x0.dtype)
    del _x0
    return _d

def reference(L0_attn_x, L0_attn_ln_g, L0_attn_ln_b, L0_attn_w_qkv, L0_attn_b_qkv, L0_attn_w_ent, L0_attn_b_ent, L0_attn_w_out, L0_attn_b_out, L0_ffn_gamma_light, L0_ffn_wq_light, L0_ffn_wkv_light, L0_ffn_wo_light, L0_ffn_q_routing_token, L0_ffn_kv_routing_token, L0_ffn_gamma_heavy, L0_ffn_wq_heavy, L0_ffn_wkv_heavy, L0_ffn_wo_heavy):

    def _L0_attn_ref(x, ln_g, ln_b, w_qkv, b_qkv, w_ent, b_ent, w_out, b_out):
        import jax, jax.numpy as jnp
        import numpy as np
        H = 256
        NH = 16
        HD = H // NH
        B, S = (2, 512)
        b, s, h = x.shape
        scale = 1.0 / jnp.sqrt(jnp.float32(HD))
        TEMP = 0.1
        mu = jnp.mean(x, axis=-1, keepdims=True)
        var = jnp.mean(jnp.square(x - mu), axis=-1, keepdims=True)
        xn = (x - mu) / jnp.sqrt(var + 1e-06) * ln_g + ln_b
        qkv = xn @ w_qkv.T + b_qkv
        qkv = qkv.reshape(b, s, 3, NH, HD).transpose(2, 0, 3, 1, 4)
        q, k, v = (qkv[0], qkv[1], qkv[2])
        scores = jnp.einsum('bhqd,bhkd->bhqk', q, k) * scale
        causal = jnp.tril(jnp.ones((s, s), dtype=bool))
        scores = jnp.where(causal[None, None], scores, -jnp.inf)
        probs = jax.nn.softmax(scores / TEMP, axis=-1)
        gate = jax.nn.sigmoid(xn @ w_ent.T + b_ent)
        gate = jnp.clip(gate, 0.1, 2.0)[:, None, None, :, 0]
        probs = probs * gate
        out = jnp.einsum('bhqk,bhkd->bhqd', probs, v)
        out = out.transpose(0, 2, 1, 3).reshape(b, s, h)
        return (out @ w_out.T + b_out) * 0.1

    def _L0_ffn_ref(x, gamma_light, wq_light, wkv_light, wo_light, q_routing_token, kv_routing_token, gamma_heavy, wq_heavy, wkv_heavy, wo_heavy):
        import jax, jax.numpy as jnp
        import numpy as np
        B, N, D = (4, 2048, 256)
        HEADS, DH = (8, 64)
        HID = HEADS * DH
        WIN = 128
        NQ, NKV = (256, 512)
        EPS, N_ITERS, FETCH_K = (1.0, 50, 9.0 / 8.0)
        SCALE = DH ** (-0.5)

        def rmsnorm(x, gamma):
            norm = jnp.maximum(jnp.linalg.norm(x, axis=-1, keepdims=True), 1e-12)
            return x / norm * x.shape[-1] ** 0.5 * gamma

        def coor_descent(s, k):
            logk = jnp.log(jnp.asarray(k, s.dtype))

            def body(_, ab):
                a, b = ab
                a = EPS * (logk - jax.nn.logsumexp((s + b) / EPS, axis=-1, keepdims=True))
                b = -jax.nn.relu(s + a)
                return (a, b)
            a, b = jax.lax.fori_loop(0, N_ITERS, body, (jnp.zeros_like(s[..., :1]), -s))
            return jnp.exp((s + a + b) / EPS)

        def route(x, routing_token, num_tokens):
            s = jnp.einsum('bnd,d->bn', x, routing_token)
            k = min(num_tokens * FETCH_K, x.shape[1])
            scores = coor_descent(s, k)
            sel_scores, sel_idx = jax.lax.top_k(scores, num_tokens)
            sel_scores = sel_scores + jax.lax.stop_gradient(1.0 - sel_scores)
            return (sel_scores, sel_idx)

        def light_local_attn(x, gamma, wq, wkv, wo):
            b, n, d = x.shape
            xn = rmsnorm(x, gamma)
            q = xn @ wq
            k, v = jnp.split(xn @ wkv, 2, axis=-1)

            def win(t):
                return t.reshape(b, n // WIN, WIN, HEADS, DH).transpose(0, 1, 3, 2, 4)
            q, k, v = (win(q) * SCALE, win(k), win(v))
            attn = jax.nn.softmax(jnp.einsum('bwhid,bwhjd->bwhij', q, k), axis=-1)
            out = jnp.einsum('bwhij,bwhjd->bwhid', attn, v)
            out = out.transpose(0, 1, 3, 2, 4).reshape(b, n, HID)
            return out @ wo

        def heavy_attn(xq, context, scores_kv, gamma, wq, wkv_t, wo):
            b, nq, d = xq.shape
            nkv = context.shape[1]
            xqn = rmsnorm(xq, gamma)
            ctx = rmsnorm(context, gamma)[:, None]
            q = (xqn @ wq).reshape(b, nq, HEADS, DH).transpose(0, 2, 1, 3) * SCALE
            kvw = wkv_t.reshape(1, HEADS, 2 * DH, d)
            kv = jnp.einsum('rhdi,brni->brhnd', kvw, ctx)
            k, v = jnp.split(kv, 2, axis=-1)
            v = v * scores_kv[:, None, None, :, None]
            k = k.reshape(b, HEADS, nkv, DH)
            v = v.reshape(b, HEADS, nkv, DH)
            attn = jax.nn.softmax(jnp.einsum('bhid,bhjd->bhij', q, k), axis=-1)
            out = jnp.einsum('bhij,bhjd->bhid', attn, v)
            out = out.transpose(0, 2, 1, 3).reshape(b, nq, HID)
            return out @ wo
        b = x.shape[0]
        light_out = light_local_attn(x, gamma_light, wq_light, wkv_light, wo_light)
        scores_q, idx_q = route(x, q_routing_token, NQ)
        scores_kv, idx_kv = route(x, kv_routing_token, NKV)
        routed_q = jnp.take_along_axis(x, idx_q[..., None], axis=1)
        routed_kv = jnp.take_along_axis(x, idx_kv[..., None], axis=1)
        routed_out = heavy_attn(routed_q, routed_kv, scores_kv, gamma_heavy, wq_heavy, wkv_heavy, wo_heavy)
        routed_out = routed_out * scores_q[..., None]
        heavy_out = jnp.zeros_like(x).at[jnp.arange(b)[:, None], idx_q].set(routed_out)
        return light_out + heavy_out
    x = L0_attn_x
    x = _layernorm(x + _L0_attn_ref(x, L0_attn_ln_g, L0_attn_ln_b, L0_attn_w_qkv, L0_attn_b_qkv, L0_attn_w_ent, L0_attn_b_ent, L0_attn_w_out, L0_attn_b_out), axis=-1)
    x = _layernorm(x + _L0_ffn_ref(x, L0_ffn_gamma_light, L0_ffn_wq_light, L0_ffn_wkv_light, L0_ffn_wo_light, L0_ffn_q_routing_token, L0_ffn_kv_routing_token, L0_ffn_gamma_heavy, L0_ffn_wq_heavy, L0_ffn_wkv_heavy, L0_ffn_wo_heavy), axis=-1)
    return x

_drawn_inputs = setup_inputs


def setup_inputs(seed=0):
    import zlib

    import numpy as np

    out = dict(_drawn_inputs(seed))
    spreads = {'L0_attn_ln_g': (1.0, 0.6),
     'L0_attn_ln_b': (0.0, 0.8),
     'L0_attn_b_qkv': (0.0, 0.8),
     'L0_attn_b_out': (0.0, 0.552),
     'L0_ffn_gamma_light': (1.0, 0.2),
     'L0_ffn_gamma_heavy': (1.0, 0.6)}
    factors = {'L0_attn_w_qkv': 8.0, 'L0_attn_w_ent': 8.0, 'L0_attn_w_out': 8.0}
    for name, (base, spread) in spreads.items():
        noise = np.random.default_rng([zlib.crc32(name.encode()), seed]).standard_normal(out[name].shape)
        drawn = base * np.exp(spread * noise) if base else spread * noise
        out[name] = jnp.asarray(drawn.astype(out[name].dtype))
    for name, factor in factors.items():
        out[name] = (out[name] * factor).astype(out[name].dtype)
    return out
```

```python
from contextlib import ExitStack

import numpy as np

import concourse.bass as bass
from concourse import mybir

P = 128
F32 = mybir.dt.float32
BF16 = mybir.dt.bfloat16
FP16 = mybir.dt.float16
I32 = mybir.dt.int32
ALU = mybir.AluOpType
ACT = mybir.ActivationFunctionType
AX = mybir.AxisListType

B, S, H = 8, 1024, 256
NT = S // P
KT = H // P
NH, HD = 16, 16
HG = 8
UNITS = B * NH // HG
PARTS = 3
QK_ROWS = 6 * HD
VC = PARTS * HD + 1
NCH = 12
RING = NT
LAG = 5
NEG = -1e30
LN_EPS, OUT_EPS = 1e-6, 1e-5
SCALE = 1.0 / (HD ** 0.5) / 0.1
SHIFT = 9.0
Q_SLOT = (0, 0, 1, 0, 2, 1)
K_SLOT = (0, 1, 0, 2, 0, 1)
CAST_ACT = (0, 2, 5, 7)
SUB_DVE = (6, 7)


def s_chunks(t):
    n = P * (t + 1)
    return [(a, min(512, n - a)) for a in range(0, n, 512)]


def t_chunks(j):
    return [(a, min(512, S - a)) for a in range(P * j, S, 512)]


S_AT = [sum(len(s_chunks(x)) for x in range(t)) for t in range(NT + 1)]
P_AT = [S * j - P * j * (j - 1) // 2 for j in range(NT + 1)]
T_AT = [sum(len(t_chunks(x)) for x in range(j)) for j in range(NT + 1)]


def need(eng, sem, value):
    if isinstance(value, int) and value <= 0:
        return
    eng.wait_ge(sem, value)


def among(js, n):
    return len(js) * ((n + 1) // NT) + sum(1 for j in range((n + 1) % NT) if j in js)


def causal_attention(nc, x, ln_g, ln_b, w_qkvT, b_qkv, w_ent, b_ent, w_outT, b_out, stat_dram, part_dram, x1_dram):
    with ExitStack() as ctx:
        def sb(name, shape, dt=F32):
            return ctx.enter_context(nc.sbuf_tensor(name, shape, dt))

        def pb(name, shape, dt=F32):
            return ctx.enter_context(nc.psum_tensor(name, shape, dt))

        def sem(name):
            return ctx.enter_context(nc.semaphore(name))

        ident = sb("ident", [P, P])
        ident_b = sb("ident_b", [P, P], BF16)
        mask_qk = sb("mask_qk", [P, P], BF16)
        mask_kq = sb("mask_kq", [P, P], BF16)
        ones_row = sb("ones_row", [1, P])
        wqk = sb("wqk", [P, KT, 2 * H])
        wv = sb("wv", [P, KT, 2, P + 1])
        bv = sb("bv", [1, 2, P + 1])
        wo = sb("wo", [P, KT, H])
        bo = sb("bo", [P, H])
        bqk = sb("bqk", [P, 4])
        carry = sb("carry", [P, 1])
        gcol = sb("gcol", [P, KT])
        bcol = sb("bcol", [P, KT])
        mhalf = sb("mhalf", [P, NT])
        eps_in = sb("eps_in", [P, NT])
        eps_out = sb("eps_out", [P, NT])
        xin = sb("xin", [P, NT, H])
        xres = sb("xres", [P, NT, H])
        xn = sb("xn", [P, NT, H])
        xnT = sb("xnT", [P, KT, S])
        AO = sb("AO", [P, NT, H])
        AOT = sb("AOT", [P, KT, S])
        stats = sb("stats", [P, NT, 6])
        mv = sb("mv", [P, NT, 2])
        rstd = sb("rstd", [P, NT])
        stats2 = sb("stats2", [P, NT, 6])
        mv2 = sb("mv2", [P, NT, 2])
        rstd2 = sb("rstd2", [P, NT])
        qp = sb("qp", [P, PARTS, S], BF16)
        kp = sb("kp", [P, PARTS, S], BF16)
        rest = sb("rest", [P, 2, 512])
        qs = [sb(f"qs{g}", [QK_ROWS + PARTS, HG, S], BF16) for g in range(2)]
        ks = [sb(f"ks{g}", [QK_ROWS + PARTS, HG, S], BF16) for g in range(2)]
        vx = [sb(f"vx{g}", [P, NT, HG, VC], BF16) for g in range(2)]
        vf = sb("vf", [P, 2, P])
        vr = sb("vr", [P, 2, P])
        gate = sb("gate", [P, 4, 2])
        m2 = sb("m2", [P, HG, NT, 2])
        mn = sb("mn", [P, 4 * NT])
        mr = sb("mr", [P, 4 * NT])
        mp = sb("mp", [P, PARTS, 4 * NT], BF16)
        mt = sb("mt", [PARTS * 4 * NT, P], BF16)
        osum = sb("osum", [P, NT, HD])
        orec = sb("orec", [P, NT])
        pf = sb("pf", [P, P_AT[NT]])
        ph = sb("ph", [P, P_AT[NT]], FP16)
        pl = sb("pl", [P, P_AT[NT]], FP16)

        psS = pb("psS", [P, 3, 512])
        psT = pb("psT", [P, 3, 512])
        psO = pb("psO", [P, 512])
        psM = pb("psM", [P, 512])
        O = psO[:, 0:NT * VC].rearrange("p (t c) -> p t c", c=VC)
        mT = psM[0:PARTS * 4 * NT, 0:P // 2].bitcast(BF16)

        w_in = sem("w_in")
        consts = sem("consts")
        consts_v = sem("consts_v")
        x_in = sem("x_in")
        xr_in = sem("xr_in")
        st_done = sem("st_done")
        rstd_ready = sem("rstd_ready")
        rs_chain = sem("rs_chain")
        xn_ready = sem("xn_ready")
        xt_ready = sem("xt_ready")
        xt_out = sem("xt_out")
        v_ps = sem("v_ps")
        gate_exp = sem("gate_exp")
        v_chain = sem("v_chain")
        v_cast = sem("v_cast")
        v_gate = sem("v_gate")
        y_st = sem("y_st")
        y_ag = sem("y_ag")
        pj_ps = sem("pj_ps")
        pj_hi = sem("pj_hi")
        pj_rest = sem("pj_rest")
        pj_mid = sem("pj_mid")
        pj_lo = sem("pj_lo")
        pt_out = sem("pt_out")
        stk = [[sem(f"stk{g}_{i}") for i in range(2)] for g in range(2)]
        sc = sem("sc")
        mx = sem("mx")
        m_chain = sem("m_chain")
        m_ps = sem("m_ps")
        m_out = sem("m_out")
        m_dram = sem("m_dram")
        m_in = sem("m_in")
        stc = sem("stc")
        ex = sem("ex")
        hi_a = sem("hi_a")
        hi_v = sem("hi_v")
        lo_p = sem("lo_p")
        lo_v = sem("lo_v")
        av = sem("av")
        o_read = sem("o_read")
        o_out = sem("o_out")
        at_ps = sem("at_ps")
        at_out = sem("at_out")
        y_ps = sem("y_ps")
        y_chain = sem("y_chain")
        rs2_chain = sem("rs2_chain")
        rstd2_ready = sem("rstd2_ready")
        y_done = sem("y_done")
        x1_out = sem("x1_out")

        AT_SLOT = (5, 6, 7, 8)
        V_SLOT = (10, 12, 14, 16)
        XT_SLOT = (18, 20, 22, 24)
        PJ_SLOT = {0: (26, 29, 35, 38), 1: (18, 21, 24, 27)}
        M0_SLOT, M1_SLOT = 33, 1
        Y_SLOT = (42, 45, 48, 51)
        LAST = NT * HG

        def flags(b, hg, mid):
            u = 0 if mid else 2 * b + hg

            def ok(v, n):
                return mid or 0 <= v < n
            return dict(
                main=ok(u, UNITS), tail=ok(u - 1, UNITS), ahead=ok(u + 1, UNITS), proj=ok(u + 2, UNITS),
                pre=hg == 0 and ok(b + 1 if not mid else 0, B), epi=hg == 0 and ok(b - 1 if not mid else 0, B))

        def evac_of(kind, b, hg, k):
            u = 2 * b + hg
            if kind == "at":
                return at_out, 4 * (b - 1) + k + 1
            if kind == "v":
                return v_chain, 5 * (4 * (u + 1) + k) + 3
            if kind == "xt":
                return xt_out, 4 * (b + 1) + k + 1
            if kind == "pj":
                return pj_rest, 4 * (u + 2) + k + 1
            if kind == "m0":
                return m_out, 2 * (u + 1) + 1
            if kind == "m1":
                return m_out, 2 * u + 2
            return y_chain, 5 * (4 * (b - 1) + k) + 1

        def tasks(b, hg, mid):
            f = flags(b, hg, mid)
            out = {}
            if f["main"]:
                out[M1_SLOT] = ("m1", 0)
            if f["epi"]:
                out.update({s: ("at", k) for k, s in enumerate(AT_SLOT)})
                out.update({s: ("y", k) for k, s in enumerate(Y_SLOT)})
            if f["ahead"]:
                out.update({s: ("v", k) for k, s in enumerate(V_SLOT)})
                out[M0_SLOT] = ("m0", 0)
            if f["pre"]:
                out.update({s: ("xt", k) for k, s in enumerate(XT_SLOT)})
            if f["proj"]:
                out.update({s: ("pj", k) for k, s in enumerate(PJ_SLOT[hg])})
            return out

        STEPS = [(-1, 0), (-1, 1), (0, 0), (0, 1), None, (B - 1, 0), (B - 1, 1), (B, 0)]

        def before(b, hg, mid, slot):
            own = [s for s in sorted(tasks(b, hg, mid)) if s < slot]
            if own:
                kind, k = tasks(b, hg, mid)[own[-1]]
                return evac_of(kind, b, hg, k)
            pb_, pg = (b, 0) if hg else (b - 1, 1)
            if not mid and pb_ < -1:
                return None
            pmid = mid
            t = tasks(pb_ if not pmid else 0, pg, pmid)
            if not t:
                return None
            kind, k = t[max(t)]
            return evac_of(kind, pb_, pg, k)

        def every_step(eng, step):
            for b, hg in ((-1, 0), (-1, 1), (0, 0), (0, 1), (1, 0), (1, 1)):
                step(b, hg, False)
            with eng.Fori(2, B - 1) as b:
                step(b, 0, True)
                step(b, 1, True)
            for b, hg in ((B - 1, 0), (B - 1, 1), (B, 0)):
                step(b, hg, False)

        def hi_wait(eng, u, n):
            js = CAST_ACT if n % NT in CAST_ACT else [j for j in range(NT) if j not in CAST_ACT]
            need(eng, hi_a if n % NT in CAST_ACT else hi_v, u * (HG * len(js)) + among(js, n))

        def lo_wait(eng, u, n):
            js = SUB_DVE if n % NT in SUB_DVE else [j for j in range(NT) if j not in SUB_DVE]
            need(eng, lo_v if n % NT in SUB_DVE else lo_p, u * (HG * len(js)) + among(js, n))

        def back(u, n, k):
            return (u, n - k) if n >= k else (u - 1, n - k + LAST)

        block = ctx.enter_context(nc.Block())

        @block.sync
        def _(sp):
            for kt in range(KT):
                rows = slice(P * kt, P * kt + P)
                sp.dma_start(wqk[:, kt, :], w_qkvT[rows, 0:2 * H]).then_inc(w_in, 16)
                sp.dma_start(wo[:, kt, :], w_outT[rows, :]).then_inc(w_in, 16)
                for g in range(2):
                    sp.dma_start(wv[:, kt, g, 0:P], w_qkvT[rows, 2 * H + P * g:2 * H + P * g + P]).then_inc(w_in, 16)
                    sp.dma_start(wv[:, kt, g, P:P + 1], w_ent[:, rows].rearrange("a p -> p a")).then_inc(w_in, 16)
                sp.dma_start(gcol[:, kt:kt + 1], ln_g[rows].rearrange("(p a) -> p a", a=1)).then_inc(w_in, 16)
                sp.dma_start(bcol[:, kt:kt + 1], ln_b[rows].rearrange("(p a) -> p a", a=1)).then_inc(w_in, 16)
            for g in range(2):
                sp.dma_start(bv[:, g, 0:P], b_qkv[2 * H + P * g:2 * H + P * g + P].rearrange("(a p) -> a p", a=1)).then_inc(w_in, 16)
                sp.dma_start(bv[:, g, P:P + 1], b_ent.rearrange("(a p) -> a p", a=1)).then_inc(w_in, 16)
            for c in range(4):
                sp.dma_start(bqk[:, c:c + 1], b_qkv[P * c:P * c + P].rearrange("(p a) -> p a", a=1)).then_inc(w_in, 16)
            sp.dma_start(bo[:], b_out.rearrange("(a n) -> a n", a=1).to_broadcast([P, H])).then_inc(w_in, 16)

            def step(b, hg, mid):
                f = flags(b, hg, mid)
                u = 2 * b + hg
                def parts_out():
                    need(sp, pj_lo, 4 * (u + 2) + 4)
                    need(sp, pj_mid, 4 * (u + 2) + 4)
                    for half in range(2):
                        need(sp, stk[1 - hg][half], 192 * ((b + 1) if hg == 0 else (b + 2)))
                    sp.dma_start(part_dram[0].rearrange("c p t -> p c t"), qp[:]).then_inc(pt_out, 16)
                    sp.dma_start(part_dram[1].rearrange("c p t -> p c t"), kp[:]).then_inc(pt_out, 16)

                def stacks(half):
                    if half == 0:
                        need(sp, pt_out, 32 * (u + 3))
                        if mid or u >= 0:
                            need(sp, sc, 8 * NCH * (u + 1))
                    if mid or u >= 0:
                        need(sp, stc, 8 * NCH * u + 4 * NCH * (half + 1))
                    hs = slice(4 * half, 4 * half + 4)
                    feats = slice(4 * HD * half, 4 * HD * half + 4 * HD)
                    for s in range(6):
                        rows = slice(HD * s, HD * s + HD)
                        sp.dma_start(qs[hg][rows, hs, :], part_dram[0, Q_SLOT[s], feats, :].rearrange("(h d) t -> d h t", d=HD))\
                          .then_inc(stk[hg][half], 16)
                        sp.dma_start(ks[hg][rows, hs, :], part_dram[1, K_SLOT[s], feats, :].rearrange("(h d) t -> d h t", d=HD))\
                          .then_inc(stk[hg][half], 16)

                def maxima(uu, half):
                    need(sp, m_out, 2 * uu + half + 1)
                    need(sp, m_in, 16 * (2 * uu + half))
                    sp.dma_start(stat_dram[half], mt[:]).then_inc(m_dram, 16)
                    need(sp, m_dram, 16 * (2 * uu + half + 1))
                    g = hg if half else 1 - hg
                    sp.dma_start(qs[g][QK_ROWS:QK_ROWS + PARTS, 4 * half:4 * half + 4, :],
                                 stat_dram[half].rearrange("(c h t) k -> c h (t k)", c=PARTS, h=4)).then_inc(m_in, 16)

                if f["main"]:
                    maxima(u, 1)
                if f["pre"]:
                    need(sp, xn_ready, NT * (b + 1))
                    sp.dma_start(xin[:], x[b + 1].rearrange("(t p) n -> p t n", p=P)).then_inc(x_in, 16)
                if hg == 1 and (mid or b >= 0):
                    need(sp, y_chain, 20 * b)
                    sp.dma_start(xres[:], x[b].rearrange("(t p) n -> p t n", p=P)).then_inc(xr_in, 16)
                for n in range(LAST):
                    if n == M0_SLOT + 2 and f["ahead"]:
                        maxima(u + 1, 0)
                    if f["proj"] and n == PJ_SLOT[hg][-1] + 2:
                        parts_out()
                    if f["proj"] and n == 42:
                        stacks(0)
                    if f["epi"] and n - 4 in Y_SLOT:
                        k = Y_SLOT.index(n - 4)
                        need(sp, y_done, 4 * (b - 1) + k + 1)
                        sp.dma_start(x1_dram[b - 1][2 * P * k:2 * P * k + 2 * P, :].rearrange("(t p) n -> p t n", p=P),
                                     xn[:, 2 * k:2 * k + 2, :]).then_inc(x1_out, 16)
                if f["proj"]:
                    stacks(1)

            every_step(sp, step)
            sp.wait_ge(x1_out, 16 * 4 * B)

        @block.gpsimd
        def _(pool):
            pool.memset(ident[:], 0.0).then_inc(consts, 1)
            pool.memset(ident_b[:], 0.0).then_inc(consts, 1)
            pool.memset(mask_qk[:], 0.0).then_inc(consts, 1)
            pool.memset(mask_kq[:], 0.0).then_inc(consts, 1)
            pool.memset(mhalf[:], -0.5).then_inc(consts, 1)
            pool.memset(eps_in[:], LN_EPS).then_inc(consts, 1)
            pool.memset(eps_out[:], OUT_EPS).then_inc(consts, 1)
            pool.wait_ge(consts, 7)
            for m in (ident, ident_b):
                pool.affine_select(out=m[:], in_=m[:], compare_op=ALU.not_equal, fill=1.0, base=0,
                                   pattern=[[-1, P]], channel_multiplier=1).then_inc(consts, 1)
            pool.affine_select(out=mask_qk[:], in_=mask_qk[:], compare_op=ALU.is_ge, fill=NEG, base=0,
                               pattern=[[-1, P]], channel_multiplier=1).then_inc(consts, 1)
            pool.affine_select(out=mask_kq[:], in_=mask_kq[:], compare_op=ALU.is_ge, fill=NEG, base=0,
                               pattern=[[1, P]], channel_multiplier=-1).then_inc(consts, 1)

            def step(b, hg, mid):
                f = flags(b, hg, mid)
                u = 2 * b + hg
                for n in range(LAST):
                    if f["main"] and n % NT not in SUB_DVE:
                        cols = slice(P_AT[n % NT], P_AT[n % NT + 1])
                        need(pool, ex, 8 * NCH * u + NCH * (n // NT) + T_AT[n % NT + 1])
                        hi_wait(pool, u, n)
                        need(pool, av, LAST * u + n + 1 - RING)
                        pool.tensor_tensor(pl[:, cols], pf[:, cols], ph[:, cols], ALU.subtract).then_inc(lo_p, 1)
                    if f["pre"] and n == 12:
                        need(pool, st_done, 2 * NT * (b + 2))
                        need(pool, xn_ready, NT * (b + 1))
                        pool.tensor_tensor(rstd[:], mv[:, :, 1], eps_in[:], ALU.add).then_inc(rs_chain, 1)
                        need(pool, rs_chain, b + 2)
                        pool.tensor_tensor(rstd[:], rstd[:], mhalf[:], ALU.pow).then_inc(rstd_ready, 1)
                    if f["epi"] and n - 1 in Y_SLOT:
                        k = Y_SLOT.index(n - 1)
                        i = 4 * (b - 1) + k
                        t = slice(2 * k, 2 * k + 2)
                        need(pool, y_chain, 5 * i + 4)
                        pool.tensor_tensor(rstd2[:, t], mv2[:, t, 1], eps_out[:, t], ALU.add).then_inc(rs2_chain, 1)
                        need(pool, rs2_chain, i + 1)
                        pool.tensor_tensor(rstd2[:, t], rstd2[:, t], mhalf[:, t], ALU.pow).then_inc(rstd2_ready, 1)

            every_step(pool, step)

        @block.scalar
        def _(act):
            act.wait_ge(w_in, 16 * 25)

            def step(b, hg, mid):
                f = flags(b, hg, mid)
                u = 2 * b + hg
                for n in range(LAST):
                    i, j = divmod(n, NT)
                    if f["main"]:
                        pu, pn = back(u, n, RING)
                        if mid or u > 0 or n >= RING:
                            hi_wait(act, pu, pn)
                            lo_wait(act, pu, pn)
                        for c, (a, w) in enumerate(t_chunks(j)):
                            g = NCH * i + T_AT[j] + c
                            need(act, stc, 8 * NCH * u + g + 1)
                            p0 = P_AT[j] + a - P * j
                            act.activation(pf[:, p0:p0 + w], psT[:, g % 3, 0:w], ACT.Exp,
                                           bias=SHIFT, scale=SCALE).then_inc(ex, 1)
                        if j in CAST_ACT:
                            need(act, ex, 8 * NCH * u + NCH * i + T_AT[j + 1])
                            need(act, av, LAST * u + n + 1 - RING)
                            cols = slice(P_AT[j], P_AT[j + 1])
                            act.activation(ph[:, cols], pf[:, cols], ACT.Copy).then_inc(hi_a, 1)
                    if f["ahead"] and n in V_SLOT:
                        k = V_SLOT.index(n)
                        need(act, v_ps, 4 * (u + 1) + k + 1)
                        need(act, v_chain, 5 * (4 * (u + 1) + k))
                        act.activation(gate[:, 0, :], psM[:, 0:2 * (P + 1)].rearrange("p (t c) -> p t c", t=2)[:, :, P],
                                       ACT.Exp, scale=-1.0).then_inc(gate_exp, 1)
                    if f["ahead"] and n - 1 in V_SLOT:
                        k = V_SLOT.index(n - 1)
                        g = 1 - hg
                        i5 = 5 * (4 * (u + 1) + k)
                        need(act, v_chain, i5 + 3)
                        need(act, av, LAST * u)
                        dst = vx[g][:, 2 * k:2 * k + 2, :, :]
                        act.activation(dst[:, :, :, 0:HD], vf[:].rearrange("p t (h d) -> p t h d", d=HD),
                                       ACT.Copy).then_inc(v_cast, 1)
                        need(act, v_chain, i5 + 4)
                        act.activation(dst[:, :, :, HD:2 * HD], vr[:].rearrange("p t (h d) -> p t h d", d=HD),
                                       ACT.Copy).then_inc(v_cast, 1)
                    if f["pre"] and n in XT_SLOT:
                        k = XT_SLOT.index(n)
                        kt, half = divmod(k, 2)
                        need(act, xt_ready, 4 * (b + 1) + k + 1)
                        act.activation(xnT[:, kt, 512 * half:512 * half + 512], psM[:], ACT.Identity,
                                       bias=bcol[:, kt:kt + 1], scale=gcol[:, kt:kt + 1]).then_inc(xt_out, 1)
                    if f["proj"] and n in PJ_SLOT[hg]:
                        k = PJ_SLOT[hg].index(n)
                        half, isk = divmod(k, 2)
                        e = 4 * (u + 2) + k
                        dst = kp if isk else qp
                        cols = slice(512 * half, 512 * half + 512)
                        need(act, pj_ps, e + 1)
                        if k == 0:
                            need(act, pt_out, 32 * (u + 2))
                        act.activation(dst[:, 0, cols], psM[:], ACT.Identity,
                                       bias=bqk[:, 2 * isk + hg:2 * isk + hg + 1]).then_inc(pj_hi, 1)
                    if f["proj"] and n - 1 in PJ_SLOT[hg]:
                        k = PJ_SLOT[hg].index(n - 1)
                        half, isk = divmod(k, 2)
                        e = 4 * (u + 2) + k
                        dst = kp if isk else qp
                        need(act, pj_rest, e + 1)
                        act.activation(dst[:, 1, 512 * half:512 * half + 512], rest[:, k % 2, :],
                                       ACT.Copy).then_inc(pj_mid, 1)
                    if f["epi"] and n in AT_SLOT:
                        k = AT_SLOT.index(n)
                        kt, half = divmod(k, 2)
                        need(act, at_ps, 4 * (b - 1) + k + 1)
                        act.activation(AOT[:, kt, 512 * half:512 * half + 512], psM[:], ACT.Copy).then_inc(at_out, 1)

            every_step(act, step)

        @block.vector
        def _(v):
            for g in range(2):
                v.memset(ks[g][QK_ROWS:QK_ROWS + PARTS, :, :], 1.0).then_inc(consts_v, 1)
                v.memset(vx[g][:, :, :, VC - 1], 1.0).then_inc(consts_v, 1)
            v.memset(m2[:], -3e38).then_inc(consts_v, 1)
            v.memset(ones_row[:], 1.0).then_inc(consts_v, 1)
            v.wait_ge(consts_v, 6)
            v.wait_ge(w_in, 16 * 25)

            def step(b, hg, mid):
                f = flags(b, hg, mid)
                u = 2 * b + hg

                def maxima(uu, half):
                    e = 5 * (2 * uu + half)
                    need(v, mx, 8 * NCH * uu + 4 * NCH * (half + 1))
                    need(v, m_ps, 2 * uu + half)
                    v.tensor_reduce(mn[:], m2[:, 4 * half:4 * half + 4, :, :].rearrange("p h t c -> p (h t) c"), AX.X,
                                    ALU.max, negate=True).then_inc(m_chain, 1)
                    need(v, m_chain, e + 1)
                    v.tensor_copy(mp[:, 0, :], mn[:]).then_inc(m_chain, 1)
                    need(v, m_chain, e + 2)
                    v.tensor_tensor(mr[:], mn[:], mp[:, 0, :], ALU.subtract).then_inc(m_chain, 1)
                    need(v, m_chain, e + 3)
                    v.tensor_copy(mp[:, 1, :], mr[:]).then_inc(m_chain, 1)
                    need(v, m_chain, e + 4)
                    v.tensor_tensor(mp[:, 2, :], mr[:], mp[:, 1, :], ALU.subtract).then_inc(m_chain, 1)

                def maxima_out(uu, half):
                    need(v, m_ps, 2 * uu + half + 1)
                    need(v, m_dram, 16 * (2 * uu + half))
                    v.tensor_copy(mt[:], mT).then_inc(m_out, 1)

                def head_out(uu, bb, g, i):
                    need(v, av, LAST * uu + NT * (i + 1))
                    need(v, o_out, HG * uu + i)
                    v.tensor_reduce(osum[:], O[:, :, 0:PARTS * HD].rearrange("p t (c d) -> p t d c", c=PARTS), AX.X,
                                    ALU.add).then_inc(o_read, 1)
                    v.reciprocal(orec[:], O[:, :, VC - 1]).then_inc(o_read, 1)
                    need(v, o_read, 2 * (HG * uu + i) + 2)
                    if i == 0 and g == 0:
                        need(v, at_ps, 4 * bb)
                    v.tensor_tensor(AO[:, :, P * g + HD * i:P * g + HD * i + HD], osum[:],
                                    orec[:].unsqueeze(2).to_broadcast([P, NT, HD]), ALU.mult).then_inc(o_out, 1)

                for n in range(LAST):
                    i, j = divmod(n, NT)
                    if f["ahead"]:
                        for c, (a, w) in enumerate(s_chunks(j)):
                            g = NCH * i + S_AT[j] + c
                            need(v, sc, 8 * NCH * (u + 1) + g + 1)
                            v.tensor_reduce(m2[:, i, j, c:c + 1], psS[:, g % 3, 0:w], AX.X, ALU.max).then_inc(mx, 1)
                    for d in (1,):
                        pu, pn = back(u, n, d)
                        if (f["main"] if n >= d else f["tail"]):
                            pj_ = pn % NT
                            cols = slice(P_AT[pj_], P_AT[pj_ + 1])
                            if pj_ not in CAST_ACT:
                                need(v, ex, 8 * NCH * pu + NCH * (pn // NT) + T_AT[pj_ + 1])
                                need(v, av, LAST * pu + pn + 1 - RING)
                                v.tensor_copy(ph[:, cols], pf[:, cols]).then_inc(hi_v, 1)
                            if pj_ in SUB_DVE:
                                hi_wait(v, pu, pn)
                                need(v, ex, 8 * NCH * pu + NCH * (pn // NT) + T_AT[pj_ + 1])
                                need(v, av, LAST * pu + pn + 1 - RING)
                                v.tensor_tensor(pl[:, cols], pf[:, cols], ph[:, cols], ALU.subtract).then_inc(lo_v, 1)
                    if (n - LAG) % NT == NT - 1:
                        if n >= LAG and f["main"]:
                            head_out(u, b, hg, (n - LAG) // NT)
                        elif n < LAG and f["tail"]:
                            head_out(u - 1, (b - 1 if hg == 0 else b), 1 - hg, HG - 1)
                    if f["main"] and n == 0:
                        maxima(u, 1)
                    if f["main"] and n == M1_SLOT:
                        maxima_out(u, 1)
                    if f["ahead"] and n == M0_SLOT - 1:
                        maxima(u + 1, 0)
                    if f["ahead"] and n == M0_SLOT:
                        maxima_out(u + 1, 0)
                    if f["pre"] and 8 <= n < 12:
                        if n == 8:
                            need(v, x_in, 16 * (b + 2))
                            need(v, rstd_ready, b + 1)
                        for t in (2 * (n - 8), 2 * (n - 8) + 1):
                            v.bn_stats(stats[:, t, :], xin[:, t, :]).then_inc(st_done, 1)
                            need(v, st_done, 2 * NT * (b + 1) + 2 * t + 1)
                            v.memset(carry[:], 0.0)
                            v.bn_aggr(mv[:, t, :], stats[:, t, :]).then_inc(st_done, 1)
                    if f["pre"] and 14 <= n < 18:
                        if n == 14:
                            need(v, rstd_ready, b + 2)
                            need(v, x1_out, 64 * (b - 1 + 0))
                        for t in (2 * (n - 14), 2 * (n - 14) + 1):
                            v.tensor_scalar(xn[:, t, :], xin[:, t, :], mv[:, t, 0:1], rstd[:, t:t + 1], ALU.subtract,
                                            ALU.mult).then_inc(xn_ready, 1)
                    if f["ahead"] and n in V_SLOT:
                        k = V_SLOT.index(n)
                        i5 = 5 * (4 * (u + 1) + k)
                        need(v, gate_exp, 4 * (u + 1) + k + 1)
                        v.tensor_scalar(gate[:, 1, :], gate[:, 0, :], 1.0, None, ALU.add).then_inc(v_chain, 1)
                        need(v, v_chain, i5 + 1)
                        v.reciprocal(gate[:, 2, :], gate[:, 1, :]).then_inc(v_chain, 1)
                        need(v, v_chain, i5 + 2)
                        v.tensor_scalar(gate[:, 3, :], gate[:, 2, :], 0.1, 2.0, ALU.max, ALU.min).then_inc(v_gate, 1)
                        need(v, v_gate, 4 * (u + 1) + k + 1)
                        need(v, v_cast, 2 * (4 * (u + 1) + k))
                        v.tensor_tensor(vf[:], psM[:, 0:2 * (P + 1)].rearrange("p (t c) -> p t c", t=2)[:, :, 0:P],
                                        gate[:, 3, :].unsqueeze(2).to_broadcast([P, 2, P]), ALU.mult).then_inc(v_chain, 1)
                    if f["ahead"] and n - 1 in V_SLOT:
                        k = V_SLOT.index(n - 1)
                        g = 1 - hg
                        e = 4 * (u + 1) + k
                        dst = vx[g][:, 2 * k:2 * k + 2, :, :]
                        need(v, v_cast, 2 * e + 1)
                        v.tensor_tensor(vr[:].rearrange("p t (h d) -> p t h d", d=HD),
                                        vf[:].rearrange("p t (h d) -> p t h d", d=HD),
                                        dst[:, :, :, 0:HD], ALU.subtract).then_inc(v_chain, 1)
                        need(v, v_cast, 2 * e + 2)
                        need(v, v_chain, 5 * e + 4)
                        v.tensor_tensor(dst[:, :, :, 2 * HD:3 * HD], vr[:].rearrange("p t (h d) -> p t h d", d=HD),
                                        dst[:, :, :, HD:2 * HD], ALU.subtract).then_inc(v_chain, 1)
                    if f["proj"] and n in PJ_SLOT[hg]:
                        k = PJ_SLOT[hg].index(n)
                        half, isk = divmod(k, 2)
                        e = 4 * (u + 2) + k
                        src = (kp if isk else qp)[:, 0, 512 * half:512 * half + 512]
                        need(v, pj_hi, e + 1)
                        need(v, pj_lo, e - 1)
                        need(v, pj_mid, e - 1)
                        v.scalar_tensor_tensor(out=rest[:, k % 2, :], in0=psM[:], scalar=bqk[:, 2 * isk + hg:2 * isk + hg + 1],
                                               in1=src, op0=ALU.add, op1=ALU.subtract).then_inc(pj_rest, 1)
                    if f["proj"] and n - 1 in PJ_SLOT[hg]:
                        k = PJ_SLOT[hg].index(n - 1)
                        half, isk = divmod(k, 2)
                        e = 4 * (u + 2) + k
                        dst = (kp if isk else qp)
                        cols = slice(512 * half, 512 * half + 512)
                        need(v, pj_mid, e + 1)
                        need(v, pj_rest, e + 1)
                        v.tensor_tensor(dst[:, 2, cols], rest[:, k % 2, :], dst[:, 1, cols], ALU.subtract).then_inc(pj_lo, 1)
                    if f["epi"] and n in Y_SLOT:
                        k = Y_SLOT.index(n)
                        e = 5 * (4 * (b - 1) + k)
                        t = slice(2 * k, 2 * k + 2)
                        need(v, y_ps, 4 * (b - 1) + k + 1)
                        if k == 0:
                            need(v, xt_ready, 4 * (b + 2) if f["pre"] else 4 * B)
                            need(v, xr_in, 16 * b)
                        v.tensor_tensor(xn[:, t, :], psM[:].rearrange("p (t n) -> p t n", t=2),
                                        bo[:].unsqueeze(1).to_broadcast([P, 2, H]), ALU.add).then_inc(y_chain, 1)
                        need(v, y_chain, e + 1)
                        v.scalar_tensor_tensor(out=xn[:, t, :], in0=xn[:, t, :], scalar=0.1, in1=xres[:, t, :],
                                               op0=ALU.mult, op1=ALU.add).then_inc(y_chain, 1)
                        need(v, y_chain, e + 2)
                        v.bn_stats(stats2[:, 2 * k, :], xn[:, 2 * k, :]).then_inc(y_st, 1)
                        v.bn_stats(stats2[:, 2 * k + 1, :], xn[:, 2 * k + 1, :]).then_inc(y_chain, 1)
                        need(v, y_st, 4 * (b - 1) + k + 1)
                        need(v, y_chain, e + 3)
                        v.memset(carry[:], 0.0)
                        v.bn_aggr(mv2[:, 2 * k, :], stats2[:, 2 * k, :]).then_inc(y_ag, 1)
                        need(v, y_ag, 4 * (b - 1) + k + 1)
                        v.memset(carry[:], 0.0)
                        v.bn_aggr(mv2[:, 2 * k + 1, :], stats2[:, 2 * k + 1, :]).then_inc(y_chain, 1)
                    if f["epi"] and n - 2 in Y_SLOT:
                        k = Y_SLOT.index(n - 2)
                        e = 4 * (b - 1) + k
                        need(v, rstd2_ready, e + 1)
                        need(v, y_chain, 5 * e + 4)
                        v.tensor_scalar(xn[:, 2 * k, :], xn[:, 2 * k, :], mv2[:, 2 * k, 0:1], rstd2[:, 2 * k:2 * k + 1],
                                        ALU.subtract, ALU.mult).then_inc(y_chain, 1)
                        v.tensor_scalar(xn[:, 2 * k + 1, :], xn[:, 2 * k + 1, :], mv2[:, 2 * k + 1, 0:1],
                                        rstd2[:, 2 * k + 1:2 * k + 2], ALU.subtract, ALU.mult).then_inc(y_done, 1)

            every_step(v, step)

        @block.tensor
        def _(pe):
            pe.wait_ge(w_in, 16 * 25)
            pe.wait_ge(consts, 11)
            pe.wait_ge(consts_v, 6)

            def step(b, hg, mid):
                f = flags(b, hg, mid)
                u = 2 * b + hg
                todo = tasks(b, hg, mid)

                def misc(n):
                    kind, k = todo[n]
                    prev = before(b, hg, mid, n)
                    if prev is not None:
                        need(pe, *prev)
                    if kind in ("m0", "m1"):
                        uu, half = (u, 1) if kind == "m1" else (u + 1, 0)
                        need(pe, m_chain, 5 * (2 * uu + half) + 5)
                        pe.transpose(mT, mp[:].rearrange("p c x -> p (c x)"), ident_b[:]).then_inc(m_ps, 1)
                    elif kind == "at":
                        kt, half = divmod(k, 2)
                        if k == 0:
                            need(pe, o_out, HG * u)
                        for t in range(4):
                            last = pe.transpose(psM[:, P * t:P * t + P], AO[:, 4 * half + t, P * kt:P * kt + P], ident[:])
                        last.then_inc(at_ps, 1)
                    elif kind == "v":
                        need(pe, xt_out, 4 * (b + 1) if hg == 0 else 4 * (b + 2))
                        for t in range(2):
                            o = psM[:, (P + 1) * t:(P + 1) * (t + 1)]
                            tok = P * (2 * k + t)
                            pe.matmul(o, ones_row[:], bv[:, 1 - hg, :], start=True, stop=False)
                            for kt in range(KT):
                                last = pe.matmul(o, xnT[:, kt, tok:tok + P], wv[:, kt, 1 - hg, :], start=False,
                                                 stop=kt == KT - 1)
                        last.then_inc(v_ps, 1)
                    elif kind == "xt":
                        kt, half = divmod(k, 2)
                        need(pe, xn_ready, NT * (b + 1) + 4 * half + 4)
                        for t in range(4):
                            last = pe.transpose(psM[:, P * t:P * t + P], xn[:, 4 * half + t, P * kt:P * kt + P], ident[:])
                        last.then_inc(xt_ready, 1)
                    elif kind == "pj":
                        half, isk = divmod(k, 2)
                        need(pe, xt_out, 4 * (b + 2))
                        col = H * isk + P * hg
                        for kt in range(KT):
                            last = pe.matmul(psM[:], wqk[:, kt, col:col + P], xnT[:, kt, 512 * half:512 * half + 512],
                                             start=kt == 0, stop=kt == KT - 1)
                        last.then_inc(pj_ps, 1)
                    else:
                        need(pe, at_out, 4 * b)
                        for t in range(2):
                            tok = P * (2 * k + t)
                            for kt in range(KT):
                                last = pe.matmul(psM[:, H * t:H * t + H], AOT[:, kt, tok:tok + P], wo[:, kt, :],
                                                 start=kt == 0, stop=kt == KT - 1)
                        last.then_inc(y_ps, 1)

                for n in range(LAST):
                    i, j = divmod(n, NT)
                    if f["ahead"]:
                        g1 = 1 - hg
                        if j == 0 and i % 4 == 0:
                            need(pe, stk[g1][i // 4], 192 * ((b + 1) if hg == 0 else (b + 2)))
                        for c, (a, w) in enumerate(s_chunks(j)):
                            g = NCH * i + S_AT[j] + c
                            need(pe, mx, 8 * NCH * (u + 1) + g + 1 - 3)
                            diag = a + w == P * (j + 1)
                            last = pe.matmul(psS[:, g % 3, 0:w], qs[g1][0:QK_ROWS, i, P * j:P * j + P],
                                             ks[g1][0:QK_ROWS, i, a:a + w], start=True, stop=not diag)
                            if diag:
                                last = pe.matmul(psS[:, g % 3, w - P:w], ident_b[:], mask_qk[:], start=False, stop=True)
                            last.then_inc(sc, 1)
                    if f["main"]:
                        if i in (0, 4) and j == 0:
                            need(pe, m_in, 16 * (2 * u + i // 4 + 1))
                        for c, (a, w) in enumerate(t_chunks(j)):
                            g = NCH * i + T_AT[j] + c
                            need(pe, ex, 8 * NCH * u + g + 1 - 3)
                            last = pe.matmul(psT[:, g % 3, 0:w], ks[hg][:, i, P * j:P * j + P], qs[hg][:, i, a:a + w],
                                             start=True, stop=c > 0)
                            if c == 0:
                                last = pe.matmul(psT[:, g % 3, 0:P], ident_b[:], mask_kq[:], start=False, stop=True)
                            last.then_inc(stc, 1)
                    if (f["main"] if n >= LAG else f["tail"]):
                        pu, pn = back(u, n, LAG)
                        pi, pj_ = divmod(pn, NT)
                        g = hg if n >= LAG else 1 - hg
                        hi_wait(pe, pu, pn)
                        lo_wait(pe, pu, pn)
                        if pj_ == 0:
                            need(pe, o_read, 2 * (HG * pu + pi))
                            if pi == 0:
                                need(pe, v_chain, 20 * (pu + 1))
                        for t in range(pj_, NT):
                            q0 = P_AT[pj_] + P * (t - pj_)
                            for m, part in enumerate((ph, pl)):
                                last = pe.matmul(O[:, t, :], part[:, q0:q0 + P], vx[g][:, pj_, pi, :],
                                                 start=pj_ == 0 and t == 0 and m == 0, stop=pj_ == NT - 1 and m == 1,
                                                 skip_group_check=True)
                        last.then_inc(av, 1)
                    if n in todo:
                        misc(n)

            every_step(pe, step)


D = H
FH, DH = 8, 64
HID = FH * DH
FT = HID // P
WT = B * NT
UW = 4
LSCALE = DH ** -0.5
NQ, NKV = 256, 512
FETCH = 9.0 / 8.0
ITERS = 50
ROUTES = 2
RC = ROUTES * WT


def local_attention(nc, x1_dram, gamma, wq, wkv, wo, q_tok, kv_tok, acc, scol, rcol):
    with ExitStack() as ctx:
        def sb(name, shape, dt=F32):
            return ctx.enter_context(nc.sbuf_tensor(name, shape, dt))

        def pb(name, shape, dt=F32):
            return ctx.enter_context(nc.psum_tensor(name, shape, dt))

        def sem(name):
            return ctx.enter_context(nc.semaphore(name))

        ident = sb("l_ident", [P, P])
        w_q = sb("l_wq", [P, KT, HID])
        w_kv = sb("l_wkv", [P, KT, 2 * HID])
        w_o = sb("l_wo", [P, FT, D])
        gcol = sb("l_gamma", [P, KT])
        toks = sb("l_toks", [P, ROUTES, D])
        half_ = sb("l_half", [P, UW])
        xu = sb("l_xu", [P, 2, UW, D])
        xh = sb("l_xh", [P, UW, D])
        junk = sb("l_junk", [P, 3 * UW, D], BF16)
        ss = sb("l_ss", [P, 2, UW])
        rn = sb("l_rn", [P, 4, UW])
        sr = sb("l_sr", [P, ROUTES, UW])
        xhT = sb("l_xhT", [P, KT, UW * P])
        qT = sb("l_qT", [P, 2, FT, UW * P])
        kT = sb("l_kT", [P, 2, FT, UW * P])
        vv = sb("l_vv", [P, 2, UW, HID])
        nmax = sb("l_nmax", [P, FH])
        sub = sb("l_sub", [P, FH, P])
        pr = sb("l_pr", [P, FH, P])
        rs = sb("l_rs", [P, 2, FH])
        pn = sb("l_pn", [P, FH, P])
        pT = sb("l_pT", [P, FH, P])
        aT = sb("l_aT", [P, FT, P])
        psS = pb("l_psS", [P, FH, P])
        psP = pb("l_psP", [P, FH, P])
        psX = pb("l_psX", [P, 2, 512])
        psA = pb("l_psA", [P, FT, P])
        psY = pb("l_psY", [P, D])

        w_in = sem("l_w_in")
        made = sem("l_made")
        made_v = sem("l_made_v")
        x_in = [sem(f"l_x_in{g}") for g in range(2)]
        x_copied = sem("l_x_copied")
        sq = sem("l_sq")
        sdot = sem("l_sdot")
        root = sem("l_root")
        rch = sem("l_rch")
        xh_ok = sem("l_xh_ok")
        aux = sem("l_aux")
        aux_a = sem("l_aux_a")
        aux_v = sem("l_aux_v")
        s_ps = sem("l_s_ps")
        s_mx = sem("l_s_mx")
        s_sub = sem("l_s_sub")
        s_ex = sem("l_s_ex")
        s_sum = sem("l_s_sum")
        s_n = sem("l_s_n")
        t_ps = sem("l_t_ps")
        t_out = sem("l_t_out")
        a_ps = sem("l_a_ps")
        a_out = sem("l_a_out")
        y_ps = sem("l_y_ps")
        y_out = sem("l_y_out")

        def every_slot(eng, slot):
            for w in range(2, NT):
                slot(-1, w, False)
            for b in (0, 1):
                for w in range(NT):
                    slot(b, w, False)
            with eng.Fori(2, B - 1) as b:
                for w in range(NT):
                    slot(b, w, True)
            for w in range(NT):
                slot(B - 1, w, False)

        def flags(b, w, mid):
            n = 0 if mid else NT * b + w
            unit = 0 if mid else 2 * b + w // UW + 1
            return dict(win=mid or n >= 0, ahead=mid or (-1 <= n < WT - 1),
                        nxt=mid or 0 <= unit < WT // UW, prep=mid or 0 <= unit + 1 < WT // UW)

        def row(h):
            return (h % 2) * (FH // 2) + h // 2

        def projected(b, w):
            return 2 * b + w // UW + 1, (w // UW + 1) % 2

        def prepared(b, w):
            return 2 * b + w // UW + 2, (w // UW) % 2

        def tiles(u, mid):
            return bass.ds(UW * u, UW) if mid else slice(UW * u, UW * u + UW)

        block = ctx.enter_context(nc.Block())

        @block.sync
        def _(sp):
            for kt in range(KT):
                rows = slice(P * kt, P * kt + P)
                sp.dma_start(w_q[:, kt, :], wq[rows, :]).then_inc(w_in, 16)
                sp.dma_start(w_kv[:, kt, :], wkv[rows, :]).then_inc(w_in, 16)
                sp.dma_start(gcol[:, kt:kt + 1], gamma[rows].rearrange("(p a) -> p a", a=1)).then_inc(w_in, 16)
            sp.dma_start(w_o[:], wo.rearrange("(f p) n -> p f n", p=P)).then_inc(w_in, 16)
            for r, tok in enumerate((q_tok, kv_tok)):
                sp.dma_start(toks[:, r, :], tok.rearrange("(a n) -> a n", a=1).to_broadcast([P, D])).then_inc(w_in, 16)

            def load(b, g):
                sp.dma_start(xu[:, g, :, :], x1_dram[b][512 * g:512 * g + 512, :].rearrange("(t p) n -> p t n", p=P))\
                  .then_inc(x_in[g], 16)

            load(0, 0)
            load(0, 1)

            def slot(b, w, mid):
                if w % UW == 0 and (mid or 2 <= 2 * b + w // UW + 2 < WT // UW):
                    u1 = 2 * b + w // UW
                    need(sp, xh_ok, UW * (u1 + 1))
                    need(sp, x_copied, u1 + 1)
                    load(b + 1, w // UW)

            every_slot(sp, slot)

        @block.gpsimd
        def _(pool):
            pool.memset(ident[:], 0.0).then_inc(made, 1)
            pool.memset(half_[:], 0.5).then_inc(made, 1)
            pool.wait_ge(made, 2)
            pool.affine_select(out=ident[:], in_=ident[:], compare_op=ALU.not_equal, fill=1.0, base=0,
                               pattern=[[-1, P]], channel_multiplier=1).then_inc(made, 1)

            def slot(b, w, mid):
                f = flags(b, w, mid)
                u, g = projected(b, w)
                pu, pg = prepared(b, w)
                n = NT * b + w
                if w % UW == 2 and f["prep"]:
                    need(pool, sq, UW * (pu + 1))
                    pool.tensor_tensor(rn[:, 0, :], ss[:, 0, :], half_[:], ALU.pow).then_inc(root, 1)
                if w % UW == 3 and f["prep"]:
                    need(pool, x_in[pg], 16 * (b + 2))
                    pool.tensor_copy(acc[:, tiles(pu, mid), :], xu[:, pg, :, :]).then_inc(x_copied, 1)
                if f["ahead"]:
                    need(pool, s_sum, 2 * (n + 2))
                    need(pool, t_ps, n + 1)
                    pool.tensor_tensor(pn[:], pr[:], rs[:, 1, :].unsqueeze(2).to_broadcast([P, FH, P]),
                                       ALU.mult).then_inc(s_n, 1)

            every_slot(pool, slot)

        @block.scalar
        def _(act):
            def slot(b, w, mid):
                f = flags(b, w, mid)
                u, g = projected(b, w)
                pu, pg = prepared(b, w)
                n = NT * b + w
                if w % UW == 2 and f["prep"]:
                    need(act, x_in[pg], 16 * (b + 2))
                    need(act, root, pu)
                    for t in range(UW):
                        act.activation(junk[:, t, :], xu[:, pg, t, :], ACT.Square, accum_out=ss[:, 0, t:t + 1]).then_inc(sq, 1)
                if f["win"]:
                    for c in range(2):
                        need(act, t_ps, n + 1)
                        need(act, a_ps, n)
                        act.activation(pT[:, 4 * c:4 * c + 4, :], psP[:, 4 * c:4 * c + 4, :], ACT.Copy).then_inc(t_out, 1)
                if f["ahead"]:
                    need(act, s_sub, n + 2)
                    need(act, s_n, n + 1)
                    act.activation(pr[:], sub[:], ACT.Exp, scale=LSCALE).then_inc(s_ex, 1)
                if f["nxt"]:
                    p = w % UW
                    for k in (0, 2):
                        need(act, aux, 4 * (UW * u + p) + k + 1)
                        src = psX[:, 0, :]
                        if p == 0:
                            act.activation(xhT[:, k // 2, 0:256], src[:, 0:256], ACT.Copy).then_inc(aux_a, 1)
                        elif p == 3:
                            act.activation(vv[:, g, k, :], src, ACT.Copy).then_inc(aux_a, 1)
                        else:
                            act.activation((qT if p == 1 else kT)[:, g, k, :], src, ACT.Copy).then_inc(aux_a, 1)

            every_slot(act, slot)

        @block.vector
        def _(v):
            v.wait_ge(w_in, 16 * 9)
            for kt in range(KT):
                v.tensor_scalar(w_q[:, kt, :], w_q[:, kt, :], gcol[:, kt:kt + 1], None, ALU.mult).then_inc(made_v, 1)
                v.tensor_scalar(w_kv[:, kt, :], w_kv[:, kt, :], gcol[:, kt:kt + 1], None, ALU.mult).then_inc(made_v, 1)

            def slot(b, w, mid):
                f = flags(b, w, mid)
                u, g = projected(b, w)
                pu, pg = prepared(b, w)
                n = NT * b + w
                if f["ahead"]:
                    need(v, s_ps, n + 2)
                    v.tensor_reduce(nmax[:], psS[:], AX.X, ALU.max).then_inc(s_mx, 1)
                    need(v, s_mx, n + 2)
                    need(v, s_ex, n + 1)
                    v.tensor_tensor(sub[:], psS[:], nmax[:].unsqueeze(2).to_broadcast([P, FH, P]), ALU.subtract)\
                     .then_inc(s_sub, 1)
                    need(v, s_ex, n + 2)
                    need(v, s_n, n + 1)
                    v.tensor_reduce(rs[:, 0, :], pr[:], AX.X, ALU.add).then_inc(s_sum, 1)
                    need(v, s_sum, 2 * (n + 1) + 1)
                    v.reciprocal(rs[:, 1, :], rs[:, 0, :]).then_inc(s_sum, 1)
                p = w % UW
                if f["nxt"]:
                    for k in (1, 3):
                        need(v, aux, 4 * (UW * u + p) + k + 1)
                        src = psX[:, 1, :]
                        if p == 0:
                            v.tensor_copy(xhT[:, k // 2, 256:512], src[:, 0:256]).then_inc(aux_v, 1)
                        elif p == 3:
                            v.tensor_copy(vv[:, g, k, :], src).then_inc(aux_v, 1)
                        else:
                            v.tensor_copy((qT if p == 1 else kT)[:, g, k, :], src).then_inc(aux_v, 1)
                        if k == 1 and f["win"]:
                            need(v, a_ps, n + 1)
                            need(v, y_ps, n)
                            v.tensor_copy(aT[:], psA[:]).then_inc(a_out, 1)
                elif f["win"]:
                    need(v, a_ps, n + 1)
                    need(v, y_ps, n)
                    v.tensor_copy(aT[:], psA[:]).then_inc(a_out, 1)
                if f["win"]:
                    need(v, y_ps, n + 1)
                    a1 = acc[:, bass.ds(n, 1) if mid else slice(n, n + 1), :]
                    if w % UW == 0:
                        need(v, x_copied, 2 * b + w // UW + 1)
                    v.tensor_tensor(a1, psY[:].unsqueeze(1), a1, ALU.add).then_inc(y_out, 1)
                if p == 2 and f["prep"]:
                    need(v, x_in[pg], 16 * (b + 2))
                    for r in range(ROUTES):
                        for t in range(UW):
                            v.tensor_tensor_reduce(junk[:, UW * (1 + r) + t, :], xu[:, pg, t, :], toks[:, r, :], 1.0, 0.0,
                                                   ALU.mult, ALU.add, sr[:, r, t:t + 1]).then_inc(sdot, 1)
                    for r in range(ROUTES):
                        need(v, sdot, 2 * UW * (pu + 1))
                        v.tensor_copy(scol[:, r, tiles(pu, mid)], sr[:, r, :]).then_inc(rch, 1)
                if p == 3 and f["prep"]:
                    need(v, root, pu + 1)
                    v.tensor_scalar(rn[:, 1, :], rn[:, 0, :], 1e-12, None, ALU.max).then_inc(rch, 1)
                    need(v, rch, 6 * pu + 3)
                    v.reciprocal(rn[:, 2, :], rn[:, 1, :]).then_inc(rch, 1)
                    need(v, rch, 6 * pu + 4)
                    v.tensor_scalar(rn[:, 3, :], rn[:, 2, :], float(D ** 0.5), None, ALU.mult).then_inc(rch, 1)
                    need(v, rch, 6 * pu + 5)
                    v.tensor_copy(rcol[:, tiles(pu, mid)], rn[:, 3, :]).then_inc(rch, 1)
                    need(v, aux, 4 * (UW * (pu - 1) + 1))
                    for t in range(UW):
                        v.tensor_scalar(xh[:, t, :], xu[:, pg, t, :], rn[:, 3, t:t + 1], None, ALU.mult).then_inc(xh_ok, 1)

            every_slot(v, slot)

        @block.tensor
        def _(pe):
            pe.wait_ge(made, 3)
            pe.wait_ge(made_v, 2 * KT)

            def slot(b, w, mid):
                f = flags(b, w, mid)
                u, g = projected(b, w)
                pu, pg = prepared(b, w)
                n = NT * b + w
                p = w % UW

                def piece(k):
                    e = 4 * (UW * u + p) + k
                    need(pe, aux_v if k % 2 else aux_a, 2 * (UW * u + p) + k // 2)
                    out = psX[:, k % 2, :]
                    if p == 0:
                        need(pe, xh_ok, UW * (u + 1))
                        for t in range(2):
                            tt = 2 * (k % 2) + t
                            last = pe.transpose(out[:, P * t:P * t + P], xh[:, tt, P * (k // 2):P * (k // 2) + P], ident[:])
                    else:
                        if p == 1 and k == 0:
                            need(pe, aux_v, 2 * (UW * u + 1))
                            need(pe, aux_a, 2 * (UW * u + 1))
                        for kt in range(KT):
                            if p == 3:
                                lhs, rhs = xhT[:, kt, P * k:P * k + P], w_kv[:, kt, HID:2 * HID]
                            else:
                                lhs, rhs = (w_q, w_kv)[p - 1][:, kt, P * k:P * k + P], xhT[:, kt, :]
                            last = pe.matmul(out, lhs, rhs, start=kt == 0, stop=kt == KT - 1)
                    last.then_inc(aux, 1)

                if f["ahead"]:
                    w1 = (w + 1) % NT
                    g1, tok = (w1 // UW) % 2, P * (w1 % UW)
                    if w1 % UW == 0:
                        need(pe, aux_v, 2 * (UW * u + 3))
                        need(pe, aux_a, 2 * (UW * u + 3))
                    need(pe, s_sub, n + 1)
                    for h in range(FH):
                        r0 = DH * (h % 2)
                        last = pe.matmul(psS[:, row(h), :], qT[r0:r0 + DH, g1, h // 2, tok:tok + P],
                                         kT[r0:r0 + DH, g1, h // 2, tok:tok + P], start=True, stop=True)
                    last.then_inc(s_ps, 1)
                if f["win"]:
                    need(pe, s_n, n + 1)
                    need(pe, t_out, 2 * n)
                    for h in range(FH):
                        last = pe.transpose(psP[:, h, :], pn[:, h, :], ident[:])
                    last.then_inc(t_ps, 1)
                if f["nxt"]:
                    piece(0)
                    piece(1)
                if f["win"]:
                    need(pe, t_out, 2 * n + 2)
                    need(pe, a_out, n)
                    if w % UW == 0:
                        gu = 2 * b + w // UW
                        need(pe, aux_v, 8 * (gu + 1))
                        need(pe, aux_a, 8 * (gu + 1))
                    for h in range(FH):
                        r0 = DH * (h % 2)
                        last = pe.matmul(psA[r0:r0 + DH, h // 2, :], vv[:, (w // UW) % 2, w % UW, DH * h:DH * h + DH],
                                         pT[:, row(h), :], start=True, stop=True)
                    last.then_inc(a_ps, 1)
                if f["nxt"]:
                    piece(2)
                    piece(3)
                if f["win"]:
                    need(pe, a_out, n + 1)
                    need(pe, y_out, n)
                    for ft in range(FT):
                        last = pe.matmul(psY[:], aT[:, ft, :], w_o[:, ft, :], start=ft == 0, stop=ft == FT - 1)
                    last.then_inc(y_ps, 1)

            every_slot(pe, slot)


def routing(nc, scol, slotT, deltaT):
    with ExitStack() as ctx:
        def sb(name, shape, dt=F32):
            return ctx.enter_context(nc.sbuf_tensor(name, shape, dt))

        def pb(name, shape, dt=F32):
            return ctx.enter_context(nc.psum_tensor(name, shape, dt))

        def sem(name):
            return ctx.enter_context(nc.semaphore(name))

        ident = sb("r_ident", [P, P])
        group = sb("r_group", [P, P])
        below = sb("r_below", [P, P])
        logk = sb("r_logk", [P, 1])
        count = sb("r_count", [P, 1])
        sx = sb("r_sx", [P, P + 1])
        cmax = sb("r_cmax", [P, 1])
        rmax = sb("r_rmax", [1, ROUTES * B])
        bmax = sb("r_bmax", [1, ROUTES * B, NT])
        one = sb("r_one", [1, 1])
        na = sb("r_na", [P, 1])
        over = sb("r_over", [P, P + 1])
        under = sb("r_under", [P, P + 1])
        e = sb("r_e", [P, P])
        z = sb("r_z", [P, 1])
        lz = sb("r_lz", [P, 1])
        scr = sb("r_scr", [P, P])
        mid_ = sb("r_mid", [P, P])
        thr = sb("r_thr", [P, 1], I32)
        cand = sb("r_cand", [P, 1], I32)
        keep = sb("r_keep", [P, 1], I32)
        hit = sb("r_hit", [P, P])
        eq = sb("r_eq", [P, P])
        gt = sb("r_gt", [P, P])
        cum = sb("r_cum", [P, P])
        zero = sb("r_zero", [P, P])
        cols = sb("r_cols", [P, 4])
        sel = sb("r_sel", [P, P])
        pos = sb("r_pos", [P, P])
        delta = sb("r_delta", [P, P])
        ps = pb("r_ps", [P, P])
        ps1 = pb("r_ps1", [P, 1])

        made = sem("r_made")
        made_v = sem("r_made_v")
        pe_d = sem("r_pe")
        v_d = sem("r_v")
        a_d = sem("r_a")
        v_i = sem("r_vi")
        v_b = sem("r_vb")
        v_c = sem("r_vc")
        v_t = sem("r_vt")
        NB = 29

        block = ctx.enter_context(nc.Block())

        @block.gpsimd
        def _(pool):
            pool.memset(ident[:], 0.0).then_inc(made, 1)
            pool.memset(group[:], 1.0).then_inc(made, 1)
            pool.wait_ge(made, 2)
            pool.affine_select(out=ident[:], in_=ident[:], compare_op=ALU.not_equal, fill=1.0, base=0,
                               pattern=[[-1, P]], channel_multiplier=1).then_inc(made, 1)
            g3 = group[:].rearrange("p (g c) -> p g c", c=NT)
            pool.affine_select(out=g3, in_=g3, compare_op=ALU.is_ge, fill=0.0, base=0,
                               pattern=[[-NT, P // NT], [0, NT]], channel_multiplier=1).then_inc(made, 1)
            pool.wait_ge(made, 4)
            pool.affine_select(out=g3, in_=g3, compare_op=ALU.is_ge, fill=0.0, base=NT - 1,
                               pattern=[[NT, P // NT], [0, NT]], channel_multiplier=-1).then_inc(made, 1)
            pool.wait_ge(made, 5)
            pool.affine_select(out=below[:], in_=group[:], compare_op=ALU.is_gt, fill=0.0, base=0,
                               pattern=[[1, P]], channel_multiplier=-1).then_inc(made, 1)

        @block.tensor
        def _(pe):
            pe.wait_ge(made, 6)
            pe.wait_ge(v_d, 3)
            pe.transpose(ps[:], scol[:].rearrange("p r t -> p (r t)"), ident[:]).then_inc(pe_d, 1)
            pe.wait_ge(v_d, 5)
            pe.transpose(ps[0:1, :], cmax[:], ident[:]).then_inc(pe_d, 1)
            pe.wait_ge(v_d, 7)
            pe.matmul(ps1[:], bmax[:].rearrange("p g c -> p (g c)"), one[:], start=True, stop=True).then_inc(pe_d, 1)
            with pe.Fori(1, ITERS) as i:
                pe.wait_ge(a_d, 2 * i - 1)
                pe.matmul(ps1[:], group[:], z[:], start=True, stop=True).then_inc(pe_d, 1)
            n = 3 + ITERS - 1
            for bit in range(NB + 1):
                pe.wait_ge(v_c, 3 * bit + 1)
                pe.matmul(ps1[:], group[:], cols[:, 0:1], start=True, stop=True).then_inc(pe_d, 1)
            n += NB + 1
            pe.wait_ge(v_t, 2)
            pe.matmul(ps1[:], group[:], cols[:, 1:2], start=True, stop=True).then_inc(pe_d, 1)
            pe.wait_ge(v_t, 4)
            pe.matmul(ps[:, 0:1], below[:], cols[:, 2:3], start=True, stop=True).then_inc(pe_d, 1)
            pe.wait_ge(v_t, 9)
            pe.matmul(ps1[:], below[:], cols[:, 3:4], start=True, stop=True).then_inc(pe_d, 1)
            pe.wait_ge(v_t, 12)
            pe.transpose(ps[:], pos[:], ident[:]).then_inc(pe_d, 1)
            pe.wait_ge(v_t, 16)
            pe.transpose(ps[:], delta[:], ident[:]).then_inc(pe_d, 1)

        @block.scalar
        def _(act):
            with act.Fori(1, ITERS) as i:
                act.wait_ge(v_i, 3 * i - 1)
                act.activation(e[:], under[:, 0:P], ACT.Exp, bias=under[:, P:P + 1], scale=-1.0,
                               accum_out=z[:]).then_inc(a_d, 1)
                act.wait_ge(pe_d, 3 + i)
                act.activation(lz[:], ps1[:], ACT.Ln).then_inc(a_d, 1)
            act.wait_ge(v_i, 3 * (ITERS - 1) + 1)
            act.activation(scr[:], mid_[:], ACT.Exp).then_inc(a_d, 1)


        @block.vector
        def _(v):
            for r, k in enumerate((NQ * FETCH, NKV * FETCH)):
                rows = slice(WT * r, WT * r + WT)
                v.memset(logk[rows, :], float(np.log(np.float32(k)))).then_inc(made_v, 1)
                v.memset(count[rows, :], float((NQ, NKV)[r])).then_inc(made_v, 1)
                v.memset(na[rows, :], float(np.log(np.float32(S)) - np.log(np.float32(k)))).then_inc(made_v, 1)
            v.memset(one[:], 1.0).then_inc(v_d, 1)
            v.memset(zero[:], 0.0).then_inc(v_d, 1)
            v.memset(thr[:], 0).then_inc(v_d, 1)
            v.wait_ge(made_v, 6)
            v.wait_ge(pe_d, 1)
            v.tensor_copy(sx[:, 0:P], ps[:]).then_inc(v_d, 1)
            v.wait_ge(v_d, 4)
            v.tensor_reduce(cmax[:], sx[:, 0:P], AX.X, ALU.max).then_inc(v_d, 1)
            v.wait_ge(pe_d, 2)
            v.tensor_reduce(rmax[:], ps[0:1, :].rearrange("p (g c) -> p g c", c=NT), AX.X, ALU.max).then_inc(v_d, 1)
            v.wait_ge(v_d, 6)
            v.tensor_copy(bmax[:], rmax[:].unsqueeze(2).to_broadcast([1, ROUTES * B, NT])).then_inc(v_d, 1)
            v.wait_ge(pe_d, 3)
            v.tensor_copy(sx[:, P:P + 1], ps1[:]).then_inc(v_d, 1)
            v.wait_ge(v_d, 8)
            with v.Fori(1, ITERS) as i:
                v.tensor_scalar(over[:], sx[:], na[:, 0:1], 0.0, ALU.subtract, ALU.max).then_inc(v_i, 1)
                v.wait_ge(v_i, 3 * i - 2)
                v.tensor_tensor(under[:], over[:], sx[:], ALU.subtract).then_inc(v_i, 1)
                v.wait_ge(a_d, 2 * i)
                v.tensor_scalar(na[:], lz[:], under[:, P:P + 1], logk[:, 0:1], ALU.subtract, ALU.subtract).then_inc(v_i, 1)
                v.wait_ge(v_i, 3 * i)
            v.tensor_scalar(mid_[:], sx[:, 0:P], na[:, 0:1], 0.0, ALU.subtract, ALU.min).then_inc(v_i, 1)
            v.wait_ge(a_d, 2 * (ITERS - 1) + 1)
            n = 3 + ITERS - 1
            for k, bit in enumerate(range(NB, -1, -1)):
                v.tensor_scalar(cand[:], thr[:], 1 << bit, None, ALU.bitwise_or).then_inc(v_b, 1)
                v.wait_ge(v_b, k + 1)
                v.tensor_scalar(hit[:], scr[:], cand[:].bitcast(F32), 0.0, ALU.is_ge, ALU.add,
                                accum_out=cols[:, 0:1]).then_inc(v_c, 1)
                v.wait_ge(pe_d, n + k + 1)
                v.tensor_tensor(keep[:], ps1[:], count[:], ALU.is_ge).then_inc(v_c, 1)
                v.wait_ge(v_c, 3 * k + 2)
                v.copy_predicated(thr[:], keep[:], cand[:]).then_inc(v_c, 1)
                v.wait_ge(v_c, 3 * k + 3)
            n += NB + 1
            th = thr[:].bitcast(F32)
            v.tensor_scalar(gt[:], scr[:], th, 0.0, ALU.is_gt, ALU.add, accum_out=cols[:, 1:2]).then_inc(v_t, 1)
            v.tensor_scalar(eq[:], scr[:], th, 0.0, ALU.is_equal, ALU.add, accum_out=cols[:, 2:3]).then_inc(v_t, 1)
            v.wait_ge(v_t, 2)
            v.tensor_tensor_scan(cum[:], eq[:], zero[:], 0.0, ALU.add, ALU.add).then_inc(v_t, 1)
            v.wait_ge(pe_d, n + 1)
            v.tensor_tensor(cmax[:], count[:], ps1[:], ALU.subtract).then_inc(v_t, 1)
            v.wait_ge(pe_d, n + 2)
            v.wait_ge(v_t, 4)
            v.tensor_scalar(cum[:], cum[:], ps[:, 0:1], cmax[:, 0:1], ALU.add, ALU.is_le).then_inc(v_t, 1)
            v.wait_ge(v_t, 5)
            v.tensor_tensor(eq[:], eq[:], cum[:], ALU.mult).then_inc(v_t, 1)
            v.wait_ge(v_t, 6)
            v.tensor_tensor(sel[:], gt[:], eq[:], ALU.add).then_inc(v_t, 1)
            v.wait_ge(v_t, 7)
            v.tensor_reduce(cols[:, 3:4], sel[:], AX.X, ALU.add).then_inc(v_t, 1)
            v.tensor_tensor_scan(cum[:], sel[:], zero[:], 0.0, ALU.add, ALU.add).then_inc(v_t, 1)
            v.wait_ge(pe_d, n + 3)
            v.wait_ge(v_t, 9)
            v.tensor_scalar(cum[:], cum[:], ps1[:, 0:1], None, ALU.add).then_inc(v_t, 1)
            v.wait_ge(v_t, 10)
            v.tensor_tensor(cum[:], cum[:], sel[:], ALU.mult).then_inc(v_t, 1)
            v.wait_ge(v_t, 11)
            v.tensor_scalar(pos[:], cum[:], -1.0, None, ALU.add).then_inc(v_t, 1)
            v.tensor_scalar(delta[:], scr[:], -1.0, 1.0, ALU.mult, ALU.add).then_inc(v_t, 1)
            v.wait_ge(v_t, 13)
            v.tensor_tensor(delta[:], delta[:], scr[:], ALU.add).then_inc(v_t, 1)
            v.wait_ge(v_t, 14)
            v.tensor_scalar(delta[:], delta[:], -1.0, None, ALU.add).then_inc(v_t, 1)
            v.wait_ge(pe_d, n + 4)
            v.tensor_copy(slotT[:], ps[:]).then_inc(v_t, 1)
            v.wait_ge(pe_d, n + 5)
            v.tensor_copy(deltaT[:], ps[:]).then_inc(v_t, 1)


ST = NQ // P
VT = NKV // P
BLOCKS = FH * ST


def routed_attention(nc, x1_dram, gamma, wq, wkvT, wo, acc, rcol, slotT, deltaT, out):
    with ExitStack() as ctx:
        def sb(name, shape, dt=F32):
            return ctx.enter_context(nc.sbuf_tensor(name, shape, dt))

        def pb(name, shape, dt=F32):
            return ctx.enter_context(nc.psum_tensor(name, shape, dt))

        def sem(name):
            return ctx.enter_context(nc.semaphore(name))

        ident = sb("h_ident", [P, P])
        ident_b = sb("h_ident_b", [P, P], BF16)
        iota_i = sb("h_iota_i", [P, NKV], I32)
        iota = sb("h_iota", [P, NKV], FP16)
        w_q = sb("h_wq", [P, KT, HID])
        w_k = sb("h_wk", [P, KT, HID])
        w_v = sb("h_wv", [P, KT, HID])
        w_o = sb("h_wo", [P, FT, D])
        gcol = sb("h_gamma", [P, KT])
        mhalf = sb("h_mhalf", [P, NT])
        eps = sb("h_eps", [P, NT])
        xb = sb("h_xb", [P, NT, D])
        xh = sb("h_xh", [P, NT, D])
        xr = sb("h_xr", [P, NT, D])
        xp = sb("h_xp", [P, NT, PARTS, D], BF16)
        oq = sb("h_oq", [P, NT, NQ], BF16)
        ok = sb("h_ok", [P, NT, NKV], BF16)
        oqT = sb("h_oqT", [P, ST, S], BF16)
        col = sb("h_col", [P, 4, NT])
        dcol = sb("h_dcol", [P, NT], BF16)
        xk = sb("h_xk", [P, KT, NKV])
        xq = sb("h_xq", [P, KT, NQ])
        svk = sb("h_svk", [P, VT])
        qh = sb("h_qh", [P, FT, NQ])
        kh = sb("h_kh", [P, FT, NKV])
        vh = sb("h_vh", [P, VT, HID])
        nm = sb("h_nm", [P, 4, 2])
        rs = sb("h_rs", [P, 4, 2])
        pr = sb("h_pr", [P, 4, NKV])
        pT = sb("h_pT", [P, 2, VT, NQ])
        aT = sb("h_aT", [P, FT, NQ])
        rr = sb("h_rr", [P, ST, D])
        rp = sb("h_rp", [P, ST, PARTS, D], BF16)
        y = sb("h_y", [P, NT, D])
        stats = sb("h_stats", [P, NT, 6])
        mv = sb("h_mv", [P, NT, 2])
        rstd = sb("h_rstd", [P, NT])
        carry = sb("h_carry", [P, 2])
        RB = 6
        ring = pb("h_ring", [P, RB, 512])
        psA = pb("h_psA", [P, FT, NQ])

        w_in = sem("h_w_in")
        made = sem("h_made")
        made_v = sem("h_made_v")
        x_in = sem("h_x_in")
        c_ok = sem("h_c_ok")
        xh_ok = sem("h_xh_ok")
        x_hi = sem("h_x_hi")
        x_re = sem("h_x_re")
        x_mi = sem("h_x_mi")
        x_lo = sem("h_x_lo")
        oh_ok = sem("h_oh_ok")
        gath = sem("h_gath")
        unit = sem("h_unit")
        ev_a = sem("h_ev_a")
        ev_v = sem("h_ev_v")
        nmx = sem("h_nmx")
        exq = sem("h_exq")
        rec = sem("h_rec")
        nrm = sem("h_nrm")
        ptc = sem("h_ptc")
        av = sem("h_av")
        at_a = sem("h_at_a")
        at_v = sem("h_at_v")
        r_hi = sem("h_r_hi")
        r_re = sem("h_r_re")
        r_mi = sem("h_r_mi")
        r_lo = sem("h_r_lo")
        y_ok = sem("h_y_ok")
        st_ok = sem("h_st_ok")
        ag_ok = sem("h_ag_ok")
        rch = sem("h_rch")
        r_ok = sem("h_r_ok")
        o_ok = sem("h_o_ok")
        o_out = sem("h_o_out")

        U_OHT, U_GK, U_GQ, U_GD, U_Q, U_K, U_V, U_S = 0, 2, 4, 5, 6, 8, 12, 16
        U_WO, U_SC, NU = 48, 50, 54

        def u_s(i):
            return U_S + i if i < 2 else U_S + 3 + 2 * (i - 2)

        def u_pt(i):
            return U_S + 2 + 2 * i if i < BLOCKS - 2 else U_S + 2 * (BLOCKS - 2) + 2 + i - (BLOCKS - 2)

        BY_A = [0, 1, U_GK, U_GQ, U_Q, U_K, U_K + 2, U_V, U_V + 2]
        BY_V = [U_GK + 1, U_GD, U_Q + 1, U_K + 1, U_K + 3, U_V + 1, U_V + 3, U_WO, U_WO + 1, *range(U_SC, NU)]
        S_OF = {u_s(i): i for i in range(BLOCKS)}
        PT_OF = {u_pt(i): i for i in range(BLOCKS)}

        def left(b, k):
            if k < 0:
                b, k = b - 1, k + NU
            if k in BY_A:
                return ev_a, len(BY_A) * b + BY_A.index(k) + 1
            if k in BY_V:
                return ev_v, len(BY_V) * b + BY_V.index(k) + 1
            if k in S_OF:
                return exq, BLOCKS * b + S_OF[k] + 1
            return ptc, BLOCKS * b + PT_OF[k] + 1

        def bank(k):
            return ring[:, k % RB, :]

        def every_batch(eng, first, batch):
            first()
            batch(0, False, True)
            with eng.Fori(1, B - 1) as b:
                batch(b, True, True)
            batch(B - 1, False, False)

        block = ctx.enter_context(nc.Block())

        @block.sync
        def _(sp):
            heads = wkvT.rearrange("(t p) (h c d) -> t p h c d", p=P, c=2, d=DH)
            for kt in range(KT):
                rows = slice(P * kt, P * kt + P)
                sp.dma_start(w_q[:, kt, :], wq[rows, :]).then_inc(w_in, 16)
                for c, w in enumerate((w_k, w_v)):
                    sp.dma_start(w[:, kt, :].rearrange("p (h d) -> p h d", d=DH), heads[kt, :, :, c, :]).then_inc(w_in, 16)
                sp.dma_start(gcol[:, kt:kt + 1], gamma[rows].rearrange("(p a) -> p a", a=1)).then_inc(w_in, 16)
            sp.dma_start(w_o[:], wo.rearrange("(f p) n -> p f n", p=P)).then_inc(w_in, 16)

            def load(b):
                sp.dma_start(xb[:], x1_dram[b].rearrange("(t p) n -> p t n", p=P)).then_inc(x_in, 16)

            def batch(b, mid, more):
                if more:
                    need(sp, xh_ok, NT * (b + 1))
                    load(b + 1)
                need(sp, o_ok, NT * (b + 1))
                sp.dma_start(out[b].rearrange("(t p) n -> p t n", p=P), y[:]).then_inc(o_out, 16)

            every_batch(sp, lambda: load(0), batch)
            sp.wait_ge(o_out, 16 * B)

        @block.gpsimd
        def _(pool):
            for k, m in enumerate((ident, ident_b)):
                pool.memset(m[:], 0.0).then_inc(made, 1)
                pool.wait_ge(made, 2 * k + 1)
                pool.affine_select(out=m[:], in_=m[:], compare_op=ALU.not_equal, fill=1.0, base=0,
                                   pattern=[[-1, P]], channel_multiplier=1).then_inc(made, 1)
            pool.iota(iota_i[:], pattern=[[1, NKV]], base=0, channel_multiplier=0).then_inc(made, 1)
            pool.memset(mhalf[:], -0.5).then_inc(made, 1)
            pool.memset(eps[:], OUT_EPS).then_inc(made, 1)

            def parts(b, c, step):
                e = NT * b + c
                if step == 0:
                    need(pool, x_hi, e + 1)
                    need(pool, x_mi, NT * (b - 1) + c + 1)
                    pool.tensor_tensor(xr[:, c, :], xh[:, c, :], xp[:, c, 0, :], ALU.subtract).then_inc(x_re, 1)
                else:
                    need(pool, x_mi, e + 1)
                    need(pool, x_re, e + 1)
                    pool.tensor_tensor(xp[:, c, 2, :], xr[:, c, :], xp[:, c, 1, :], ALU.subtract).then_inc(x_lo, 1)

            def batch(b, mid, more):
                for i in range(BLOCKS):
                    if more:
                        parts(b + 1, i // 2, i % 2)
                need(pool, ag_ok, NT * (b + 1))
                pool.tensor_tensor(rstd[:], mv[:, :, 1], eps[:], ALU.add).then_inc(rch, 1)
                need(pool, rch, b + 1)
                pool.tensor_tensor(rstd[:], rstd[:], mhalf[:], ALU.pow).then_inc(r_ok, 1)

            def first():
                pool.wait_ge(made, 7)
                for i in range(BLOCKS):
                    parts(0, i // 2, i % 2)

            every_batch(pool, first, batch)

        @block.scalar
        def _(act):
            def parts(b, c, step):
                e = NT * b + c
                if step == 0:
                    need(act, xh_ok, e + 1)
                    need(act, gath, b)
                    act.activation(xp[:, c, 0, :], xh[:, c, :], ACT.Copy).then_inc(x_hi, 1)
                else:
                    need(act, x_re, e + 1)
                    act.activation(xp[:, c, 1, :], xr[:, c, :], ACT.Copy).then_inc(x_mi, 1)

            def batch(b, mid, more):
                def filled(k):
                    need(act, unit, NU * b + k + 1)

                for k in BY_A:
                    filled(k)
                    src = bank(k)
                    if k < 2:
                        o = act.activation(oqT[:, k, :], src.bitcast(BF16), ACT.Copy)
                    elif k == U_GK:
                        o = act.activation(xk[:, 0, :], src, ACT.Copy)
                    elif k == U_GQ:
                        o = act.activation(xq[:].rearrange("p t n -> p (t n)"), src, ACT.Copy)
                    elif k == U_Q:
                        o = act.activation(qh[:, 0:2, :].rearrange("p t n -> p (t n)"), src, ACT.Copy)
                    elif k < U_V:
                        o = act.activation(kh[:, k - U_K, :], src, ACT.Copy)
                    else:
                        if k == U_V:
                            need(act, ev_v, len(BY_V) * b + BY_V.index(U_GD) + 1)
                        o = act.activation(vh[:, k - U_V, :], src, ACT.Copy, scale=svk[:, k - U_V:k - U_V + 1])
                    o.then_inc(ev_a, 1)

                def block_exp(i):
                    e = BLOCKS * b + i
                    need(act, nmx, 2 * e + 2)
                    need(act, nrm, e - 3)
                    need(act, unit, NU * b + u_pt(i - 4) + 1) if i >= 4 else need(act, unit, NU * (b - 1) + u_pt(i + BLOCKS - 4) + 1)
                    act.activation(pr[:, i % 4, :], bank(u_s(i)), ACT.Exp, bias=nm[:, i % 4, 1:2], scale=LSCALE,
                                   accum_out=rs[:, i % 4, 0:1]).then_inc(exq, 1)

                def block_out(i):
                    h, qt = divmod(i, ST)
                    filled(u_pt(i))
                    need(act, av, FH * b + h - 1)
                    act.activation(pT[:, h % 2, :, P * qt:P * qt + P], bank(u_pt(i)).rearrange("p (t q) -> p t q", q=P),
                                   ACT.Copy).then_inc(ptc, 1)

                block_exp(0)
                for i in range(BLOCKS):
                    if i + 1 < BLOCKS:
                        block_exp(i + 1)
                    if i >= 1:
                        block_out(i - 1)
                    if more:
                        parts(b + 1, i // 2, i % 2)
                block_out(BLOCKS - 1)
                need(act, av, FH * (b + 1))
                act.activation(aT[:, 0:2, :], psA[:, 0:2, :], ACT.Copy).then_inc(at_a, 1)
                for s in range(ST):
                    filled(U_WO + s)
                    need(act, unit, NU * b)
                    act.activation(rp[:, s, 0, :], bank(U_WO + s)[:, 0:D], ACT.Copy).then_inc(r_hi, 1)
                for s in range(ST):
                    need(act, r_re, ST * b + s + 1)
                    act.activation(rp[:, s, 1, :], rr[:, s, :], ACT.Copy).then_inc(r_mi, 1)

            def first():
                for i in range(BLOCKS):
                    parts(0, i // 2, i % 2)

            every_batch(act, first, batch)

        @block.vector
        def _(v):
            v.wait_ge(w_in, 16 * 9)
            for kt in range(KT):
                for w in (w_q, w_k, w_v):
                    v.tensor_scalar(w[:, kt, :], w[:, kt, :], gcol[:, kt:kt + 1], None, ALU.mult).then_inc(made_v, 1)
            v.wait_ge(made, 7)
            v.tensor_copy(iota[:], iota_i[:]).then_inc(made_v, 1)
            v.wait_ge(made_v, 7)

            def stage(b, mid):
                t = bass.ds(NT * b, NT) if mid else slice(NT * b, NT * b + NT)
                t2 = bass.ds(NT * b + WT, NT) if mid else slice(NT * b + WT, NT * b + WT + NT)
                need(v, gath, b)
                v.tensor_copy(col[:, 0, :], slotT[:, t]).then_inc(c_ok, 1)
                v.tensor_copy(col[:, 1, :], slotT[:, t2]).then_inc(c_ok, 1)
                v.tensor_copy(col[:, 2, :], rcol[:, t]).then_inc(c_ok, 1)
                v.tensor_copy(dcol[:], deltaT[:, t2]).then_inc(c_ok, 1)
                need(v, c_ok, 4 if not mid and b == 0 else 5 * b + 3)

            def chunk(b, c):
                if c == 0:
                    need(v, x_in, 16 * (b + 1))
                need(v, x_re, NT * (b - 1) + c + 1)
                v.tensor_scalar(xh[:, c, :], xb[:, c, :], col[:, 2, c:c + 1], None, ALU.mult).then_inc(xh_ok, 1)
                v.tensor_scalar(oq[:, c, :], iota[:, 0:NQ], col[:, 0, c:c + 1], None, ALU.is_equal).then_inc(oh_ok, 1)
                v.tensor_scalar(ok[:, c, :], iota[:], col[:, 1, c:c + 1], None, ALU.is_equal).then_inc(oh_ok, 1)

            def batch(b, mid, more):
                def filled(k):
                    need(v, unit, NU * b + k + 1)

                for k in BY_V[:7]:
                    filled(k)
                    src = bank(k)
                    if k == U_GK + 1:
                        o = v.tensor_copy(xk[:, 1, :], src)
                    elif k == U_GD:
                        o = v.tensor_scalar(svk[:], src[:, 0:VT], 1.0, None, ALU.add)
                    elif k == U_Q + 1:
                        o = v.tensor_copy(qh[:, 2:4, :].rearrange("p t n -> p (t n)"), src)
                    elif k < U_V:
                        o = v.tensor_copy(kh[:, k - U_K, :], src)
                    else:
                        if k == U_V + 1:
                            need(v, ev_v, len(BY_V) * b + BY_V.index(U_GD) + 1)
                        o = v.tensor_scalar(vh[:, k - U_V, :], src, svk[:, k - U_V:k - U_V + 1], None, ALU.mult)
                    o.then_inc(ev_v, 1)

                def block_max(i):
                    e = BLOCKS * b + i
                    filled(u_s(i))
                    need(v, exq, e - 3)
                    v.tensor_reduce(nm[:, i % 4, 0:1], bank(u_s(i)), AX.X, ALU.max, negate=True).then_inc(nmx, 1)
                    need(v, nmx, 2 * e + 1)
                    v.tensor_scalar(nm[:, i % 4, 1:2], nm[:, i % 4, 0:1], LSCALE, None, ALU.mult).then_inc(nmx, 1)

                def block_norm(i):
                    e = BLOCKS * b + i
                    need(v, exq, e + 1)
                    v.reciprocal(rs[:, i % 4, 1:2], rs[:, i % 4, 0:1]).then_inc(rec, 1)
                    need(v, rec, e + 1)
                    v.tensor_scalar(pr[:, i % 4, :], pr[:, i % 4, :], rs[:, i % 4, 1:2], None, ALU.mult).then_inc(nrm, 1)

                block_max(0)
                for i in range(BLOCKS):
                    if i + 1 < BLOCKS:
                        block_max(i + 1)
                    block_norm(i)
                    if more:
                        if i == 0:
                            stage(b + 1, mid)
                        if i % 2 == 0:
                            chunk(b + 1, i // 2)
                need(v, av, FH * (b + 1))
                v.tensor_copy(aT[:, 2:4, :], psA[:, 2:4, :]).then_inc(at_v, 1)
                for s in range(ST):
                    need(v, r_hi, ST * b + s + 1)
                    need(v, r_mi, ST * (b - 1) + s + 1)
                    v.tensor_tensor(rr[:, s, :], bank(U_WO + s)[:, 0:D], rp[:, s, 0, :], ALU.subtract).then_inc(r_re, 1)
                    need(v, r_re, ST * b + s + 1)
                    v.sem_inc(ev_v, 1)
                for s in range(ST):
                    need(v, r_mi, ST * b + s + 1)
                    v.tensor_tensor(rp[:, s, 2, :], rr[:, s, :], rp[:, s, 1, :], ALU.subtract).then_inc(r_lo, 1)
                t = bass.ds(NT * b, NT) if mid else slice(NT * b, NT * b + NT)
                v.tensor_scalar(col[:, 3, :], deltaT[:, t], 1.0, None, ALU.add).then_inc(c_ok, 1)
                need(v, c_ok, 5 * b + 5 + (4 if more else 0))
                need(v, o_out, 16 * b)
                for k in range(NT // 2):
                    filled(U_SC + k)
                    for c in range(2):
                        tt = 2 * k + c
                        at = acc[:, bass.ds(NT * b + tt, 1), :] if mid else acc[:, NT * b + tt:NT * b + tt + 1, :]
                        o = v.scalar_tensor_tensor(out=y[:, tt:tt + 1, :], in0=bank(U_SC + k)[:, D * c:D * c + D].unsqueeze(1),
                                                   scalar=col[:, 3, tt:tt + 1], in1=at, op0=ALU.mult, op1=ALU.add)
                        o.then_inc(y_ok, 1) if c == 0 else o.then_inc(ev_v, 1)
                    need(v, y_ok, NT // 2 * b + k + 1)
                    v.bn_stats(stats[:, 2 * k, :], y[:, 2 * k, :]).then_inc(st_ok, 1)
                    need(v, ev_v, len(BY_V) * b + BY_V.index(U_SC + k) + 1)
                    v.bn_stats(stats[:, 2 * k + 1, :], y[:, 2 * k + 1, :]).then_inc(st_ok, 1)
                need(v, st_ok, NT * (b + 1))
                v.memset(carry[:, 0:1], 0.0)
                for tt in range(NT):
                    v.bn_aggr(mv[:, tt, :], stats[:, tt, :]).then_inc(ag_ok, 1)
                need(v, r_ok, b + 1)
                for tt in range(NT):
                    v.tensor_scalar(y[:, tt, :], y[:, tt, :], mv[:, tt, 0:1], rstd[:, tt:tt + 1], ALU.subtract,
                                    ALU.mult).then_inc(o_ok, 1)

            def first():
                stage(0, False)
                for c in range(NT):
                    chunk(0, c)

            every_batch(v, first, batch)

        @block.tensor
        def _(pe):
            pe.wait_ge(made, 7)
            pe.wait_ge(made_v, 7)

            def batch(b, mid, more):
                def fill(k):
                    need(pe, *left(b, k - RB))

                for s in range(ST):
                    fill(U_OHT + s)
                    need(pe, oh_ok, 2 * NT * (b + 1))
                    o = bank(U_OHT + s).bitcast(BF16)
                    for c in range(NT):
                        last = pe.transpose(o[:, P * c:P * c + P], oq[:, c, P * s:P * s + P], ident_b[:])
                    last.then_inc(unit, 1)
                need(pe, x_lo, NT * (b + 1))
                for ft in range(KT):
                    fill(U_GK + ft)
                    for c in range(NT):
                        for m in range(PARTS):
                            last = pe.matmul(bank(U_GK + ft), xp[:, c, m, P * ft:P * ft + P], ok[:, c, :],
                                             start=c == 0 and m == 0, stop=c == NT - 1 and m == PARTS - 1)
                    last.then_inc(unit, 1)
                fill(U_GQ)
                for ft in range(KT):
                    for c in range(NT):
                        for m in range(PARTS):
                            last = pe.matmul(bank(U_GQ)[:, NQ * ft:NQ * ft + NQ], xp[:, c, m, P * ft:P * ft + P],
                                             oq[:, c, :], start=c == 0 and m == 0, stop=c == NT - 1 and m == PARTS - 1)
                last.then_inc(unit, 1)
                fill(U_GD)
                for s in range(VT):
                    for c in range(NT):
                        last = pe.matmul(bank(U_GD)[:, s:s + 1], ok[:, c, P * s:P * s + P], dcol[:, c:c + 1],
                                         start=c == 0, stop=c == NT - 1)
                last.then_inc(unit, 1)
                need(pe, unit, NU * b + U_GD + 1)
                pe.sem_inc(gath, 1)
                for k in range(2):
                    fill(U_Q + k)
                    need(pe, *left(b, U_GQ))
                    for f in range(2):
                        for kt in range(KT):
                            ft = 2 * k + f
                            last = pe.matmul(bank(U_Q + k)[:, NQ * f:NQ * f + NQ], w_q[:, kt, P * ft:P * ft + P], xq[:, kt, :],
                                             start=kt == 0, stop=kt == KT - 1)
                    last.then_inc(unit, 1)
                need(pe, *left(b, U_GK))
                need(pe, *left(b, U_GK + 1))
                for ft in range(FT):
                    fill(U_K + ft)
                    for kt in range(KT):
                        last = pe.matmul(bank(U_K + ft), w_k[:, kt, P * ft:P * ft + P], xk[:, kt, :], start=kt == 0,
                                         stop=kt == KT - 1)
                    last.then_inc(unit, 1)
                for s in range(VT):
                    fill(U_V + s)
                    for kt in range(KT):
                        last = pe.matmul(bank(U_V + s), xk[:, kt, P * s:P * s + P], w_v[:, kt, :], start=kt == 0,
                                         stop=kt == KT - 1)
                    last.then_inc(unit, 1)

                def scores(i):
                    h, qt = divmod(i, ST)
                    r0 = DH * (h % 2)
                    fill(u_s(i))
                    pe.matmul(bank(u_s(i)), qh[r0:r0 + DH, h // 2, P * qt:P * qt + P], kh[r0:r0 + DH, h // 2, :],
                              start=True, stop=True).then_inc(unit, 1)

                def values(h):
                    need(pe, ptc, BLOCKS * b + ST * (h + 1))
                    if h == 0:
                        need(pe, at_a, b)
                        need(pe, at_v, b)
                    r0 = DH * (h % 2)
                    for t in range(VT):
                        last = pe.matmul(psA[r0:r0 + DH, h // 2, :], vh[:, t, DH * h:DH * h + DH], pT[:, h % 2, t, :],
                                         start=t == 0, stop=t == VT - 1)
                    last.then_inc(av, 1)

                need(pe, *left(b, U_K + 2))
                need(pe, *left(b, U_K + 3))
                need(pe, *left(b, U_V + 2))
                need(pe, *left(b, U_V + 3))
                scores(0)
                scores(1)
                for i in range(BLOCKS):
                    need(pe, nrm, BLOCKS * b + i + 1)
                    fill(u_pt(i))
                    for t in range(VT):
                        last = pe.transpose(bank(u_pt(i))[:, P * t:P * t + P], pr[:, i % 4, P * t:P * t + P], ident[:])
                    last.then_inc(unit, 1)
                    if i + 2 < BLOCKS:
                        scores(i + 2)
                    if i % ST == 0 and i >= ST:
                        values(i // ST - 1)
                values(FH - 1)
                need(pe, at_a, b + 1)
                need(pe, at_v, b + 1)
                for s in range(ST):
                    fill(U_WO + s)
                    for ft in range(FT):
                        last = pe.matmul(bank(U_WO + s)[:, 0:D], aT[:, ft, P * s:P * s + P], w_o[:, ft, :], start=ft == 0,
                                         stop=ft == FT - 1)
                    last.then_inc(unit, 1)
                need(pe, r_lo, ST * (b + 1))
                for k in range(NT // 2):
                    fill(U_SC + k)
                    for c in range(2):
                        t0 = P * (2 * k + c)
                        for s in range(ST):
                            for m in range(PARTS):
                                last = pe.matmul(bank(U_SC + k)[:, D * c:D * c + D], oqT[:, s, t0:t0 + P], rp[:, s, m, :],
                                                 start=s == 0 and m == 0, stop=s == ST - 1 and m == PARTS - 1)
                    last.then_inc(unit, 1)

            every_batch(pe, lambda: None, batch)


def build(nc, a, out):
    nc.disable_value_cache = True
    stat = nc.dram_tensor("max_scratch", (2, PARTS * 4 * NT, P), BF16, kind="Internal").ap()
    part = nc.dram_tensor("part_scratch", (2, PARTS, P, S), BF16, kind="Internal").ap()
    x1 = nc.dram_tensor("x1_scratch", (B, S, H), F32, kind="Internal").ap()
    causal_attention(nc, a["L0_attn_x"], a["L0_attn_ln_g"], a["L0_attn_ln_b"], a["L0_attn_w_qkv"], a["L0_attn_b_qkv"],
                     a["L0_attn_w_ent"], a["L0_attn_b_ent"], a["L0_attn_w_out"], a["L0_attn_b_out"], stat, part, x1)
    with ExitStack() as ctx:
        def sb(name, shape):
            return ctx.enter_context(nc.sbuf_tensor(name, shape, F32))

        acc = sb("acc", [P, WT, D])
        scol = sb("scol", [P, ROUTES, WT])
        rcol = sb("rcol", [P, WT])
        slotT = sb("slotT", [P, RC])
        deltaT = sb("deltaT", [P, RC])
        local_attention(nc, x1, a["L0_ffn_gamma_light"], a["L0_ffn_wq_light"], a["L0_ffn_wkv_light"],
                        a["L0_ffn_wo_light"], a["L0_ffn_q_routing_token"], a["L0_ffn_kv_routing_token"], acc, scol, rcol)
        routing(nc, scol, slotT, deltaT)
        routed_attention(nc, x1, a["L0_ffn_gamma_heavy"], a["L0_ffn_wq_heavy"], a["L0_ffn_wkv_heavy"],
                         a["L0_ffn_wo_heavy"], acc, rcol, slotT, deltaT, out)


_INS = ['L0_attn_x', 'L0_attn_ln_g', 'L0_attn_ln_b', 'L0_attn_w_qkv', 'L0_attn_b_qkv', 'L0_attn_w_ent', 'L0_attn_b_ent', 'L0_attn_w_out', 'L0_attn_b_out', 'L0_ffn_gamma_light', 'L0_ffn_wq_light', 'L0_ffn_wkv_light', 'L0_ffn_wo_light', 'L0_ffn_q_routing_token', 'L0_ffn_kv_routing_token', 'L0_ffn_gamma_heavy', 'L0_ffn_wq_heavy', 'L0_ffn_wkv_heavy', 'L0_ffn_wo_heavy']


def kernel(**inputs):
    import numpy as _np
    import concourse.bacc as _bacc
    from concourse import mybir as _mybir
    from concourse.bass_utils import run_bass_kernel_spmd as _run

    nc = _bacc.Bacc("TRN2", target_bir_lowering=False, num_devices=1)
    arrays, args = {}, {}
    for name in _INS:
        a = _np.asarray(inputs[name])
        if name in ("L0_attn_w_qkv", "L0_attn_w_out", "L0_ffn_wkv_heavy"):
            a = a.T
        a = _np.ascontiguousarray(a)
        arrays[f"in_{name}_dram"] = a
        args[name] = nc.dram_tensor(f"in_{name}_dram", a.shape, _mybir.dt.from_np(a.dtype), kind="ExternalInput").ap()
    out = nc.dram_tensor("out_0_dram", (B, S, H), _mybir.dt.float32, kind="ExternalOutput").ap()
    build(nc, args, out)
    r = _run(nc, [arrays], core_ids=[0])
    return r.results[0]["out_0_dram"]
```

```python
from contextlib import ExitStack

import numpy as np

import concourse.bass as bass
from concourse import mybir

P = 128
F32 = mybir.dt.float32
BF16 = mybir.dt.bfloat16
FP16 = mybir.dt.float16
I32 = mybir.dt.int32
ALU = mybir.AluOpType
ACT = mybir.ActivationFunctionType
AX = mybir.AxisListType

B, S, H = 8, 1024, 256
NT = S // P
KT = H // P
NH, HD = 16, 16
HG = 8
ROUTES = 2
UNITS = B * NH // HG
PARTS = 3
QK_ROWS = 6 * HD
VC = PARTS * HD + 1
NCH = 12
RING = NT
LAG = 8
NEG = -1e30
LN_EPS, OUT_EPS = 1e-6, 1e-5
SCALE = 1.0 / (HD ** 0.5) / 0.1
SHIFT = 9.0
Q_SLOT = (0, 0, 1, 0, 2, 1)
K_SLOT = (0, 1, 0, 2, 0, 1)
CAST_ACT = {2: 2, 3: 2, 4: 2, 5: 2, 6: 1, 7: 1}
SUB_DVE = (7,)


def s_chunks(t):
    n = P * (t + 1)
    return [(a, min(512, n - a)) for a in range(0, n, 512)]


def t_chunks(j):
    return [(a, min(512, S - a)) for a in range(P * j, S, 512)]


S_AT = [sum(len(s_chunks(x)) for x in range(t)) for t in range(NT + 1)]
P_AT = [S * j - P * j * (j - 1) // 2 for j in range(NT + 1)]
T_AT = [sum(len(t_chunks(x)) for x in range(j)) for j in range(NT + 1)]


def need(eng, sem, value):
    if isinstance(value, int) and value <= 0:
        return
    eng.wait_ge(sem, value)


def among(js, n):
    return len(js) * ((n + 1) // NT) + sum(1 for j in range((n + 1) % NT) if j in js)


def causal_attention(nc, x, ln_g, ln_b, w_qkvT, b_qkv, w_ent, b_ent, w_outT, b_out, toks_in, stat_dram, part_dram, x1_dram, scol):
    with ExitStack() as ctx:
        def sb(name, shape, dt=F32):
            return ctx.enter_context(nc.sbuf_tensor(name, shape, dt))

        def pb(name, shape, dt=F32):
            return ctx.enter_context(nc.psum_tensor(name, shape, dt))

        def sem(name):
            return ctx.enter_context(nc.semaphore(name))

        ident = sb("ident", [P, P])
        ident_b = sb("ident_b", [P, P], BF16)
        mask_qk = sb("mask_qk", [P, P], BF16)
        mask_kq = sb("mask_kq", [P, P], BF16)
        ones_row = sb("ones_row", [1, P], BF16)
        wqk = sb("wqk", [P, KT, 2 * H])
        wv = sb("wv", [P, KT, 2, P + 1])
        bv = sb("bv", [1, 2, P + 1])
        bvr = sb("bvr", [1, 2, P + 1])
        bvp = sb("bvp", [1, PARTS, 2, P + 1], BF16)
        wo = sb("wo", [P, KT, H])
        bo = sb("bo", [P, H])
        bqk = sb("bqk", [P, 4])
        carry = sb("carry", [P, 1])
        gcol = sb("gcol", [P, KT])
        bcol = sb("bcol", [P, KT])
        mhalf = sb("mhalf", [P, NT])
        eps_in = sb("eps_in", [P, NT])
        eps_out = sb("eps_out", [P, NT])
        toks = sb("toks", [P, ROUTES, H])
        junk = sb("junk", [P, 2 * ROUTES, H], BF16)
        sr = sb("sr", [P, ROUTES, NT])
        xin = sb("xin", [P, NT, H])
        xres = sb("xres", [P, NT, H])
        xn = sb("xn", [P, NT, H])
        xnT = sb("xnT", [P, KT, S])
        AO = sb("AO", [P, NT, H])
        AOT = sb("AOT", [P, KT, S])
        stats = sb("stats", [P, NT, 6])
        mv = sb("mv", [P, NT, 2])
        rstd = sb("rstd", [P, NT])
        stats2 = sb("stats2", [P, NT, 6])
        mv2 = sb("mv2", [P, NT, 2])
        rstd2 = sb("rstd2", [P, NT])
        qp = sb("qp", [P, PARTS, S], BF16)
        kp = sb("kp", [P, PARTS, S], BF16)
        rest = sb("rest", [P, 2, 512])
        qs = [sb(f"qs{g}", [QK_ROWS + PARTS, HG, S], BF16) for g in range(2)]
        ks = [sb(f"ks{g}", [QK_ROWS + PARTS, HG, S], BF16) for g in range(2)]
        vx = [sb(f"vx{g}", [P, NT, HG, VC], BF16) for g in range(2)]
        vf = sb("vf", [P, 2, P])
        vr = sb("vr", [P, 2, P])
        gate = sb("gate", [P, 4, 2])
        m2 = sb("m2", [P, HG, NT, 2])
        mn = sb("mn", [P, 4 * NT])
        mr = sb("mr", [P, 4 * NT])
        mp = sb("mp", [P, PARTS, 4 * NT], BF16)
        mt = sb("mt", [PARTS * 4 * NT, P], BF16)
        osum = sb("osum", [P, NT, HD])
        orec = sb("orec", [P, NT])
        pf = sb("pf", [P, P_AT[NT]])
        ph = sb("ph", [P, P_AT[NT]], FP16)
        pl = sb("pl", [P, P_AT[NT]], FP16)

        psS = pb("psS", [P, 3, 512])
        psT = pb("psT", [P, 3, 512])
        psO = pb("psO", [P, 512])
        psM = pb("psM", [P, 512])
        O = psO[:, 0:NT * VC].rearrange("p (t c) -> p t c", c=VC)
        mT = psM[0:PARTS * 4 * NT, 0:P // 2].bitcast(BF16)

        w_first = sem("w_first")
        w_in = sem("w_in")
        consts = sem("consts")
        consts_v = sem("consts_v")
        bias_ok = sem("bias_ok")
        k_ones = sem("k_ones")
        x_in = sem("x_in")
        xr_in = sem("xr_in")
        st_done = sem("st_done")
        mv_done = sem("mv_done")
        rstd_ready = sem("rstd_ready")
        rs_chain = sem("rs_chain")
        xn_ready = sem("xn_ready")
        xt_ready = sem("xt_ready")
        xt_out = sem("xt_out")
        v_ps = sem("v_ps")
        gate_exp = sem("gate_exp")
        v_gate = sem("v_gate")
        v_gated = sem("v_gated")
        v_hi = sem("v_hi")
        v_rest = sem("v_rest")
        v_mid = sem("v_mid")
        v_lo = sem("v_lo")
        pj_ps = sem("pj_ps")
        pj_hi = sem("pj_hi")
        pj_rest = sem("pj_rest")
        pj_mid = sem("pj_mid")
        pj_lo = sem("pj_lo")
        pt_out = sem("pt_out")
        stk = [[sem(f"stk{g}_{i}") for i in range(2)] for g in range(2)]
        sc = sem("sc")
        mx = sem("mx")
        m_chain = sem("m_chain")
        m_ps = sem("m_ps")
        m_out = sem("m_out")
        m_dram = sem("m_dram")
        m_in = sem("m_in")
        stc = sem("stc")
        ex = sem("ex")
        hi_a = sem("hi_a")
        hi_v = sem("hi_v")
        lo_p = sem("lo_p")
        lo_v = sem("lo_v")
        av = sem("av")
        o_read = sem("o_read")
        o_out = sem("o_out")
        at_ps = sem("at_ps")
        at_out = sem("at_out")
        y_ps = sem("y_ps")
        y_bias = sem("y_bias")
        y_sum = sem("y_sum")
        y_st = sem("y_st")
        y_ag = sem("y_ag")
        rs2_chain = sem("rs2_chain")
        rstd2_ready = sem("rstd2_ready")
        y_done = sem("y_done")
        x1_out = sem("x1_out")
        s_dot = sem("s_dot")
        s_out = sem("s_out")

        FIRST = 3 * KT + 4
        WEIGHTS = 2 * (2 * KT + 2) + KT + 1 + ROUTES

        AT_SLOT = (9, 10, 12, 13)
        V_SLOT = (14, 17, 20, 23)
        XT_SLOT = (25, 27, 29, 31)
        PJ_SLOT = {0: (33, 36, 40, 43), 1: (25, 28, 31, 34)}
        M0_SLOT, M1_SLOT = 38, 5
        Y_SLOT = (45, 48, 50, 53)
        STAT_SLOT, NORM_SLOT = 8, 19
        LAST = NT * HG

        def flags(b, hg, mid):
            u = 0 if mid else 2 * b + hg

            def ok(v, n):
                return mid or 0 <= v < n
            return dict(
                main=ok(u, UNITS), tail=ok(u - 1, UNITS), ahead=ok(u + 1, UNITS), proj=ok(u + 2, UNITS),
                pre=hg == 0 and ok(b + 1 if not mid else 0, B), epi=hg == 0 and ok(b - 1 if not mid else 0, B))

        def evac_of(kind, b, hg, k):
            u = 2 * b + hg
            if kind == "at":
                return at_out, 4 * (b - 1) + k + 1
            if kind == "v":
                return v_gated, 4 * (u + 1) + k + 1
            if kind == "xt":
                return xt_out, 4 * (b + 1) + k + 1
            if kind == "pj":
                return pj_rest, 4 * (u + 2) + k + 1
            if kind == "m0":
                return m_out, 2 * (u + 1) + 1
            if kind == "m1":
                return m_out, 2 * u + 2
            return y_bias, 4 * (b - 1) + k + 1

        def tasks(b, hg, mid):
            f = flags(b, hg, mid)
            out = {}
            if f["main"]:
                out[M1_SLOT] = ("m1", 0)
            if f["epi"]:
                out.update({s: ("at", k) for k, s in enumerate(AT_SLOT)})
                out.update({s: ("y", k) for k, s in enumerate(Y_SLOT)})
            if f["ahead"]:
                out.update({s: ("v", k) for k, s in enumerate(V_SLOT)})
                out[M0_SLOT] = ("m0", 0)
            if f["pre"]:
                out.update({s: ("xt", k) for k, s in enumerate(XT_SLOT)})
            if f["proj"]:
                out.update({s: ("pj", k) for k, s in enumerate(PJ_SLOT[hg])})
            return out

        STEPS = [(-1, 0), (-1, 1), (0, 0), (0, 1), None, (B - 1, 0), (B - 1, 1), (B, 0)]

        def before(b, hg, mid, slot):
            own = [s for s in sorted(tasks(b, hg, mid)) if s < slot]
            if own:
                kind, k = tasks(b, hg, mid)[own[-1]]
                return evac_of(kind, b, hg, k)
            pb_, pg = (b, 0) if hg else (b - 1, 1)
            if not mid and pb_ < -1:
                return None
            pmid = mid
            t = tasks(pb_ if not pmid else 0, pg, pmid)
            if not t:
                return None
            kind, k = t[max(t)]
            return evac_of(kind, pb_, pg, k)

        def every_step(eng, step):
            for b, hg in ((-1, 0), (-1, 1), (0, 0), (0, 1), (1, 0), (1, 1)):
                step(b, hg, False)
            with eng.Fori(2, B - 1) as b:
                step(b, 0, True)
                step(b, 1, True)
            for b, hg in ((B - 1, 0), (B - 1, 1), (B, 0)):
                step(b, hg, False)

        def hi_wait(eng, u, n):
            js = CAST_ACT if n % NT in CAST_ACT else [j for j in range(NT) if j not in CAST_ACT]
            need(eng, hi_a if n % NT in CAST_ACT else hi_v, u * (HG * len(js)) + among(js, n))

        def lo_wait(eng, u, n):
            js = SUB_DVE if n % NT in SUB_DVE else [j for j in range(NT) if j not in SUB_DVE]
            need(eng, lo_v if n % NT in SUB_DVE else lo_p, u * (HG * len(js)) + among(js, n))

        def back(u, n, k):
            return (u, n - k) if n >= k else (u - 1, n - k + LAST)

        block = ctx.enter_context(nc.Block())

        @block.sync
        def _(sp):
            sp.dma_start(xin[:], x[0].rearrange("(t p) n -> p t n", p=P)).then_inc(x_in, 16)
            for kt in range(KT):
                rows = slice(P * kt, P * kt + P)
                sp.dma_start(gcol[:, kt:kt + 1], ln_g[rows].rearrange("(p a) -> p a", a=1)).then_inc(w_first, 16)
                sp.dma_start(bcol[:, kt:kt + 1], ln_b[rows].rearrange("(p a) -> p a", a=1)).then_inc(w_first, 16)
                sp.dma_start(wqk[:, kt, :], w_qkvT[rows, 0:2 * H]).then_inc(w_first, 16)
            for c in range(4):
                sp.dma_start(bqk[:, c:c + 1], b_qkv[P * c:P * c + P].rearrange("(p a) -> p a", a=1)).then_inc(w_first, 16)
            for g in range(2):
                for kt in range(KT):
                    rows = slice(P * kt, P * kt + P)
                    sp.dma_start(wv[:, kt, g, 0:P], w_qkvT[rows, 2 * H + P * g:2 * H + P * g + P]).then_inc(w_in, 16)
                    sp.dma_start(wv[:, kt, g, P:P + 1], w_ent[:, rows].rearrange("a p -> p a")).then_inc(w_in, 16)
                sp.dma_start(bv[:, g, 0:P], b_qkv[2 * H + P * g:2 * H + P * g + P].rearrange("(a p) -> a p", a=1)).then_inc(w_in, 16)
                sp.dma_start(bv[:, g, P:P + 1], b_ent.rearrange("(a p) -> a p", a=1)).then_inc(w_in, 16)
            for kt in range(KT):
                sp.dma_start(wo[:, kt, :], w_outT[P * kt:P * kt + P, :]).then_inc(w_in, 16)
            sp.dma_start(bo[:], b_out.rearrange("(a n) -> a n", a=1).to_broadcast([P, H])).then_inc(w_in, 16)
            for route, tok in enumerate(toks_in):
                sp.dma_start(toks[:, route, :], tok.rearrange("(a n) -> a n", a=1).to_broadcast([P, H])).then_inc(w_in, 16)

            def step(b, hg, mid):
                f = flags(b, hg, mid)
                u = 2 * b + hg

                def parts_out():
                    need(sp, pj_lo, 4 * (u + 2) + 4)
                    need(sp, pj_mid, 4 * (u + 2) + 4)
                    for half in range(2):
                        need(sp, stk[1 - hg][half], 192 * ((b + 1) if hg == 0 else (b + 2)))
                    sp.dma_start(part_dram[0].rearrange("c p t -> p c t"), qp[:]).then_inc(pt_out, 16)
                    sp.dma_start(part_dram[1].rearrange("c p t -> p c t"), kp[:]).then_inc(pt_out, 16)

                def stacks(half):
                    if half == 0:
                        need(sp, pt_out, 32 * (u + 3))
                        if mid or u >= 0:
                            need(sp, sc, 8 * NCH * (u + 1))
                    if mid or u >= 0:
                        need(sp, stc, 8 * NCH * u + 4 * NCH * (half + 1))
                    hs = slice(4 * half, 4 * half + 4)
                    feats = slice(4 * HD * half, 4 * HD * half + 4 * HD)
                    for s in range(6):
                        rows = slice(HD * s, HD * s + HD)
                        sp.dma_start(qs[hg][rows, hs, :], part_dram[0, Q_SLOT[s], feats, :].rearrange("(h d) t -> d h t", d=HD))\
                          .then_inc(stk[hg][half], 16)
                        sp.dma_start(ks[hg][rows, hs, :], part_dram[1, K_SLOT[s], feats, :].rearrange("(h d) t -> d h t", d=HD))\
                          .then_inc(stk[hg][half], 16)

                def maxima(uu, half):
                    need(sp, m_out, 2 * uu + half + 1)
                    need(sp, m_in, 16 * (2 * uu + half))
                    sp.dma_start(stat_dram[half], mt[:]).then_inc(m_dram, 16)
                    need(sp, m_dram, 16 * (2 * uu + half + 1))
                    g = hg if half else 1 - hg
                    sp.dma_start(qs[g][QK_ROWS:QK_ROWS + PARTS, 4 * half:4 * half + 4, :],
                                 stat_dram[half].rearrange("(c h t) k -> c h (t k)", c=PARTS, h=4)).then_inc(m_in, 16)

                if f["pre"] and (mid or b >= 0):
                    need(sp, xn_ready, NT * (b + 1))
                    sp.dma_start(xin[:], x[b + 1].rearrange("(t p) n -> p t n", p=P)).then_inc(x_in, 16)
                if f["main"]:
                    maxima(u, 1)
                if hg == 1 and (mid or b >= 0):
                    need(sp, y_sum, 4 * b)
                    sp.dma_start(xres[:], x[b].rearrange("(t p) n -> p t n", p=P)).then_inc(xr_in, 16)
                for n in range(LAST):
                    if n == M0_SLOT + 2 and f["ahead"]:
                        maxima(u + 1, 0)
                    if f["proj"] and n == PJ_SLOT[hg][-1] + 3:
                        parts_out()
                    if f["proj"] and n == 47:
                        stacks(0)
                    if f["epi"] and n - 9 in Y_SLOT:
                        k = Y_SLOT.index(n - 9)
                        need(sp, y_done, 2 * (4 * (b - 1) + k + 1))
                        sp.dma_start(x1_dram[b - 1][2 * P * k:2 * P * k + 2 * P, :].rearrange("(t p) n -> p t n", p=P),
                                     xn[:, 2 * k:2 * k + 2, :]).then_inc(x1_out, 16)
                if f["proj"]:
                    stacks(1)

            every_step(sp, step)
            sp.wait_ge(x1_out, 16 * 4 * B)

        @block.gpsimd
        def _(pool):
            pool.memset(ident[:], 0.0).then_inc(consts, 1)
            pool.memset(ident_b[:], 0.0).then_inc(consts, 1)
            pool.memset(mask_qk[:], 0.0).then_inc(consts, 1)
            pool.memset(mask_kq[:], 0.0).then_inc(consts, 1)
            pool.memset(mhalf[:], -0.5).then_inc(consts, 1)
            pool.memset(eps_in[:], LN_EPS).then_inc(consts, 1)
            pool.memset(eps_out[:], OUT_EPS).then_inc(consts, 1)
            pool.wait_ge(consts, 7)
            for m in (ident, ident_b):
                pool.affine_select(out=m[:], in_=m[:], compare_op=ALU.not_equal, fill=1.0, base=0,
                                   pattern=[[-1, P]], channel_multiplier=1).then_inc(consts, 1)
            pool.affine_select(out=mask_qk[:], in_=mask_qk[:], compare_op=ALU.is_ge, fill=NEG, base=0,
                               pattern=[[-1, P]], channel_multiplier=1).then_inc(consts, 1)
            pool.affine_select(out=mask_kq[:], in_=mask_kq[:], compare_op=ALU.is_ge, fill=NEG, base=0,
                               pattern=[[1, P]], channel_multiplier=-1).then_inc(consts, 1)

            def step(b, hg, mid):
                f = flags(b, hg, mid)
                u = 2 * b + hg
                for n in range(LAST):
                    if f["pre"] and n == NORM_SLOT - 5:
                        need(pool, mv_done, NT * (b + 2))
                        need(pool, xn_ready, NT * (b + 1))
                        pool.tensor_tensor(rstd[:], mv[:, :, 1], eps_in[:], ALU.add).then_inc(rs_chain, 1)
                        need(pool, rs_chain, b + 2)
                        pool.tensor_tensor(rstd[:], rstd[:], mhalf[:], ALU.pow).then_inc(rstd_ready, 1)
                        if not mid and b == -1:
                            need(pool, rstd_ready, 1)
                            for g in range(2):
                                need(pool, k_ones, g)
                                pool.memset(ks[g][QK_ROWS:QK_ROWS + PARTS, :, :], 1.0).then_inc(k_ones, 1)
                    if f["epi"] and n - 5 in Y_SLOT:
                        k = Y_SLOT.index(n - 5)
                        i = 4 * (b - 1) + k
                        t = slice(2 * k, 2 * k + 2)
                        need(pool, y_ag, 2 * i + 2)
                        pool.tensor_tensor(rstd2[:, t], mv2[:, t, 1], eps_out[:, t], ALU.add).then_inc(rs2_chain, 1)
                        need(pool, rs2_chain, i + 1)
                        pool.tensor_tensor(rstd2[:, t], rstd2[:, t], mhalf[:, t], ALU.pow).then_inc(rstd2_ready, 1)
                    if f["main"] and n % NT not in SUB_DVE:
                        cols = slice(P_AT[n % NT], P_AT[n % NT + 1])
                        need(pool, ex, 8 * NCH * u + NCH * (n // NT) + T_AT[n % NT + 1])
                        hi_wait(pool, u, n)
                        need(pool, av, LAST * u + n + 1 - RING)
                        pool.tensor_tensor(pl[:, cols], pf[:, cols], ph[:, cols], ALU.subtract).then_inc(lo_p, 1)

            every_step(pool, step)

        @block.scalar
        def _(act):
            act.wait_ge(w_first, 16 * FIRST)

            def step(b, hg, mid):
                f = flags(b, hg, mid)
                u = 2 * b + hg
                for n in range(LAST):
                    i, j = divmod(n, NT)
                    if f["ahead"] and n - 1 in V_SLOT:
                        k = V_SLOT.index(n - 1)
                        need(act, v_ps, 4 * (u + 1) + k + 1)
                        need(act, v_gate, 3 * (4 * (u + 1) + k))
                        act.activation(gate[:, 0, :], psM[:, 0:2 * (P + 1)].rearrange("p (t c) -> p t c", t=2)[:, :, P],
                                       ACT.Exp, scale=-1.0).then_inc(gate_exp, 1)
                    if f["ahead"] and n - 2 in V_SLOT:
                        k = V_SLOT.index(n - 2)
                        need(act, v_gated, 4 * (u + 1) + k + 1)
                        need(act, av, LAST * u)
                        act.activation(vx[1 - hg][:, 2 * k:2 * k + 2, :, 0:HD],
                                       vf[:].rearrange("p t (h d) -> p t h d", d=HD), ACT.Copy).then_inc(v_hi, 1)
                    if f["ahead"] and n - 3 in V_SLOT:
                        k = V_SLOT.index(n - 3)
                        need(act, v_rest, 4 * (u + 1) + k + 1)
                        act.activation(vx[1 - hg][:, 2 * k:2 * k + 2, :, HD:2 * HD],
                                       vr[:].rearrange("p t (h d) -> p t h d", d=HD), ACT.Copy).then_inc(v_mid, 1)
                    if f["pre"] and n - 1 in XT_SLOT:
                        k = XT_SLOT.index(n - 1)
                        kt, half = divmod(k, 2)
                        need(act, xt_ready, 4 * (b + 1) + k + 1)
                        act.activation(xnT[:, kt, 512 * half:512 * half + 512], psM[:], ACT.Identity,
                                       bias=bcol[:, kt:kt + 1], scale=gcol[:, kt:kt + 1]).then_inc(xt_out, 1)
                    if f["proj"] and n - 1 in PJ_SLOT[hg]:
                        k = PJ_SLOT[hg].index(n - 1)
                        half, isk = divmod(k, 2)
                        need(act, pj_ps, 4 * (u + 2) + k + 1)
                        if k == 0:
                            need(act, pt_out, 32 * (u + 2))
                        act.activation((kp if isk else qp)[:, 0, 512 * half:512 * half + 512], psM[:], ACT.Identity,
                                       bias=bqk[:, 2 * isk + hg:2 * isk + hg + 1]).then_inc(pj_hi, 1)
                    if f["proj"] and n - 2 in PJ_SLOT[hg]:
                        k = PJ_SLOT[hg].index(n - 2)
                        half, isk = divmod(k, 2)
                        need(act, pj_rest, 4 * (u + 2) + k + 1)
                        act.activation((kp if isk else qp)[:, 1, 512 * half:512 * half + 512], rest[:, k % 2, :],
                                       ACT.Copy).then_inc(pj_mid, 1)
                    if f["epi"] and n - 1 in AT_SLOT:
                        k = AT_SLOT.index(n - 1)
                        kt, half = divmod(k, 2)
                        need(act, at_ps, 4 * (b - 1) + k + 1)
                        act.activation(AOT[:, kt, 512 * half:512 * half + 512], psM[:], ACT.Copy).then_inc(at_out, 1)
                    if f["main"]:
                        pu, pn = back(u, n, RING)
                        if mid or u > 0 or n >= RING:
                            hi_wait(act, pu, pn)
                            lo_wait(act, pu, pn)
                        for c, (a, w) in enumerate(t_chunks(j)):
                            g = NCH * i + T_AT[j] + c
                            need(act, stc, 8 * NCH * u + g + 1)
                            p0 = P_AT[j] + a - P * j
                            act.activation(pf[:, p0:p0 + w], psT[:, g % 3, 0:w], ACT.Exp,
                                           bias=SHIFT, scale=SCALE).then_inc(ex, 1)
                    for back_ in sorted(set(CAST_ACT.values()), reverse=True):
                        pu, pn = back(u, n, back_)
                        pj = pn % NT
                        if (f["main"] if n >= back_ else f["tail"]) and CAST_ACT.get(pj) == back_:
                            cols = slice(P_AT[pj], P_AT[pj + 1])
                            need(act, ex, 8 * NCH * pu + NCH * (pn // NT) + T_AT[pj + 1])
                            need(act, av, LAST * pu + pn + 1 - RING)
                            act.activation(ph[:, cols], pf[:, cols], ACT.Copy).then_inc(hi_a, 1)

            every_step(act, step)

        @block.vector
        def _(v):
            for g in range(2):
                v.memset(vx[g][:, :, :, VC - 1], 1.0).then_inc(consts_v, 1)
            v.memset(m2[:], -3e38).then_inc(consts_v, 1)
            v.memset(ones_row[:], 1.0).then_inc(consts_v, 1)
            v.wait_ge(consts_v, 4)

            def step(b, hg, mid):
                f = flags(b, hg, mid)
                u = 2 * b + hg

                def maxima(uu, half, stage):
                    e = 5 * (2 * uu + half)
                    need(v, m_chain, e + stage)
                    if stage == 0:
                        need(v, mx, 8 * NCH * uu + 4 * NCH * (half + 1))
                        need(v, m_ps, 2 * uu + half)
                        last = v.tensor_reduce(mn[:], m2[:, 4 * half:4 * half + 4, :, :].rearrange("p h t c -> p (h t) c"),
                                               AX.X, ALU.max, negate=True)
                    elif stage == 1:
                        last = v.tensor_copy(mp[:, 0, :], mn[:])
                    elif stage == 2:
                        last = v.tensor_tensor(mr[:], mn[:], mp[:, 0, :], ALU.subtract)
                    elif stage == 3:
                        last = v.tensor_copy(mp[:, 1, :], mr[:])
                    else:
                        last = v.tensor_tensor(mp[:, 2, :], mr[:], mp[:, 1, :], ALU.subtract)
                    last.then_inc(m_chain, 1)

                def maxima_out(uu, half):
                    need(v, m_ps, 2 * uu + half + 1)
                    need(v, m_dram, 16 * (2 * uu + half))
                    v.tensor_copy(mt[:], mT).then_inc(m_out, 1)

                def head_read(uu, i):
                    need(v, av, LAST * uu + NT * (i + 1))
                    need(v, o_out, HG * uu + i)
                    v.tensor_reduce(osum[:], O[:, :, 0:PARTS * HD].rearrange("p t (c d) -> p t d c", c=PARTS), AX.X,
                                    ALU.add).then_inc(o_read, 1)
                    v.reciprocal(orec[:], O[:, :, VC - 1]).then_inc(o_read, 1)

                def head_out(uu, bb, g, i):
                    need(v, o_read, 2 * (HG * uu + i) + 2)
                    if i == 0 and g == 0:
                        need(v, at_ps, 4 * bb)
                    v.tensor_tensor(AO[:, :, P * g + HD * i:P * g + HD * i + HD], osum[:],
                                    orec[:].unsqueeze(2).to_broadcast([P, NT, HD]), ALU.mult).then_inc(o_out, 1)

                for n in range(LAST):
                    i, j = divmod(n, NT)
                    eu, en = back(u, n, LAG + 1)
                    ended = (f["main"] if n > LAG else f["tail"]) and en % NT == NT - 1
                    if f["ahead"]:
                        for c, (a, w) in enumerate(s_chunks(j)):
                            g = NCH * i + S_AT[j] + c
                            need(v, sc, 8 * NCH * (u + 1) + g + 1)
                            v.tensor_reduce(m2[:, i, j, c:c + 1], psS[:, g % 3, 0:w], AX.X, ALU.max).then_inc(mx, 1)
                    if ended and n > LAG:
                        head_out(u, b, hg, en // NT)
                    elif ended:
                        head_out(u - 1, (b - 1 if hg == 0 else b), 1 - hg, en // NT)
                    pu, pn = back(u, n, 1)
                    pj_ = pn % NT
                    if (f["main"] if n >= 1 else f["tail"]) and pj_ not in CAST_ACT:
                        cols = slice(P_AT[pj_], P_AT[pj_ + 1])
                        need(v, ex, 8 * NCH * pu + NCH * (pn // NT) + T_AT[pj_ + 1])
                        need(v, av, LAST * pu + pn + 1 - RING)
                        v.tensor_copy(ph[:, cols], pf[:, cols]).then_inc(hi_v, 1)
                    pu, pn = back(u, n, 3)
                    pj_ = pn % NT
                    if (f["main"] if n >= 3 else f["tail"]) and pj_ in SUB_DVE:
                        cols = slice(P_AT[pj_], P_AT[pj_ + 1])
                        hi_wait(v, pu, pn)
                        need(v, ex, 8 * NCH * pu + NCH * (pn // NT) + T_AT[pj_ + 1])
                        need(v, av, LAST * pu + pn + 1 - RING)
                        v.tensor_tensor(pl[:, cols], pf[:, cols], ph[:, cols], ALU.subtract).then_inc(lo_v, 1)
                    eu, en = back(u, n, LAG)
                    if (f["main"] if n >= LAG else f["tail"]) and en % NT == NT - 1:
                        head_read(eu, en // NT)
                    if f["main"] and n <= 4:
                        maxima(u, 1, n)
                    if f["main"] and n == M1_SLOT + 1:
                        maxima_out(u, 1)
                    if f["ahead"] and 0 <= n - M0_SLOT + 5 <= 4:
                        maxima(u + 1, 0, n - M0_SLOT + 5)
                    if f["ahead"] and n == M0_SLOT + 1:
                        maxima_out(u + 1, 0)
                    if f["pre"] and 0 <= n - STAT_SLOT < 4:
                        if n == STAT_SLOT:
                            need(v, x_in, 16 * (b + 2))
                            need(v, rstd_ready, b + 1)
                        for t in (2 * (n - STAT_SLOT), 2 * (n - STAT_SLOT) + 1):
                            v.bn_stats(stats[:, t, :], xin[:, t, :]).then_inc(st_done, 1)
                    if f["pre"] and n == STAT_SLOT + 4:
                        need(v, st_done, NT * (b + 2))
                        v.memset(carry[:], 0.0)
                    if f["pre"] and 0 <= n - STAT_SLOT - 4 < 2:
                        for t in range(4 * (n - STAT_SLOT - 4), 4 * (n - STAT_SLOT - 4) + 4):
                            v.bn_aggr(mv[:, t, :], stats[:, t, :]).then_inc(mv_done, 1)
                    if f["pre"] and 0 <= n - NORM_SLOT < 4:
                        if n == NORM_SLOT:
                            need(v, rstd_ready, b + 2)
                            need(v, x1_out, 64 * (b - 1))
                        for t in (2 * (n - NORM_SLOT), 2 * (n - NORM_SLOT) + 1):
                            v.tensor_scalar(xn[:, t, :], xin[:, t, :], mv[:, t, 0:1], rstd[:, t:t + 1], ALU.subtract,
                                            ALU.mult).then_inc(xn_ready, 1)
                    if not mid and (b, hg, n) == (-1, 0, NORM_SLOT + 4):
                        need(v, w_first, 16 * FIRST)
                    if not mid and (b, hg, n) == (-1, 1, 0):
                        need(v, w_in, 16 * WEIGHTS)
                        v.tensor_copy(bvp[:, 0], bv[:]).then_inc(bias_ok, 1)
                        need(v, bias_ok, 1)
                        v.tensor_tensor(bvr[:], bv[:], bvp[:, 0], ALU.subtract).then_inc(bias_ok, 1)
                        need(v, bias_ok, 2)
                        v.tensor_copy(bvp[:, 1], bvr[:]).then_inc(bias_ok, 1)
                        need(v, bias_ok, 3)
                        v.tensor_tensor(bvp[:, 2], bvr[:], bvp[:, 1], ALU.subtract).then_inc(bias_ok, 1)
                    if f["ahead"] and n - 1 in V_SLOT:
                        k = V_SLOT.index(n - 1)
                        e = 4 * (u + 1) + k
                        need(v, gate_exp, e + 1)
                        v.tensor_scalar(gate[:, 1, :], gate[:, 0, :], 1.0, None, ALU.add).then_inc(v_gate, 1)
                        need(v, v_gate, 3 * e + 1)
                        v.reciprocal(gate[:, 2, :], gate[:, 1, :]).then_inc(v_gate, 1)
                        need(v, v_gate, 3 * e + 2)
                        v.tensor_scalar(gate[:, 3, :], gate[:, 2, :], 0.1, 2.0, ALU.max, ALU.min).then_inc(v_gate, 1)
                        need(v, v_gate, 3 * e + 3)
                        need(v, v_rest, e)
                        v.tensor_tensor(vf[:], psM[:, 0:2 * (P + 1)].rearrange("p (t c) -> p t c", t=2)[:, :, 0:P],
                                        gate[:, 3, :].unsqueeze(2).to_broadcast([P, 2, P]), ALU.mult).then_inc(v_gated, 1)
                    if f["ahead"] and n - 3 in V_SLOT:
                        k = V_SLOT.index(n - 3)
                        e = 4 * (u + 1) + k
                        dst = vx[1 - hg][:, 2 * k:2 * k + 2, :, :]
                        need(v, v_mid, e + 1)
                        v.tensor_tensor(dst[:, :, :, 2 * HD:3 * HD], vr[:].rearrange("p t (h d) -> p t h d", d=HD),
                                        dst[:, :, :, HD:2 * HD], ALU.subtract).then_inc(v_lo, 1)
                    if f["ahead"] and n - 2 in V_SLOT:
                        k = V_SLOT.index(n - 2)
                        e = 4 * (u + 1) + k
                        need(v, v_hi, e + 1)
                        need(v, v_lo, e)
                        v.tensor_tensor(vr[:].rearrange("p t (h d) -> p t h d", d=HD),
                                        vf[:].rearrange("p t (h d) -> p t h d", d=HD),
                                        vx[1 - hg][:, 2 * k:2 * k + 2, :, 0:HD], ALU.subtract).then_inc(v_rest, 1)
                    if f["proj"] and n - 2 in PJ_SLOT[hg]:
                        k = PJ_SLOT[hg].index(n - 2)
                        half, isk = divmod(k, 2)
                        e = 4 * (u + 2) + k
                        dst = kp if isk else qp
                        cols = slice(512 * half, 512 * half + 512)
                        need(v, pj_mid, e + 1)
                        need(v, pj_rest, e + 1)
                        v.tensor_tensor(dst[:, 2, cols], rest[:, k % 2, :], dst[:, 1, cols], ALU.subtract).then_inc(pj_lo, 1)
                    if f["proj"] and n - 1 in PJ_SLOT[hg]:
                        k = PJ_SLOT[hg].index(n - 1)
                        half, isk = divmod(k, 2)
                        e = 4 * (u + 2) + k
                        src = (kp if isk else qp)[:, 0, 512 * half:512 * half + 512]
                        need(v, pj_hi, e + 1)
                        need(v, pj_lo, e - 1)
                        need(v, pj_mid, e - 1)
                        v.scalar_tensor_tensor(out=rest[:, k % 2, :], in0=psM[:], scalar=bqk[:, 2 * isk + hg:2 * isk + hg + 1],
                                               in1=src, op0=ALU.add, op1=ALU.subtract).then_inc(pj_rest, 1)
                    for stage in (10, 9, 8, 4, 3, 2, 1):
                        if not f["epi"] or n - stage not in Y_SLOT:
                            continue
                        k = Y_SLOT.index(n - stage)
                        e = 4 * (b - 1) + k
                        t = slice(2 * k, 2 * k + 2)
                        if stage == 1:
                            need(v, y_ps, e + 1)
                            if k == 0:
                                need(v, xt_ready, 4 * (b + 2) if f["pre"] else 4 * B)
                            v.tensor_tensor(xn[:, t, :], psM[:].rearrange("p (t n) -> p t n", t=2),
                                            bo[:].unsqueeze(1).to_broadcast([P, 2, H]), ALU.add).then_inc(y_bias, 1)
                        elif stage == 2:
                            if k == 0:
                                need(v, xr_in, 16 * b)
                            need(v, y_bias, e + 1)
                            v.scalar_tensor_tensor(out=xn[:, t, :], in0=xn[:, t, :], scalar=0.1, in1=xres[:, t, :],
                                                   op0=ALU.mult, op1=ALU.add).then_inc(y_sum, 1)
                        elif stage == 3:
                            need(v, y_sum, e + 1)
                            for tt in (2 * k, 2 * k + 1):
                                v.bn_stats(stats2[:, tt, :], xn[:, tt, :]).then_inc(y_st, 1)
                        elif stage == 4:
                            need(v, y_st, 2 * e + 2)
                            v.memset(carry[:], 0.0)
                            for tt in (2 * k, 2 * k + 1):
                                v.bn_aggr(mv2[:, tt, :], stats2[:, tt, :]).then_inc(y_ag, 1)
                        elif stage == 9:
                            need(v, y_done, 2 * e + 2)
                            need(v, s_dot, 2 * ROUTES * e)
                            for route in range(ROUTES):
                                for c in range(2):
                                    v.tensor_tensor_reduce(junk[:, 2 * route + c, :], xn[:, 2 * k + c, :], toks[:, route, :],
                                                           1.0, 0.0, ALU.mult, ALU.add,
                                                           sr[:, route, 2 * k + c:2 * k + c + 1]).then_inc(s_dot, 1)
                        elif stage == 10:
                            if k == NT // 2 - 1:
                                need(v, s_dot, 2 * ROUTES * (e + 1))
                                at = bass.ds(NT * (b - 1), NT) if mid else slice(NT * (b - 1), NT * b)
                                for route in range(ROUTES):
                                    v.tensor_copy(scol[:, route, at], sr[:, route, :]).then_inc(s_out, 1)
                        else:
                            need(v, rstd2_ready, e + 1)
                            for tt in (2 * k, 2 * k + 1):
                                v.tensor_scalar(xn[:, tt, :], xn[:, tt, :], mv2[:, tt, 0:1], rstd2[:, tt:tt + 1],
                                                ALU.subtract, ALU.mult).then_inc(y_done, 1)

            every_step(v, step)

        @block.tensor
        def _(pe):
            pe.wait_ge(consts, 11)
            pe.wait_ge(consts_v, 4)

            def step(b, hg, mid):
                f = flags(b, hg, mid)
                u = 2 * b + hg
                todo = tasks(b, hg, mid)

                def misc(n, part):
                    kind, k = todo[n]
                    whole = kind not in ("v", "pj", "y")
                    if whole and part == 0:
                        return
                    prev = before(b, hg, mid, n)
                    if prev is not None and (part == 0 or whole):
                        need(pe, *prev)
                    ends = part == 1
                    if kind in ("m0", "m1"):
                        uu, half = (u, 1) if kind == "m1" else (u + 1, 0)
                        need(pe, m_chain, 5 * (2 * uu + half) + 5)
                        last, done = pe.transpose(mT, mp[:].rearrange("p c x -> p (c x)"), ident_b[:]), m_ps
                    elif kind in ("at", "xt"):
                        kt, half = divmod(k, 2)
                        src, done = (AO, at_ps) if kind == "at" else (xn, xt_ready)
                        if kind == "xt":
                            need(pe, xn_ready, NT * (b + 1) + 4 * half + 4)
                        elif k == 0:
                            need(pe, o_out, HG * u)
                        for t in range(4):
                            last = pe.transpose(psM[:, P * t:P * t + P], src[:, 4 * half + t, P * kt:P * kt + P], ident[:])
                    elif kind == "v":
                        need(pe, xt_out, 4 * (b + 1) if hg == 0 else 4 * (b + 2))
                        if not mid and u < 0:
                            need(pe, bias_ok, 4)
                            need(pe, w_in, 16 * WEIGHTS)
                        o = psM[:, (P + 1) * part:(P + 1) * (part + 1)]
                        tok = P * (2 * k + part)
                        for c in range(PARTS):
                            pe.matmul(o, ones_row[:], bvp[:, c, 1 - hg, :], start=c == 0, stop=False)
                        for kt in range(KT):
                            last = pe.matmul(o, xnT[:, kt, tok:tok + P], wv[:, kt, 1 - hg, :], start=False,
                                             stop=kt == KT - 1)
                        done = v_ps
                    elif kind == "pj":
                        half, isk = divmod(k, 2)
                        need(pe, xt_out, 4 * (b + 2))
                        if not mid and b < 0:
                            need(pe, w_first, 16 * FIRST)
                        col = H * isk + P * hg
                        last = pe.matmul(psM[:], wqk[:, part, col:col + P], xnT[:, part, 512 * half:512 * half + 512],
                                         start=part == 0, stop=ends)
                        done = pj_ps
                    else:
                        need(pe, at_out, 4 * b)
                        tok = P * (2 * k + part)
                        for kt in range(KT):
                            last = pe.matmul(psM[:, H * part:H * part + H], AOT[:, kt, tok:tok + P], wo[:, kt, :],
                                             start=kt == 0, stop=kt == KT - 1)
                        done = y_ps
                    if ends:
                        last.then_inc(done, 1)

                def values(pu, here, blocks):
                    for pn in blocks:
                        pi, pj = divmod(pn, NT)
                        hi_wait(pe, pu, pn)
                        lo_wait(pe, pu, pn)
                        if pj == 0:
                            need(pe, o_read, 2 * (HG * pu + pi))
                            if pi == 0:
                                need(pe, v_lo, 4 * (pu + 1))
                        for t in range(pj, NT):
                            q0 = P_AT[pj] + P * (t - pj)
                            for m, part in enumerate((ph, pl)):
                                last = pe.matmul(O[:, t, :], part[:, q0:q0 + P], vx[hg if here else 1 - hg][:, pj, pi, :],
                                                 start=pj == 0 and t == 0 and m == 0, stop=pj == NT - 1 and m == 1,
                                                 skip_group_check=True)
                        last.then_inc(av, 1)

                for n in range(LAST):
                    i, j = divmod(n, NT)
                    if f["ahead"] and j == 0 and i % 4 == 0:
                        need(pe, stk[1 - hg][i // 4], 192 * ((b + 1) if hg == 0 else (b + 2)))
                    if f["main"] and j == 0 and i % 4 == 0:
                        need(pe, m_in, 16 * (2 * u + i // 4 + 1))
                        need(pe, k_ones, 2)
                    for c in range(2):
                        if f["ahead"] and c < len(s_chunks(j)):
                            a, w = s_chunks(j)[c]
                            g1, g = 1 - hg, NCH * i + S_AT[j] + c
                            need(pe, mx, 8 * NCH * (u + 1) + g + 1 - 3)
                            diag = a + w == P * (j + 1)
                            last = pe.matmul(psS[:, g % 3, 0:w], qs[g1][0:QK_ROWS, i, P * j:P * j + P],
                                             ks[g1][0:QK_ROWS, i, a:a + w], start=True, stop=not diag)
                            if diag:
                                last = pe.matmul(psS[:, g % 3, w - P:w], ident_b[:], mask_qk[:], start=False, stop=True)
                            last.then_inc(sc, 1)
                        if f["main"] and c < len(t_chunks(j)):
                            a, w = t_chunks(j)[c]
                            g = NCH * i + T_AT[j] + c
                            need(pe, ex, 8 * NCH * u + g + 1 - 3)
                            last = pe.matmul(psT[:, g % 3, 0:w], ks[hg][:, i, P * j:P * j + P], qs[hg][:, i, a:a + w],
                                             start=True, stop=c > 0)
                            if c == 0:
                                last = pe.matmul(psT[:, g % 3, 0:P], ident_b[:], mask_kq[:], start=False, stop=True)
                            last.then_inc(stc, 1)
                        if c == 0 and (f["main"] if n >= LAG else f["tail"]) and (n - LAG) % NT:
                            pu, pn = back(u, n, LAG)
                            values(pu, n >= LAG, (pn - 1, pn) if pn % NT == 1 else (pn,))
                        if n in todo and c == 0:
                            misc(n, 0)
                    if n in todo:
                        misc(n, 1)

            every_step(pe, step)


D = H
FH, DH = 8, 64
HID = FH * DH
FT = HID // P
WT = B * NT
UW = 4
LSCALE = DH ** -0.5
NQ, NKV = 256, 512
FETCH = 9.0 / 8.0
ITERS = 50
RC = ROUTES * WT


class LocalInputs:
    def __init__(self, ctx, nc):
        def sb(name, shape):
            return ctx.enter_context(nc.sbuf_tensor(name, shape, F32))

        self.w_q = sb("l_wq", [P, KT, HID])
        self.w_kv = sb("l_wkv", [P, KT, 2 * HID])
        self.w_o = sb("l_wo", [P, FT, D])
        self.gcol = sb("l_gamma", [P, KT])
        self.xu = sb("l_xu", [P, 2, UW, D])
        self.w_in = ctx.enter_context(nc.semaphore("l_w_in"))
        self.x_in = [ctx.enter_context(nc.semaphore(f"l_x_in{g}")) for g in range(2)]

    def load_x(self, sp, x1_dram, b, g):
        sp.dma_start(self.xu[:, g, :, :], x1_dram[b][512 * g:512 * g + 512, :].rearrange("(t p) n -> p t n", p=P))\
          .then_inc(self.x_in[g], 16)

    def load_first(self, sp, x1_dram, gamma, wq, wkv, wo):
        self.load_x(sp, x1_dram, 0, 0)
        for kt in range(KT):
            rows = slice(P * kt, P * kt + P)
            sp.dma_start(self.w_q[:, kt, :], wq[rows, :]).then_inc(self.w_in, 16)
            sp.dma_start(self.w_kv[:, kt, :], wkv[rows, :]).then_inc(self.w_in, 16)
            sp.dma_start(self.gcol[:, kt:kt + 1], gamma[rows].rearrange("(p a) -> p a", a=1)).then_inc(self.w_in, 16)
        sp.dma_start(self.w_o[:], wo.rearrange("(f p) n -> p f n", p=P)).then_inc(self.w_in, 16)
        self.load_x(sp, x1_dram, 0, 1)


def local_attention(nc, x1_dram, inputs, acc, rcol, d):
    with ExitStack() as ctx:
        def sb(name, shape, dt=F32):
            return ctx.enter_context(nc.sbuf_tensor(name, shape, dt))

        def pb(name, shape, dt=F32):
            return ctx.enter_context(nc.psum_tensor(name, shape, dt))

        def sem(name):
            return ctx.enter_context(nc.semaphore(name))

        ident = sb("l_ident", [P, P])
        w_q, w_kv, w_o, gcol, xu = inputs.w_q, inputs.w_kv, inputs.w_o, inputs.gcol, inputs.xu
        half_ = sb("l_half", [P, UW])
        xh = sb("l_xh", [P, UW, D])
        junk = sb("l_junk", [P, UW, D], BF16)
        ss = sb("l_ss", [P, 2, UW])
        rn = sb("l_rn", [P, 4, UW])
        xhT = sb("l_xhT", [P, KT, UW * P])
        qT = sb("l_qT", [P, 2, FT, UW * P])
        kT = sb("l_kT", [P, 2, FT, UW * P])
        vv = sb("l_vv", [P, 2, UW, HID])
        nmax = sb("l_nmax", [P, FH])
        sub = sb("l_sub", [P, FH, P])
        pr = sb("l_pr", [P, FH, P])
        rs = sb("l_rs", [P, 2, FH])
        pn = sb("l_pn", [P, FH, P])
        pT = sb("l_pT", [P, FH, P])
        aT = sb("l_aT", [P, FT, P])
        psS = pb("l_psS", [P, FH, P])
        psP = pb("l_psP", [P, FH, P])
        psX = pb("l_psX", [P, 2, 512])
        psA = pb("l_psA", [P, FT, P])
        psYZ = pb("l_psYZ", [P, 512])
        psY = psYZ[:, 0:D]
        psZ = psYZ[:, D:D + 1]

        w_in, x_in = inputs.w_in, inputs.x_in
        made = sem("l_made")
        made_v = sem("l_made_v")
        x_copied = sem("l_x_copied")
        sq = sem("l_sq")
        root = sem("l_root")
        rch = sem("l_rch")
        xh_ok = sem("l_xh_ok")
        aux = sem("l_aux")
        aux_a = sem("l_aux_a")
        aux_v = sem("l_aux_v")
        s_ps = sem("l_s_ps")
        s_mx = sem("l_s_mx")
        s_sub = sem("l_s_sub")
        s_ex = sem("l_s_ex")
        s_sum = sem("l_s_sum")
        s_n = sem("l_s_n")
        t_ps = sem("l_t_ps")
        t_out = sem("l_t_out")
        a_ps = sem("l_a_ps")
        a_out = sem("l_a_out")
        y_ps = sem("l_y_ps")
        y_out = sem("l_y_out")
        d_sb = sem("l_d_sb")
        d_ex = sem("l_d_ex")
        d_sum = sem("l_d_sum")
        d_ln = sem("l_d_ln")
        d_a = sem("l_d_a")

        def every_slot(eng, slot):
            for w in range(1, NT):
                slot(-1, w, False)
            for b in (0, 1):
                for w in range(NT):
                    slot(b, w, False)
            with eng.Fori(2, B - 1) as b:
                for w in range(NT):
                    slot(b, w, True)
            for w in range(NT):
                slot(B - 1, w, False)

        def flags(b, w, mid):
            n = 0 if mid else NT * b + w
            unit = 0 if mid else 2 * b + w // UW + 1
            return dict(win=mid or n >= 0, ahead=mid or (-1 <= n < WT - 1),
                        nxt=mid or 0 <= unit < WT // UW, prep=mid or 0 <= unit + 1 < WT // UW)

        def descent(b, w):
            return NT * b + w - (NT * (B - 1) - ITERS)

        def descends(b, w, mid):
            return mid or 1 <= descent(b, w) < ITERS

        def row(h):
            return (h % 2) * (FH // 2) + h // 2

        def projected(b, w):
            return 2 * b + w // UW + 1, (w // UW + 1) % 2

        def prepared(b, w):
            return 2 * b + w // UW + 2, (w // UW) % 2

        def tiles(u, mid):
            return bass.ds(UW * u, UW) if mid else slice(UW * u, UW * u + UW)

        block = ctx.enter_context(nc.Block())

        @block.sync
        def _(sp):
            def slot(b, w, mid):
                if w % UW == 0 and (mid or 2 <= 2 * b + w // UW + 2 < WT // UW):
                    u1 = 2 * b + w // UW
                    need(sp, xh_ok, UW * (u1 + 1))
                    need(sp, x_copied, u1 + 1)
                    inputs.load_x(sp, x1_dram, b + 1, w // UW)

            every_slot(sp, slot)

        @block.gpsimd
        def _(pool):
            pool.memset(ident[:], 0.0).then_inc(made, 1)
            pool.memset(half_[:], 0.5).then_inc(made, 1)
            pool.wait_ge(made, 2)
            pool.affine_select(out=ident[:], in_=ident[:], compare_op=ALU.not_equal, fill=1.0, base=0,
                               pattern=[[-1, P]], channel_multiplier=1).then_inc(made, 1)

            def slot(b, w, mid):
                f = flags(b, w, mid)
                u, g = projected(b, w)
                pu, pg = prepared(b, w)
                n = NT * b + w
                if w % UW == 1 and f["prep"]:
                    need(pool, sq, UW * (pu + 1))
                    pool.tensor_tensor(rn[:, 0, :], ss[:, 0, :], half_[:], ALU.pow).then_inc(root, 1)
                if w % UW == 2 and f["prep"]:
                    need(pool, x_in[pg], 16 * (b + 2))
                    pool.tensor_copy(acc[:, tiles(pu, mid), :], xu[:, pg, :, :]).then_inc(x_copied, 1)
                if f["ahead"]:
                    need(pool, s_sum, 2 * (n + 2))
                    need(pool, t_ps, n + 1)
                    pool.tensor_tensor(pn[:], pr[:], rs[:, 1, :].unsqueeze(2).to_broadcast([P, FH, P]),
                                       ALU.mult).then_inc(s_n, 1)

            every_slot(pool, slot)

        @block.scalar
        def _(act):
            def slot(b, w, mid):
                f = flags(b, w, mid)
                u, g = projected(b, w)
                pu, pg = prepared(b, w)
                n = NT * b + w
                if w % UW == 1 and f["prep"]:
                    need(act, x_in[pg], 16 * (b + 2))
                    need(act, root, pu)
                    for t in range(UW):
                        act.activation(junk[:, t, :], xu[:, pg, t, :], ACT.Square, accum_out=ss[:, 0, t:t + 1]).then_inc(sq, 1)
                if f["win"]:
                    for c in range(2):
                        need(act, t_ps, n + 1)
                        need(act, a_ps, n)
                        act.activation(pT[:, 4 * c:4 * c + 4, :], psP[:, 4 * c:4 * c + 4, :], ACT.Copy).then_inc(t_out, 1)
                if descends(b, w, mid):
                    i = descent(b, w)
                    need(act, d_sb, 2 * i)
                    act.activation(d.e[:], d.under[:, 0:P], ACT.Exp, bias=d.under[:, P:P + 1], scale=-1.0,
                                   accum_out=d.z[:]).then_inc(d_ex, 1)
                if f["ahead"]:
                    need(act, s_sub, n + 2)
                    need(act, s_n, n + 1)
                    act.activation(pr[:], sub[:], ACT.Exp, scale=LSCALE).then_inc(s_ex, 1)
                if f["nxt"]:
                    p = w % UW
                    for k in (0, 2):
                        need(act, aux, 4 * (UW * u + p) + k + 1)
                        src = psX[:, 0, :]
                        if p == 0:
                            act.activation(xhT[:, k // 2, 0:256], src[:, 0:256], ACT.Copy).then_inc(aux_a, 1)
                        elif p == 3:
                            act.activation(vv[:, g, k, :], src, ACT.Copy).then_inc(aux_a, 1)
                        else:
                            act.activation((qT if p == 1 else kT)[:, g, k, :], src, ACT.Copy).then_inc(aux_a, 1)
                        if k == 0 and descends(b, w, mid):
                            need(act, d_sum, descent(b, w))
                            act.activation(d.lz[:], psZ, ACT.Ln).then_inc(d_ln, 1)

            every_slot(act, slot)

        @block.vector
        def _(v):
            v.wait_ge(w_in, 16 * 7)
            for kt in range(KT):
                v.tensor_scalar(w_q[:, kt, :], w_q[:, kt, :], gcol[:, kt:kt + 1], None, ALU.mult).then_inc(made_v, 1)
                v.tensor_scalar(w_kv[:, kt, :], w_kv[:, kt, :], gcol[:, kt:kt + 1], None, ALU.mult).then_inc(made_v, 1)

            def slot(b, w, mid):
                f = flags(b, w, mid)
                u, g = projected(b, w)
                pu, pg = prepared(b, w)
                n = NT * b + w
                if descends(b, w, mid):
                    i = descent(b, w)
                    need(v, d_a, i - 1)
                    v.tensor_scalar(d.over[:], d.sx[:], d.na[:, 0:1], 0.0, ALU.subtract, ALU.max).then_inc(d_sb, 1)
                    need(v, d_sb, 2 * i - 1)
                    need(v, d_ex, i - 1)
                    v.tensor_tensor(d.under[:], d.over[:], d.sx[:], ALU.subtract).then_inc(d_sb, 1)
                if f["ahead"]:
                    need(v, s_ps, n + 2)
                    v.tensor_reduce(nmax[:], psS[:], AX.X, ALU.max).then_inc(s_mx, 1)
                    need(v, s_mx, n + 2)
                    need(v, s_ex, n + 1)
                    v.tensor_tensor(sub[:], psS[:], nmax[:].unsqueeze(2).to_broadcast([P, FH, P]), ALU.subtract)\
                     .then_inc(s_sub, 1)
                    need(v, s_ex, n + 2)
                    need(v, s_n, n + 1)
                    v.tensor_reduce(rs[:, 0, :], pr[:], AX.X, ALU.add).then_inc(s_sum, 1)
                    need(v, s_sum, 2 * (n + 1) + 1)
                    v.reciprocal(rs[:, 1, :], rs[:, 0, :]).then_inc(s_sum, 1)
                p = w % UW
                if f["nxt"]:
                    for k in (1, 3):
                        need(v, aux, 4 * (UW * u + p) + k + 1)
                        src = psX[:, 1, :]
                        if p == 0:
                            v.tensor_copy(xhT[:, k // 2, 256:512], src[:, 0:256]).then_inc(aux_v, 1)
                        elif p == 3:
                            v.tensor_copy(vv[:, g, k, :], src).then_inc(aux_v, 1)
                        else:
                            v.tensor_copy((qT if p == 1 else kT)[:, g, k, :], src).then_inc(aux_v, 1)
                        if k == 1 and f["win"]:
                            need(v, a_ps, n + 1)
                            need(v, y_ps, n)
                            v.tensor_copy(aT[:], psA[:]).then_inc(a_out, 1)
                elif f["win"]:
                    need(v, a_ps, n + 1)
                    need(v, y_ps, n)
                    v.tensor_copy(aT[:], psA[:]).then_inc(a_out, 1)
                if f["win"]:
                    need(v, y_ps, n + 1)
                    a1 = acc[:, bass.ds(n, 1) if mid else slice(n, n + 1), :]
                    if w % UW == 0:
                        need(v, x_copied, 2 * b + w // UW + 1)
                    v.tensor_tensor(a1, psY.unsqueeze(1), a1, ALU.add).then_inc(y_out, 1)
                if p == 2 and f["prep"]:
                    need(v, x_in[pg], 16 * (b + 2))
                    need(v, root, pu + 1)
                    v.tensor_scalar(rn[:, 1, :], rn[:, 0, :], 1e-12, None, ALU.max).then_inc(rch, 1)
                    need(v, rch, 4 * pu + 1)
                    v.reciprocal(rn[:, 2, :], rn[:, 1, :]).then_inc(rch, 1)
                    need(v, rch, 4 * pu + 2)
                    v.tensor_scalar(rn[:, 3, :], rn[:, 2, :], float(D ** 0.5), None, ALU.mult).then_inc(rch, 1)
                    need(v, rch, 4 * pu + 3)
                    v.tensor_copy(rcol[:, tiles(pu, mid)], rn[:, 3, :]).then_inc(rch, 1)
                    need(v, aux, 4 * (UW * (pu - 1) + 1))
                    for t in range(UW):
                        v.tensor_scalar(xh[:, t, :], xu[:, pg, t, :], rn[:, 3, t:t + 1], None, ALU.mult).then_inc(xh_ok, 1)
                if descends(b, w, mid):
                    i = descent(b, w)
                    need(v, d_ln, i)
                    v.tensor_scalar(d.na[:], d.lz[:], d.under[:, P:P + 1], d.logk[:, 0:1], ALU.subtract, ALU.subtract)\
                     .then_inc(d_a, 1)

            every_slot(v, slot)

        @block.tensor
        def _(pe):
            pe.wait_ge(made, 3)
            pe.wait_ge(made_v, 2 * KT)

            def slot(b, w, mid):
                f = flags(b, w, mid)
                u, g = projected(b, w)
                pu, pg = prepared(b, w)
                n = NT * b + w
                p = w % UW

                def piece(k):
                    e = 4 * (UW * u + p) + k
                    need(pe, aux_v if k % 2 else aux_a, 2 * (UW * u + p) + k // 2)
                    out = psX[:, k % 2, :]
                    if p == 0:
                        need(pe, xh_ok, UW * (u + 1))
                        for t in range(2):
                            tt = 2 * (k % 2) + t
                            last = pe.transpose(out[:, P * t:P * t + P], xh[:, tt, P * (k // 2):P * (k // 2) + P], ident[:])
                    else:
                        if p == 1 and k == 0:
                            need(pe, aux_v, 2 * (UW * u + 1))
                            need(pe, aux_a, 2 * (UW * u + 1))
                        for kt in range(KT):
                            if p == 3:
                                lhs, rhs = xhT[:, kt, P * k:P * k + P], w_kv[:, kt, HID:2 * HID]
                            else:
                                lhs, rhs = (w_q, w_kv)[p - 1][:, kt, P * k:P * k + P], xhT[:, kt, :]
                            last = pe.matmul(out, lhs, rhs, start=kt == 0, stop=kt == KT - 1)
                    last.then_inc(aux, 1)

                if f["ahead"]:
                    w1 = (w + 1) % NT
                    g1, tok = (w1 // UW) % 2, P * (w1 % UW)
                    if w1 % UW == 0:
                        need(pe, aux_v, 2 * (UW * u + 3))
                        need(pe, aux_a, 2 * (UW * u + 3))
                    need(pe, s_sub, n + 1)
                    for h in range(FH):
                        r0 = DH * (h % 2)
                        last = pe.matmul(psS[:, row(h), :], qT[r0:r0 + DH, g1, h // 2, tok:tok + P],
                                         kT[r0:r0 + DH, g1, h // 2, tok:tok + P], start=True, stop=True)
                    last.then_inc(s_ps, 1)
                if f["win"]:
                    need(pe, s_n, n + 1)
                    need(pe, t_out, 2 * n)
                    for h in range(FH):
                        last = pe.transpose(psP[:, h, :], pn[:, h, :], ident[:])
                    last.then_inc(t_ps, 1)
                if f["nxt"]:
                    piece(0)
                    piece(1)
                if f["win"]:
                    need(pe, t_out, 2 * n + 2)
                    need(pe, a_out, n)
                    if w % UW == 0:
                        gu = 2 * b + w // UW
                        need(pe, aux_v, 8 * (gu + 1))
                        need(pe, aux_a, 8 * (gu + 1))
                    for h in range(FH):
                        r0 = DH * (h % 2)
                        last = pe.matmul(psA[r0:r0 + DH, h // 2, :], vv[:, (w // UW) % 2, w % UW, DH * h:DH * h + DH],
                                         pT[:, row(h), :], start=True, stop=True)
                    last.then_inc(a_ps, 1)
                if descends(b, w, mid):
                    i = descent(b, w)
                    need(pe, d_ex, i)
                    need(pe, y_out, n)
                    pe.matmul(psZ, d.group[:], d.z[:], start=True, stop=True).then_inc(d_sum, 1)
                if f["nxt"]:
                    piece(2)
                    piece(3)
                if f["win"]:
                    need(pe, a_out, n + 1)
                    need(pe, y_out, n)
                    if descends(b, w, mid):
                        need(pe, d_ln, descent(b, w))
                    for ft in range(FT):
                        last = pe.matmul(psY, aT[:, ft, :], w_o[:, ft, :], start=ft == 0, stop=ft == FT - 1)
                    last.then_inc(y_ps, 1)

            every_slot(pe, slot)


class RoutingBuffers:
    def __init__(self, ctx, nc):
        def sb(name, shape):
            return ctx.enter_context(nc.sbuf_tensor(name, shape, F32))

        self.ident = sb("r_ident", [P, P])
        self.group = sb("r_group", [P, P])
        self.below = sb("r_below", [P, P])
        self.logk = sb("r_logk", [P, 1])
        self.count = sb("r_count", [P, 1])
        self.sx = sb("r_sx", [P, P + 1])
        self.na = sb("r_na", [P, 1])
        self.over = sb("r_over", [P, P + 1])
        self.under = sb("r_under", [P, P + 1])
        self.e = sb("r_e", [P, P])
        self.z = sb("r_z", [P, 1])
        self.lz = sb("r_lz", [P, 1])


def descent_start(nc, scol, d, load_next):
    with ExitStack() as ctx:
        def sb(name, shape, dt=F32):
            return ctx.enter_context(nc.sbuf_tensor(name, shape, dt))

        def sem(name):
            return ctx.enter_context(nc.semaphore(name))

        cmax = sb("i_cmax", [P, 1])
        rmax = sb("i_rmax", [1, ROUTES * B])
        bmax = sb("i_bmax", [1, ROUTES * B, NT])
        one = sb("i_one", [1, 1])
        ps = ctx.enter_context(nc.psum_tensor("i_ps", [P, P], F32))
        ps1 = ctx.enter_context(nc.psum_tensor("i_ps1", [P, 1], F32))
        made = sem("i_made")
        made_v = sem("i_made_v")
        pe_d = sem("i_pe")
        v_d = sem("i_v")

        block = ctx.enter_context(nc.Block())

        @block.sync
        def _(sp):
            load_next(sp)

        @block.gpsimd
        def _(pool):
            pool.memset(d.ident[:], 0.0).then_inc(made, 1)
            pool.memset(d.group[:], 1.0).then_inc(made, 1)
            pool.wait_ge(made, 2)
            pool.affine_select(out=d.ident[:], in_=d.ident[:], compare_op=ALU.not_equal, fill=1.0, base=0,
                               pattern=[[-1, P]], channel_multiplier=1).then_inc(made, 1)
            g3 = d.group[:].rearrange("p (g c) -> p g c", c=NT)
            pool.affine_select(out=g3, in_=g3, compare_op=ALU.is_ge, fill=0.0, base=0,
                               pattern=[[-NT, P // NT], [0, NT]], channel_multiplier=1).then_inc(made, 1)
            pool.wait_ge(made, 4)
            pool.affine_select(out=g3, in_=g3, compare_op=ALU.is_ge, fill=0.0, base=NT - 1,
                               pattern=[[NT, P // NT], [0, NT]], channel_multiplier=-1).then_inc(made, 1)
            pool.wait_ge(made, 5)
            pool.affine_select(out=d.below[:], in_=d.group[:], compare_op=ALU.is_gt, fill=0.0, base=0,
                               pattern=[[1, P]], channel_multiplier=-1).then_inc(made, 1)

        @block.tensor
        def _(pe):
            pe.wait_ge(made, 6)
            pe.transpose(ps[:], scol[:].rearrange("p r t -> p (r t)"), d.ident[:]).then_inc(pe_d, 1)
            pe.wait_ge(v_d, 3)
            pe.transpose(ps[0:1, :], cmax[:], d.ident[:]).then_inc(pe_d, 1)
            pe.wait_ge(v_d, 5)
            pe.matmul(ps1[:], bmax[:].rearrange("p g c -> p (g c)"), one[:], start=True, stop=True).then_inc(pe_d, 1)

        @block.vector
        def _(v):
            for r, k in enumerate((NQ * FETCH, NKV * FETCH)):
                rows = slice(WT * r, WT * r + WT)
                v.memset(d.logk[rows, :], float(np.log(np.float32(k)))).then_inc(made_v, 1)
                v.memset(d.count[rows, :], float((NQ, NKV)[r])).then_inc(made_v, 1)
                v.memset(d.na[rows, :], float(np.log(np.float32(S)) - np.log(np.float32(k)))).then_inc(made_v, 1)
            v.memset(one[:], 1.0).then_inc(v_d, 1)
            v.wait_ge(pe_d, 1)
            v.tensor_copy(d.sx[:, 0:P], ps[:]).then_inc(v_d, 1)
            v.wait_ge(v_d, 2)
            v.tensor_reduce(cmax[:], d.sx[:, 0:P], AX.X, ALU.max).then_inc(v_d, 1)
            v.wait_ge(pe_d, 2)
            v.tensor_reduce(rmax[:], ps[0:1, :].rearrange("p (g c) -> p g c", c=NT), AX.X, ALU.max).then_inc(v_d, 1)
            v.wait_ge(v_d, 4)
            v.tensor_copy(bmax[:], rmax[:].unsqueeze(2).to_broadcast([1, ROUTES * B, NT])).then_inc(v_d, 1)
            v.wait_ge(pe_d, 3)
            v.tensor_copy(d.sx[:, P:P + 1], ps1[:]).then_inc(v_d, 1)


def choose(nc, d, slotT, deltaT, load_next):
    with ExitStack() as ctx:
        def sb(name, shape, dt=F32):
            return ctx.enter_context(nc.sbuf_tensor(name, shape, dt))

        def pb(name, shape, dt=F32):
            return ctx.enter_context(nc.psum_tensor(name, shape, dt))

        def sem(name):
            return ctx.enter_context(nc.semaphore(name))

        cmax = sb("r_cmax", [P, 1])
        scr = sb("r_scr", [P, P])
        mid_ = sb("r_mid", [P, P])
        thr = sb("r_thr", [P, 1], I32)
        cand = sb("r_cand", [P, 1], I32)
        keep = sb("r_keep", [P, 1], I32)
        hit = sb("r_hit", [P, P])
        eq = sb("r_eq", [P, P])
        gt = sb("r_gt", [P, P])
        cum = sb("r_cum", [P, P])
        zero = sb("r_zero", [P, P])
        cols = sb("r_cols", [P, 4])
        sel = sb("r_sel", [P, P])
        pos = sb("r_pos", [P, P])
        delta = sb("r_delta", [P, P])
        ps = pb("r_ps", [P, P])
        ps1 = pb("r_ps1", [P, 1])

        made_v = sem("r_made_v")
        pe_d = sem("r_pe")
        v_d = sem("r_v")
        a_d = sem("r_a")
        v_b = sem("r_vb")
        v_c = sem("r_vc")
        v_t = sem("r_vt")
        NB = 29

        block = ctx.enter_context(nc.Block())

        @block.sync
        def _(sp):
            load_next(sp)

        @block.tensor
        def _(pe):
            n = 0
            for bit in range(NB + 1):
                pe.wait_ge(v_c, 3 * bit + 1)
                pe.matmul(ps1[:], d.group[:], cols[:, 0:1], start=True, stop=True).then_inc(pe_d, 1)
            n += NB + 1
            pe.wait_ge(v_t, 2)
            pe.matmul(ps1[:], d.group[:], cols[:, 1:2], start=True, stop=True).then_inc(pe_d, 1)
            pe.wait_ge(v_t, 4)
            pe.matmul(ps[:, 0:1], d.below[:], cols[:, 2:3], start=True, stop=True).then_inc(pe_d, 1)
            pe.wait_ge(v_t, 9)
            pe.matmul(ps1[:], d.below[:], cols[:, 3:4], start=True, stop=True).then_inc(pe_d, 1)
            pe.wait_ge(v_t, 12)
            pe.transpose(ps[:], pos[:], d.ident[:]).then_inc(pe_d, 1)
            pe.wait_ge(v_t, 16)
            pe.transpose(ps[:], delta[:], d.ident[:]).then_inc(pe_d, 1)

        @block.scalar
        def _(act):
            act.wait_ge(v_d, 1)
            act.activation(scr[:], mid_[:], ACT.Exp).then_inc(a_d, 1)

        @block.vector
        def _(v):
            v.tensor_scalar(mid_[:], d.sx[:, 0:P], d.na[:, 0:1], 0.0, ALU.subtract, ALU.min).then_inc(v_d, 1)
            v.memset(zero[:], 0.0).then_inc(made_v, 1)
            v.memset(thr[:], 0).then_inc(made_v, 1)
            v.wait_ge(made_v, 2)
            v.wait_ge(a_d, 1)
            n = 0
            for k, bit in enumerate(range(NB, -1, -1)):
                v.tensor_scalar(cand[:], thr[:], 1 << bit, None, ALU.bitwise_or).then_inc(v_b, 1)
                v.wait_ge(v_b, k + 1)
                v.tensor_scalar(hit[:], scr[:], cand[:].bitcast(F32), 0.0, ALU.is_ge, ALU.add,
                                accum_out=cols[:, 0:1]).then_inc(v_c, 1)
                v.wait_ge(pe_d, n + k + 1)
                v.tensor_tensor(keep[:], ps1[:], d.count[:], ALU.is_ge).then_inc(v_c, 1)
                v.wait_ge(v_c, 3 * k + 2)
                v.copy_predicated(thr[:], keep[:], cand[:]).then_inc(v_c, 1)
                v.wait_ge(v_c, 3 * k + 3)
            n += NB + 1
            th = thr[:].bitcast(F32)
            v.tensor_scalar(gt[:], scr[:], th, 0.0, ALU.is_gt, ALU.add, accum_out=cols[:, 1:2]).then_inc(v_t, 1)
            v.tensor_scalar(eq[:], scr[:], th, 0.0, ALU.is_equal, ALU.add, accum_out=cols[:, 2:3]).then_inc(v_t, 1)
            v.wait_ge(v_t, 2)
            v.tensor_tensor_scan(cum[:], eq[:], zero[:], 0.0, ALU.add, ALU.add).then_inc(v_t, 1)
            v.wait_ge(pe_d, n + 1)
            v.tensor_tensor(cmax[:], d.count[:], ps1[:], ALU.subtract).then_inc(v_t, 1)
            v.wait_ge(pe_d, n + 2)
            v.wait_ge(v_t, 4)
            v.tensor_scalar(cum[:], cum[:], ps[:, 0:1], cmax[:, 0:1], ALU.add, ALU.is_le).then_inc(v_t, 1)
            v.wait_ge(v_t, 5)
            v.tensor_tensor(eq[:], eq[:], cum[:], ALU.mult).then_inc(v_t, 1)
            v.wait_ge(v_t, 6)
            v.tensor_tensor(sel[:], gt[:], eq[:], ALU.add).then_inc(v_t, 1)
            v.wait_ge(v_t, 7)
            v.tensor_reduce(cols[:, 3:4], sel[:], AX.X, ALU.add).then_inc(v_t, 1)
            v.tensor_tensor_scan(cum[:], sel[:], zero[:], 0.0, ALU.add, ALU.add).then_inc(v_t, 1)
            v.wait_ge(pe_d, n + 3)
            v.wait_ge(v_t, 9)
            v.tensor_scalar(cum[:], cum[:], ps1[:, 0:1], None, ALU.add).then_inc(v_t, 1)
            v.wait_ge(v_t, 10)
            v.tensor_tensor(cum[:], cum[:], sel[:], ALU.mult).then_inc(v_t, 1)
            v.wait_ge(v_t, 11)
            v.tensor_scalar(pos[:], cum[:], -1.0, None, ALU.add).then_inc(v_t, 1)
            v.tensor_scalar(delta[:], scr[:], -1.0, 1.0, ALU.mult, ALU.add).then_inc(v_t, 1)
            v.wait_ge(v_t, 13)
            v.tensor_tensor(delta[:], delta[:], scr[:], ALU.add).then_inc(v_t, 1)
            v.wait_ge(v_t, 14)
            v.tensor_scalar(delta[:], delta[:], -1.0, None, ALU.add).then_inc(v_t, 1)
            v.wait_ge(pe_d, n + 4)
            v.tensor_copy(slotT[:], ps[:]).then_inc(v_t, 1)
            v.wait_ge(pe_d, n + 5)
            v.tensor_copy(deltaT[:], ps[:]).then_inc(v_t, 1)


ST = NQ // P
VT = NKV // P
BLOCKS = FH * ST
S_AHEAD, X_AHEAD = 3, 2


class RoutedInputs:
    def __init__(self, ctx, nc):
        def sb(name, shape):
            return ctx.enter_context(nc.sbuf_tensor(name, shape, F32))

        self.w_q = sb("h_wq", [P, KT, HID])
        self.w_k = sb("h_wk", [P, KT, HID])
        self.w_v = sb("h_wv", [P, KT, HID])
        self.w_o = sb("h_wo", [P, FT, D])
        self.gcol = sb("h_gamma", [P, KT])
        self.xb = sb("h_xb", [P, NT, D])
        self.w_in = ctx.enter_context(nc.semaphore("h_w_in"))
        self.x_in = ctx.enter_context(nc.semaphore("h_x_in"))

    def load_x(self, sp, x1_dram, b):
        sp.dma_start(self.xb[:], x1_dram[b].rearrange("(t p) n -> p t n", p=P)).then_inc(self.x_in, 16)

    def load_first(self, sp, x1_dram, gamma, wq, wkvT, wo):
        heads = wkvT.rearrange("(t p) (h c d) -> t p h c d", p=P, c=2, d=DH)
        for kt in range(KT):
            rows = slice(P * kt, P * kt + P)
            sp.dma_start(self.w_q[:, kt, :], wq[rows, :]).then_inc(self.w_in, 16)
            for c, w in enumerate((self.w_k, self.w_v)):
                sp.dma_start(w[:, kt, :].rearrange("p (h d) -> p h d", d=DH), heads[kt, :, :, c, :]).then_inc(self.w_in, 16)
            sp.dma_start(self.gcol[:, kt:kt + 1], gamma[rows].rearrange("(p a) -> p a", a=1)).then_inc(self.w_in, 16)
        sp.dma_start(self.w_o[:], wo.rearrange("(f p) n -> p f n", p=P)).then_inc(self.w_in, 16)
        self.load_x(sp, x1_dram, 0)


def routed_attention(nc, x1_dram, inputs, acc, rcol, slotT, deltaT, out):
    with ExitStack() as ctx:
        def sb(name, shape, dt=F32):
            return ctx.enter_context(nc.sbuf_tensor(name, shape, dt))

        def pb(name, shape, dt=F32):
            return ctx.enter_context(nc.psum_tensor(name, shape, dt))

        def sem(name):
            return ctx.enter_context(nc.semaphore(name))

        ident = sb("h_ident", [P, P])
        ident_b = sb("h_ident_b", [P, P], BF16)
        iota_i = sb("h_iota_i", [P, NKV], I32)
        iota = sb("h_iota", [P, NKV], FP16)
        w_q, w_k, w_v, w_o = inputs.w_q, inputs.w_k, inputs.w_v, inputs.w_o
        gcol, xb = inputs.gcol, inputs.xb
        mhalf = sb("h_mhalf", [P, NT])
        eps = sb("h_eps", [P, NT])
        xh = sb("h_xh", [P, NT, D])
        xr = sb("h_xr", [P, NT, D])
        xp = sb("h_xp", [P, NT, PARTS, D], BF16)
        oq = sb("h_oq", [P, NT, NQ], BF16)
        ok = sb("h_ok", [P, NT, NKV], BF16)
        oqT = sb("h_oqT", [P, ST, S], BF16)
        col = sb("h_col", [P, 4, NT])
        dcol = sb("h_dcol", [P, NT], BF16)
        xk = sb("h_xk", [P, KT, NKV])
        xq = sb("h_xq", [P, KT, NQ])
        svk = sb("h_svk", [P, VT])
        qh = sb("h_qh", [P, FT, NQ])
        kh = sb("h_kh", [P, FT, NKV])
        vh = sb("h_vh", [P, VT, HID])
        nm = sb("h_nm", [P, 4, 2])
        rs = sb("h_rs", [P, 4, 2])
        pr = sb("h_pr", [P, 4, NKV])
        pT = sb("h_pT", [P, 2, VT, NQ])
        aT = sb("h_aT", [P, FT, NQ])
        rr = sb("h_rr", [P, ST, D])
        rp = sb("h_rp", [P, ST, PARTS, D], BF16)
        y = sb("h_y", [P, NT, D])
        stats = sb("h_stats", [P, NT, 6])
        mv = sb("h_mv", [P, NT, 2])
        rstd = sb("h_rstd", [P, NT])
        carry = sb("h_carry", [P, 2])
        RB = 6
        ring = pb("h_ring", [P, RB, 512])
        psA = pb("h_psA", [P, FT, NQ])

        w_in, x_in = inputs.w_in, inputs.x_in
        made = sem("h_made")
        made_v = sem("h_made_v")
        c_ok = sem("h_c_ok")
        xh_ok = sem("h_xh_ok")
        x_hi = sem("h_x_hi")
        x_re = sem("h_x_re")
        x_mi = sem("h_x_mi")
        x_lo = sem("h_x_lo")
        oh_ok = sem("h_oh_ok")
        gath = sem("h_gath")
        unit = sem("h_unit")
        ev_a = sem("h_ev_a")
        ev_v = sem("h_ev_v")
        nmx = sem("h_nmx")
        exq = sem("h_exq")
        rec = sem("h_rec")
        nrm = sem("h_nrm")
        ptc = sem("h_ptc")
        av = sem("h_av")
        at_a = sem("h_at_a")
        at_v = sem("h_at_v")
        r_hi = sem("h_r_hi")
        r_re = sem("h_r_re")
        r_mi = sem("h_r_mi")
        r_lo = sem("h_r_lo")
        y_ok = sem("h_y_ok")
        st_ok = sem("h_st_ok")
        ag_ok = sem("h_ag_ok")
        rch = sem("h_rch")
        r_ok = sem("h_r_ok")
        o_ok = sem("h_o_ok")
        o_out = sem("h_o_out")

        U_OHT, U_GK, U_GQ, U_GD, U_Q, U_K, U_V, U_S = 0, 2, 4, 5, 6, 8, 12, 16
        U_WO, U_SC, NU = 48, 50, 54

        def u_s(i):
            return U_S + i if i < S_AHEAD else U_S + S_AHEAD + 2 * (i - S_AHEAD) + 1

        def u_pt(i):
            return U_S + S_AHEAD + (2 * i if i < BLOCKS - S_AHEAD else BLOCKS - S_AHEAD + i)

        BY_A = [0, 1, U_GK, U_GQ, U_Q, U_K, U_K + 2, U_V, U_V + 2]
        BY_V = [U_GK + 1, U_GD, U_Q + 1, U_K + 1, U_K + 3, U_V + 1, U_V + 3, U_WO, U_WO + 1, *range(U_SC, NU)]
        S_OF = {u_s(i): i for i in range(BLOCKS)}
        PT_OF = {u_pt(i): i for i in range(BLOCKS)}

        def left(b, k):
            if k < 0:
                b, k = b - 1, k + NU
            if k in BY_A:
                return ev_a, len(BY_A) * b + BY_A.index(k) + 1
            if k in BY_V:
                return ev_v, len(BY_V) * b + BY_V.index(k) + 1
            if k in S_OF:
                return exq, BLOCKS * b + S_OF[k] + 1
            return ptc, BLOCKS * b + PT_OF[k] + 1

        def bank(k):
            return ring[:, k % RB, :]

        def every_batch(eng, first, batch):
            first()
            batch(0, False, True)
            with eng.Fori(1, B - 1) as b:
                batch(b, True, True)
            batch(B - 1, False, False)

        block = ctx.enter_context(nc.Block())

        @block.sync
        def _(sp):
            def batch(b, mid, more):
                if more:
                    need(sp, xh_ok, NT * (b + 1))
                    inputs.load_x(sp, x1_dram, b + 1)
                need(sp, o_ok, NT * (b + 1))
                sp.dma_start(out[b].rearrange("(t p) n -> p t n", p=P), y[:]).then_inc(o_out, 16)

            every_batch(sp, lambda: None, batch)
            sp.wait_ge(o_out, 16 * B)

        @block.gpsimd
        def _(pool):
            for k, m in enumerate((ident, ident_b)):
                pool.memset(m[:], 0.0).then_inc(made, 1)
                pool.wait_ge(made, 2 * k + 1)
                pool.affine_select(out=m[:], in_=m[:], compare_op=ALU.not_equal, fill=1.0, base=0,
                                   pattern=[[-1, P]], channel_multiplier=1).then_inc(made, 1)
            pool.iota(iota_i[:], pattern=[[1, NKV]], base=0, channel_multiplier=0).then_inc(made, 1)
            pool.memset(mhalf[:], -0.5).then_inc(made, 1)
            pool.memset(eps[:], OUT_EPS).then_inc(made, 1)

            def parts(b, c, step):
                e = NT * b + c
                if step == 0:
                    need(pool, x_hi, e + 1)
                    need(pool, x_mi, NT * (b - 1) + c + 1)
                    pool.tensor_tensor(xr[:, c, :], xh[:, c, :], xp[:, c, 0, :], ALU.subtract).then_inc(x_re, 1)
                else:
                    need(pool, x_mi, e + 1)
                    need(pool, x_re, e + 1)
                    pool.tensor_tensor(xp[:, c, 2, :], xr[:, c, :], xp[:, c, 1, :], ALU.subtract).then_inc(x_lo, 1)

            def batch(b, mid, more):
                for i in range(BLOCKS):
                    if more:
                        parts(b + 1, i // 2, i % 2)
                need(pool, ag_ok, NT * (b + 1))
                pool.tensor_tensor(rstd[:], mv[:, :, 1], eps[:], ALU.add).then_inc(rch, 1)
                need(pool, rch, b + 1)
                pool.tensor_tensor(rstd[:], rstd[:], mhalf[:], ALU.pow).then_inc(r_ok, 1)

            def first():
                pool.wait_ge(made, 7)
                for i in range(BLOCKS):
                    parts(0, i // 2, i % 2)

            every_batch(pool, first, batch)

        @block.scalar
        def _(act):
            def parts(b, c, step):
                e = NT * b + c
                if step == 0:
                    need(act, xh_ok, e + 1)
                    need(act, gath, b)
                    act.activation(xp[:, c, 0, :], xh[:, c, :], ACT.Copy).then_inc(x_hi, 1)
                else:
                    need(act, x_re, e + 1)
                    act.activation(xp[:, c, 1, :], xr[:, c, :], ACT.Copy).then_inc(x_mi, 1)

            def batch(b, mid, more):
                def filled(k):
                    need(act, unit, NU * b + k + 1)

                for k in BY_A:
                    filled(k)
                    src = bank(k)
                    if k < 2:
                        o = act.activation(oqT[:, k, :], src.bitcast(BF16), ACT.Copy)
                    elif k == U_GK:
                        o = act.activation(xk[:, 0, :], src, ACT.Copy)
                    elif k == U_GQ:
                        o = act.activation(xq[:].rearrange("p t n -> p (t n)"), src, ACT.Copy)
                    elif k == U_Q:
                        o = act.activation(qh[:, 0:2, :].rearrange("p t n -> p (t n)"), src, ACT.Copy)
                    elif k < U_V:
                        o = act.activation(kh[:, k - U_K, :], src, ACT.Copy)
                    else:
                        if k == U_V:
                            need(act, ev_v, len(BY_V) * b + BY_V.index(U_GD) + 1)
                        o = act.activation(vh[:, k - U_V, :], src, ACT.Copy, scale=svk[:, k - U_V:k - U_V + 1])
                    o.then_inc(ev_a, 1)

                def block_exp(i):
                    e = BLOCKS * b + i
                    need(act, nmx, 2 * e + 2)
                    need(act, nrm, e - 3)
                    need(act, unit, NU * b + u_pt(i - 4) + 1) if i >= 4 else need(act, unit, NU * (b - 1) + u_pt(i + BLOCKS - 4) + 1)
                    act.activation(pr[:, i % 4, :], bank(u_s(i)), ACT.Exp, bias=nm[:, i % 4, 1:2], scale=LSCALE,
                                   accum_out=rs[:, i % 4, 0:1]).then_inc(exq, 1)

                def block_out(i):
                    h, qt = divmod(i, ST)
                    filled(u_pt(i))
                    need(act, av, FH * b + h - 1)
                    act.activation(pT[:, h % 2, :, P * qt:P * qt + P], bank(u_pt(i)).rearrange("p (t q) -> p t q", q=P),
                                   ACT.Copy).then_inc(ptc, 1)

                for i in range(X_AHEAD):
                    block_exp(i)
                for i in range(BLOCKS):
                    if i >= 1:
                        block_out(i - 1)
                    if i + X_AHEAD < BLOCKS:
                        block_exp(i + X_AHEAD)
                    if more:
                        parts(b + 1, i // 2, i % 2)
                block_out(BLOCKS - 1)
                need(act, av, FH * (b + 1))
                act.activation(aT[:, 0:2, :], psA[:, 0:2, :], ACT.Copy).then_inc(at_a, 1)
                for s in range(ST):
                    filled(U_WO + s)
                    need(act, unit, NU * b)
                    act.activation(rp[:, s, 0, :], bank(U_WO + s)[:, 0:D], ACT.Copy).then_inc(r_hi, 1)
                for s in range(ST):
                    need(act, r_re, ST * b + s + 1)
                    act.activation(rp[:, s, 1, :], rr[:, s, :], ACT.Copy).then_inc(r_mi, 1)

            def first():
                for i in range(BLOCKS):
                    parts(0, i // 2, i % 2)

            every_batch(act, first, batch)

        @block.vector
        def _(v):
            v.wait_ge(w_in, 16 * 9)
            for kt in range(KT):
                for w in (w_q, w_k, w_v):
                    v.tensor_scalar(w[:, kt, :], w[:, kt, :], gcol[:, kt:kt + 1], None, ALU.mult).then_inc(made_v, 1)
            v.wait_ge(made, 7)
            v.tensor_copy(iota[:], iota_i[:]).then_inc(made_v, 1)
            v.wait_ge(made_v, 7)

            def stage(b, mid):
                t = bass.ds(NT * b, NT) if mid else slice(NT * b, NT * b + NT)
                t2 = bass.ds(NT * b + WT, NT) if mid else slice(NT * b + WT, NT * b + WT + NT)
                need(v, gath, b)
                v.tensor_copy(col[:, 0, :], slotT[:, t]).then_inc(c_ok, 1)
                v.tensor_copy(col[:, 1, :], slotT[:, t2]).then_inc(c_ok, 1)
                v.tensor_copy(col[:, 2, :], rcol[:, t]).then_inc(c_ok, 1)
                v.tensor_copy(dcol[:], deltaT[:, t2]).then_inc(c_ok, 1)
                need(v, c_ok, 4 if not mid and b == 0 else 5 * b + 3)

            def chunk(b, c):
                if c == 0:
                    need(v, x_in, 16 * (b + 1))
                need(v, x_re, NT * (b - 1) + c + 1)
                v.tensor_scalar(xh[:, c, :], xb[:, c, :], col[:, 2, c:c + 1], None, ALU.mult).then_inc(xh_ok, 1)
                v.tensor_scalar(oq[:, c, :], iota[:, 0:NQ], col[:, 0, c:c + 1], None, ALU.is_equal).then_inc(oh_ok, 1)
                v.tensor_scalar(ok[:, c, :], iota[:], col[:, 1, c:c + 1], None, ALU.is_equal).then_inc(oh_ok, 1)

            def batch(b, mid, more):
                def filled(k):
                    need(v, unit, NU * b + k + 1)

                for k in BY_V[:7]:
                    filled(k)
                    src = bank(k)
                    if k == U_GK + 1:
                        o = v.tensor_copy(xk[:, 1, :], src)
                    elif k == U_GD:
                        o = v.tensor_scalar(svk[:], src[:, 0:VT], 1.0, None, ALU.add)
                    elif k == U_Q + 1:
                        o = v.tensor_copy(qh[:, 2:4, :].rearrange("p t n -> p (t n)"), src)
                    elif k < U_V:
                        o = v.tensor_copy(kh[:, k - U_K, :], src)
                    else:
                        if k == U_V + 1:
                            need(v, ev_v, len(BY_V) * b + BY_V.index(U_GD) + 1)
                        o = v.tensor_scalar(vh[:, k - U_V, :], src, svk[:, k - U_V:k - U_V + 1], None, ALU.mult)
                    o.then_inc(ev_v, 1)

                def block_max(i):
                    e = BLOCKS * b + i
                    filled(u_s(i))
                    need(v, exq, e - 3)
                    v.tensor_reduce(nm[:, i % 4, 0:1], bank(u_s(i)), AX.X, ALU.max, negate=True).then_inc(nmx, 1)
                    need(v, nmx, 2 * e + 1)
                    v.tensor_scalar(nm[:, i % 4, 1:2], nm[:, i % 4, 0:1], LSCALE, None, ALU.mult).then_inc(nmx, 1)

                def block_norm(i):
                    e = BLOCKS * b + i
                    need(v, exq, e + 1)
                    v.reciprocal(rs[:, i % 4, 1:2], rs[:, i % 4, 0:1]).then_inc(rec, 1)
                    need(v, rec, e + 1)
                    v.tensor_scalar(pr[:, i % 4, :], pr[:, i % 4, :], rs[:, i % 4, 1:2], None, ALU.mult).then_inc(nrm, 1)

                for i in range(X_AHEAD):
                    block_max(i)
                for i in range(BLOCKS):
                    block_norm(i)
                    if i + X_AHEAD < BLOCKS:
                        block_max(i + X_AHEAD)
                    if more:
                        if i == 0:
                            stage(b + 1, mid)
                        if i % 2 == 0:
                            chunk(b + 1, i // 2)
                need(v, av, FH * (b + 1))
                v.tensor_copy(aT[:, 2:4, :], psA[:, 2:4, :]).then_inc(at_v, 1)
                for s in range(ST):
                    need(v, r_hi, ST * b + s + 1)
                    need(v, r_mi, ST * (b - 1) + s + 1)
                    v.tensor_tensor(rr[:, s, :], bank(U_WO + s)[:, 0:D], rp[:, s, 0, :], ALU.subtract).then_inc(r_re, 1)
                    need(v, r_re, ST * b + s + 1)
                    v.sem_inc(ev_v, 1)
                for s in range(ST):
                    need(v, r_mi, ST * b + s + 1)
                    v.tensor_tensor(rp[:, s, 2, :], rr[:, s, :], rp[:, s, 1, :], ALU.subtract).then_inc(r_lo, 1)
                t = bass.ds(NT * b, NT) if mid else slice(NT * b, NT * b + NT)
                v.tensor_scalar(col[:, 3, :], deltaT[:, t], 1.0, None, ALU.add).then_inc(c_ok, 1)
                need(v, c_ok, 5 * b + 5 + (4 if more else 0))
                need(v, o_out, 16 * b)
                for k in range(NT // 2):
                    filled(U_SC + k)
                    for c in range(2):
                        tt = 2 * k + c
                        at = acc[:, bass.ds(NT * b + tt, 1), :] if mid else acc[:, NT * b + tt:NT * b + tt + 1, :]
                        o = v.scalar_tensor_tensor(out=y[:, tt:tt + 1, :], in0=bank(U_SC + k)[:, D * c:D * c + D].unsqueeze(1),
                                                   scalar=col[:, 3, tt:tt + 1], in1=at, op0=ALU.mult, op1=ALU.add)
                        o.then_inc(y_ok, 1) if c == 0 else o.then_inc(ev_v, 1)
                    need(v, y_ok, NT // 2 * b + k + 1)
                    v.bn_stats(stats[:, 2 * k, :], y[:, 2 * k, :]).then_inc(st_ok, 1)
                    need(v, ev_v, len(BY_V) * b + BY_V.index(U_SC + k) + 1)
                    v.bn_stats(stats[:, 2 * k + 1, :], y[:, 2 * k + 1, :]).then_inc(st_ok, 1)
                need(v, st_ok, NT * (b + 1))
                v.memset(carry[:, 0:1], 0.0)
                for tt in range(NT):
                    v.bn_aggr(mv[:, tt, :], stats[:, tt, :]).then_inc(ag_ok, 1)
                need(v, r_ok, b + 1)
                for tt in range(NT):
                    v.tensor_scalar(y[:, tt, :], y[:, tt, :], mv[:, tt, 0:1], rstd[:, tt:tt + 1], ALU.subtract,
                                    ALU.mult).then_inc(o_ok, 1)

            def first():
                stage(0, False)
                for c in range(NT):
                    chunk(0, c)

            every_batch(v, first, batch)

        @block.tensor
        def _(pe):
            pe.wait_ge(made, 7)
            pe.wait_ge(made_v, 7)

            def batch(b, mid, more):
                def fill(k):
                    need(pe, *left(b, k - RB))

                for s in range(ST):
                    fill(U_OHT + s)
                    need(pe, oh_ok, 2 * NT * (b + 1))
                    o = bank(U_OHT + s).bitcast(BF16)
                    for c in range(NT):
                        last = pe.transpose(o[:, P * c:P * c + P], oq[:, c, P * s:P * s + P], ident_b[:])
                    last.then_inc(unit, 1)
                need(pe, x_lo, NT * (b + 1))
                for ft in range(KT):
                    fill(U_GK + ft)
                    for c in range(NT):
                        for m in range(PARTS):
                            last = pe.matmul(bank(U_GK + ft), xp[:, c, m, P * ft:P * ft + P], ok[:, c, :],
                                             start=c == 0 and m == 0, stop=c == NT - 1 and m == PARTS - 1)
                    last.then_inc(unit, 1)
                fill(U_GQ)
                for ft in range(KT):
                    for c in range(NT):
                        for m in range(PARTS):
                            last = pe.matmul(bank(U_GQ)[:, NQ * ft:NQ * ft + NQ], xp[:, c, m, P * ft:P * ft + P],
                                             oq[:, c, :], start=c == 0 and m == 0, stop=c == NT - 1 and m == PARTS - 1)
                last.then_inc(unit, 1)
                fill(U_GD)
                for s in range(VT):
                    for c in range(NT):
                        last = pe.matmul(bank(U_GD)[:, s:s + 1], ok[:, c, P * s:P * s + P], dcol[:, c:c + 1],
                                         start=c == 0, stop=c == NT - 1)
                last.then_inc(unit, 1)
                need(pe, unit, NU * b + U_GD + 1)
                pe.sem_inc(gath, 1)
                for k in range(2):
                    fill(U_Q + k)
                    need(pe, *left(b, U_GQ))
                    for f in range(2):
                        for kt in range(KT):
                            ft = 2 * k + f
                            last = pe.matmul(bank(U_Q + k)[:, NQ * f:NQ * f + NQ], w_q[:, kt, P * ft:P * ft + P], xq[:, kt, :],
                                             start=kt == 0, stop=kt == KT - 1)
                    last.then_inc(unit, 1)
                need(pe, *left(b, U_GK))
                need(pe, *left(b, U_GK + 1))
                for ft in range(FT):
                    fill(U_K + ft)
                    for kt in range(KT):
                        last = pe.matmul(bank(U_K + ft), w_k[:, kt, P * ft:P * ft + P], xk[:, kt, :], start=kt == 0,
                                         stop=kt == KT - 1)
                    last.then_inc(unit, 1)
                for s in range(VT):
                    fill(U_V + s)
                    for kt in range(KT):
                        last = pe.matmul(bank(U_V + s), xk[:, kt, P * s:P * s + P], w_v[:, kt, :], start=kt == 0,
                                         stop=kt == KT - 1)
                    last.then_inc(unit, 1)

                def scores(i):
                    h, qt = divmod(i, ST)
                    r0 = DH * (h % 2)
                    fill(u_s(i))
                    pe.matmul(bank(u_s(i)), qh[r0:r0 + DH, h // 2, P * qt:P * qt + P], kh[r0:r0 + DH, h // 2, :],
                              start=True, stop=True).then_inc(unit, 1)

                def values(h):
                    need(pe, ptc, BLOCKS * b + ST * (h + 1))
                    if h == 0:
                        need(pe, at_a, b)
                        need(pe, at_v, b)
                    r0 = DH * (h % 2)
                    for t in range(VT):
                        last = pe.matmul(psA[r0:r0 + DH, h // 2, :], vh[:, t, DH * h:DH * h + DH], pT[:, h % 2, t, :],
                                         start=t == 0, stop=t == VT - 1)
                    last.then_inc(av, 1)

                need(pe, *left(b, U_K + 2))
                need(pe, *left(b, U_K + 3))
                need(pe, *left(b, U_V + 2))
                need(pe, *left(b, U_V + 3))
                for i in range(S_AHEAD):
                    scores(i)
                for i in range(BLOCKS):
                    need(pe, nrm, BLOCKS * b + i + 1)
                    fill(u_pt(i))
                    for t in range(VT):
                        last = pe.transpose(bank(u_pt(i))[:, P * t:P * t + P], pr[:, i % 4, P * t:P * t + P], ident[:])
                    last.then_inc(unit, 1)
                    if i + S_AHEAD < BLOCKS:
                        scores(i + S_AHEAD)
                    if i % ST == ST - 1 and i >= 2 * ST - 1:
                        values(i // ST - 1)
                values(FH - 1)
                need(pe, at_a, b + 1)
                need(pe, at_v, b + 1)
                for s in range(ST):
                    fill(U_WO + s)
                    for ft in range(FT):
                        last = pe.matmul(bank(U_WO + s)[:, 0:D], aT[:, ft, P * s:P * s + P], w_o[:, ft, :], start=ft == 0,
                                         stop=ft == FT - 1)
                    last.then_inc(unit, 1)
                need(pe, r_lo, ST * (b + 1))
                for k in range(NT // 2):
                    fill(U_SC + k)
                    for c in range(2):
                        t0 = P * (2 * k + c)
                        for s in range(ST):
                            for m in range(PARTS):
                                last = pe.matmul(bank(U_SC + k)[:, D * c:D * c + D], oqT[:, s, t0:t0 + P], rp[:, s, m, :],
                                                 start=s == 0 and m == 0, stop=s == ST - 1 and m == PARTS - 1)
                    last.then_inc(unit, 1)

            every_batch(pe, lambda: None, batch)


def build(nc, a, out):
    nc.disable_value_cache = True
    stat = nc.dram_tensor("max_scratch", (2, PARTS * 4 * NT, P), BF16, kind="Internal").ap()
    part = nc.dram_tensor("part_scratch", (2, PARTS, P, S), BF16, kind="Internal").ap()
    x1 = nc.dram_tensor("x1_scratch", (B, S, H), F32, kind="Internal").ap()
    with ExitStack() as ctx:
        def sb(name, shape):
            return ctx.enter_context(nc.sbuf_tensor(name, shape, F32))

        scol = sb("scol", [P, ROUTES, WT])
        causal_attention(nc, a["L0_attn_x"], a["L0_attn_ln_g"], a["L0_attn_ln_b"], a["L0_attn_w_qkv"], a["L0_attn_b_qkv"],
                         a["L0_attn_w_ent"], a["L0_attn_b_ent"], a["L0_attn_w_out"], a["L0_attn_b_out"],
                         (a["L0_ffn_q_routing_token"], a["L0_ffn_kv_routing_token"]), stat, part, x1, scol)
        d = RoutingBuffers(ctx, nc)
        acc = sb("acc", [P, WT, D])
        rcol = sb("rcol", [P, WT])
        slotT = sb("slotT", [P, RC])
        deltaT = sb("deltaT", [P, RC])
        with ExitStack() as local:
            inputs = LocalInputs(local, nc)
            descent_start(nc, scol, d, lambda sp: inputs.load_first(
                sp, x1, a["L0_ffn_gamma_light"], a["L0_ffn_wq_light"], a["L0_ffn_wkv_light"], a["L0_ffn_wo_light"]))
            local_attention(nc, x1, inputs, acc, rcol, d)
        routed = RoutedInputs(ctx, nc)
        choose(nc, d, slotT, deltaT, lambda sp: routed.load_first(
            sp, x1, a["L0_ffn_gamma_heavy"], a["L0_ffn_wq_heavy"], a["L0_ffn_wkv_heavy"], a["L0_ffn_wo_heavy"]))
        routed_attention(nc, x1, routed, acc, rcol, slotT, deltaT, out)


_INS = ['L0_attn_x', 'L0_attn_ln_g', 'L0_attn_ln_b', 'L0_attn_w_qkv', 'L0_attn_b_qkv', 'L0_attn_w_ent', 'L0_attn_b_ent', 'L0_attn_w_out', 'L0_attn_b_out', 'L0_ffn_gamma_light', 'L0_ffn_wq_light', 'L0_ffn_wkv_light', 'L0_ffn_wo_light', 'L0_ffn_q_routing_token', 'L0_ffn_kv_routing_token', 'L0_ffn_gamma_heavy', 'L0_ffn_wq_heavy', 'L0_ffn_wkv_heavy', 'L0_ffn_wo_heavy']


def kernel(**inputs):
    import numpy as _np
    import concourse.bacc as _bacc
    from concourse import mybir as _mybir
    from concourse.bass_utils import run_bass_kernel_spmd as _run

    nc = _bacc.Bacc("TRN2", target_bir_lowering=False, num_devices=1)
    arrays, args = {}, {}
    for name in _INS:
        a = _np.asarray(inputs[name])
        if name in ("L0_attn_w_qkv", "L0_attn_w_out", "L0_ffn_wkv_heavy"):
            a = a.T
        a = _np.ascontiguousarray(a)
        arrays[f"in_{name}_dram"] = a
        args[name] = nc.dram_tensor(f"in_{name}_dram", a.shape, _mybir.dt.from_np(a.dtype), kind="ExternalInput").ap()
    out = nc.dram_tensor("out_0_dram", (B, S, H), _mybir.dt.float32, kind="ExternalOutput").ap()
    build(nc, args, out)
    r = _run(nc, [arrays], core_ids=[0])
    return r.results[0]["out_0_dram"]
```
